# Optimizing a Trainium2 kernel written in Bass

```python
import numpy as np
import jax
import jax.numpy as jnp

def _softmax(x, axis=-1):
    return jax.nn.softmax(x, axis=axis)

def _gelu(x):
    return jax.nn.gelu(x, approximate=True)

def _silu(x):
    return jax.nn.silu(x)

def _sigmoid(x):
    return jax.nn.sigmoid(x)

def _layernorm(x, axis=-1, eps=1e-05):
    m = jnp.mean(x, axis=axis, keepdims=True)
    v = jnp.var(x, axis=axis, keepdims=True)
    return (x - m) / jnp.sqrt(v + eps)

def _scatter_add(tgt, idx, src, axis=0):
    return tgt.at[idx].add(src)

def _segment_sum(src, seg, n):
    return jax.ops.segment_sum(src, seg, n)
kernel_name = 'mk_gnn_ffn_d2_gnn_r8_d0b781'

def setup_inputs(seed: int=0):
    np.random.seed(seed)
    _w = jnp.asarray

    def _rec_inputs():
        import jax
        import jax.numpy as jnp
        _gk = jax.random.key(seed)
        x = -8.776e-05 + 1 * jax.random.normal(jax.random.fold_in(_gk, 1), (2500, 256), jnp.float32)
        src = jax.random.randint(jax.random.fold_in(_gk, 2), (80000,), 0, 2500, jnp.int32)
        dst = jnp.minimum((2500 * jax.random.uniform(jax.random.fold_in(_gk, 3), (80000,)) ** 2.0).astype(jnp.int32), 19999)
        _o = jnp.argsort(dst, stable=True)
        src = src[_o]
        dst = dst[_o]
        edge_type_8 = jax.random.randint(jax.random.fold_in(_gk, 13), (80000,), 0, 8, jnp.int32)
        return (x, src, dst, edge_type_8)
    x, src, dst, edge_type_8 = _rec_inputs()

    def _L0_gnn_setup():
        import jax, jax.numpy as jnp
        import numpy as np
        N_NODES = 2500
        N_EDGES = 37500
        D = 256
        NUM_RELS = 8
        NUM_BASES = 4
        key = jax.random.key(seed)
        ks = jax.random.split(key, 8)
        x = jax.random.normal(ks[0], (N_NODES, D), dtype=jnp.float32)
        src = jax.random.randint(ks[1], (N_EDGES,), 0, N_NODES, dtype=jnp.int32)
        dst = jax.random.randint(ks[2], (N_EDGES,), 0, N_NODES, dtype=jnp.int32)
        etypes = jax.random.randint(ks[3], (N_EDGES,), 0, NUM_RELS, dtype=jnp.int32)
        scale = 1.0 / np.sqrt(D)
        basis = jax.random.normal(ks[4], (NUM_BASES, D, D), dtype=jnp.float32) * scale
        comp = jax.random.normal(ks[5], (NUM_RELS, NUM_BASES), dtype=jnp.float32)
        loop_weight = jax.random.normal(ks[6], (D, D), dtype=jnp.float32) * scale
        bias_param = jnp.zeros((D,), dtype=jnp.float32)
        return {'x': x, 'src': src, 'dst': dst, 'etypes': etypes, 'basis': basis, 'comp': comp, 'loop_weight': loop_weight, 'bias_param': bias_param}
    _L0_gnn_all = _L0_gnn_setup()
    _L0_gnn_in = {k: v for k, v in _L0_gnn_all.items() if k in ('basis', 'comp', 'loop_weight', 'bias_param')}
    del _L0_gnn_all

    def _L0_ffn_setup():
        import jax, jax.numpy as jnp
        import numpy as np
        B, S, D = (8, 512, 256)
        H = 4 * D
        CAPACITY = 0.5
        key = jax.random.key(seed)
        ks = jax.random.split(key, 6)
        x = jax.random.normal(ks[0], (B, S, D), dtype=jnp.float32)
        attention_mask = jnp.zeros((B, 1, 1, S), dtype=jnp.float32)
        wr = jax.random.normal(ks[1], (D, 1), dtype=jnp.float32) * 0.02
        br = jnp.zeros((1,), dtype=jnp.float32)
        w1 = jax.random.normal(ks[2], (D, H), dtype=jnp.float32) * 0.02
        b1 = jnp.zeros((H,), dtype=jnp.float32)
        w2 = jax.random.normal(ks[3], (H, D), dtype=jnp.float32) * 0.02
        b2 = jnp.zeros((D,), dtype=jnp.float32)
        return {'x': x, 'attention_mask': attention_mask, 'wr': wr, 'br': br, 'w1': w1, 'b1': b1, 'w2': w2, 'b2': b2}
    _L0_ffn_all = _L0_ffn_setup()
    _L0_ffn_in = {k: v for k, v in _L0_ffn_all.items() if k in ('attention_mask', 'wr', 'br', 'w1', 'b1', 'w2', 'b2')}
    del _L0_ffn_all

    def _L1_gnn_setup():
        import jax, jax.numpy as jnp
        import numpy as np
        N = 12500
        E = 200000
        D = 256
        BN_EPS = 1e-05

        def _batchnorm(x, gamma, beta):
            mu = jnp.mean(x, axis=0)
            var = jnp.var(x, axis=0)
            return (x - mu) * jax.lax.rsqrt(var + BN_EPS) * gamma + beta

        def _gin_conv(x, src, dst, n, W1, b1, gamma, beta, W2, b2):
            agg = jax.ops.segment_sum(x[src], dst, num_segments=n)
            h = x + agg
            h = jax.nn.relu(_batchnorm(h @ W1 + b1, gamma, beta))
            return jax.nn.relu(h @ W2 + b2)
        key = jax.random.key(seed)
        ks = jax.random.split(key, 8)
        x = jax.random.normal(ks[0], (N, D), dtype=jnp.float32)
        edge_index = jax.random.randint(ks[1], (2, E), 0, N, dtype=jnp.int64)
        s = 0.02
        inp = {'x': x, 'edge_index': edge_index, 'g0': jnp.ones((D,), jnp.float32), 'b0': jnp.zeros((D,), jnp.float32), 'W1a': jax.random.normal(ks[2], (D, D), jnp.float32) * s, 'b1a': jnp.zeros((D,), jnp.float32), 'g1': jnp.ones((D,), jnp.float32), 'bt1': jnp.zeros((D,), jnp.float32), 'W1b': jax.random.normal(ks[3], (D, D), jnp.float32) * s, 'b1b': jnp.zeros((D,), jnp.float32), 'W2a': jax.random.normal(ks[4], (D, D), jnp.float32) * s, 'b2a': jnp.zeros((D,), jnp.float32), 'g2': jnp.ones((D,), jnp.float32), 'bt2': jnp.zeros((D,), jnp.float32), 'W2b': jax.random.normal(ks[5], (D, D), jnp.float32) * s, 'b2b': jnp.zeros((D,), jnp.float32)}
        return inp
    _L1_gnn_all = _L1_gnn_setup()
    _L1_gnn_in = {k: v for k, v in _L1_gnn_all.items() if k in ('g0', 'b0', 'W1a', 'b1a', 'g1', 'bt1', 'W1b', 'b1b', 'W2a', 'b2a', 'g2', 'bt2', 'W2b', 'b2b')}
    del _L1_gnn_all

    def _L1_ffn_setup():
        import jax, jax.numpy as jnp
        import numpy as np
        B, A = (512, 8)
        IN, OUT = (256, 256)
        SH1, SH2 = (256, 128)
        EH1, EH2 = (128, 64)
        E, TOPK = (4, 2)

        def _shared_mlp(x, W1, b1, W2, b2, W3, b3):
            h = jax.nn.relu(x @ W1 + b1)
            h = jax.nn.relu(h @ W2 + b2)
            return h @ W3 + b3

        def _experts_mlp(x, eW1, eb1, eW2, eb2, eW3, eb3):
            h = jax.nn.relu(jnp.einsum('baf,efh->ebah', x, eW1) + eb1[:, None, None, :])
            h = jax.nn.relu(jnp.einsum('ebah,ehg->ebag', h, eW2) + eb2[:, None, None, :])
            o = jnp.einsum('ebag,ego->ebao', h, eW3) + eb3[:, None, None, :]
            return jnp.moveaxis(o, 0, -1)
        key = jax.random.key(seed)
        ks = jax.random.split(key, 16)
        s = 0.05
        return {'x': jax.random.normal(ks[0], (B, A, IN), jnp.float32), 'sW1': jax.random.normal(ks[1], (IN, SH1), jnp.float32) * s, 'sb1': jnp.zeros((SH1,), jnp.float32), 'sW2': jax.random.normal(ks[2], (SH1, SH2), jnp.float32) * s, 'sb2': jnp.zeros((SH2,), jnp.float32), 'sW3': jax.random.normal(ks[3], (SH2, OUT), jnp.float32) * s, 'sb3': jnp.zeros((OUT,), jnp.float32), 'eW1': jax.random.normal(ks[4], (E, IN, EH1), jnp.float32) * s, 'eb1': jnp.zeros((E, EH1), jnp.float32), 'eW2': jax.random.normal(ks[5], (E, EH1, EH2), jnp.float32) * s, 'eb2': jnp.zeros((E, EH2), jnp.float32), 'eW3': jax.random.normal(ks[6], (E, EH2, OUT), jnp.float32) * s, 'eb3': jnp.zeros((E, OUT), jnp.float32), 'gW': jax.random.normal(ks[7], (IN, E), jnp.float32) * s, 'gb': jnp.zeros((E,), jnp.float32)}
    _L1_ffn_all = _L1_ffn_setup()
    _L1_ffn_in = {k: v for k, v in _L1_ffn_all.items() if k in ('sW1', 'sb1', 'sW2', 'sb2', 'sW3', 'sb3', 'eW1', 'eb1', 'eW2', 'eb2', 'eW3', 'eb3', 'gW', 'gb')}
    del _L1_ffn_all
    return {'x': x, 'src': src, 'dst': dst, 'edge_type_8': edge_type_8, 'L0_gnn_basis': _L0_gnn_in['basis'], 'L0_gnn_comp': _L0_gnn_in['comp'], 'L0_gnn_loop_weight': _L0_gnn_in['loop_weight'], 'L0_gnn_bias_param': _L0_gnn_in['bias_param'], 'L0_ffn_attention_mask': _L0_ffn_in['attention_mask'], 'L0_ffn_wr': _L0_ffn_in['wr'], 'L0_ffn_br': _L0_ffn_in['br'], 'L0_ffn_w1': _L0_ffn_in['w1'], 'L0_ffn_b1': _L0_ffn_in['b1'], 'L0_ffn_w2': _L0_ffn_in['w2'], 'L0_ffn_b2': _L0_ffn_in['b2'], 'L1_gnn_g0': _L1_gnn_in['g0'], 'L1_gnn_b0': _L1_gnn_in['b0'], 'L1_gnn_W1a': _L1_gnn_in['W1a'], 'L1_gnn_b1a': _L1_gnn_in['b1a'], 'L1_gnn_g1': _L1_gnn_in['g1'], 'L1_gnn_bt1': _L1_gnn_in['bt1'], 'L1_gnn_W1b': _L1_gnn_in['W1b'], 'L1_gnn_b1b': _L1_gnn_in['b1b'], 'L1_gnn_W2a': _L1_gnn_in['W2a'], 'L1_gnn_b2a': _L1_gnn_in['b2a'], 'L1_gnn_g2': _L1_gnn_in['g2'], 'L1_gnn_bt2': _L1_gnn_in['bt2'], 'L1_gnn_W2b': _L1_gnn_in['W2b'], 'L1_gnn_b2b': _L1_gnn_in['b2b'], 'L1_ffn_sW1': _L1_ffn_in['sW1'], 'L1_ffn_sb1': _L1_ffn_in['sb1'], 'L1_ffn_sW2': _L1_ffn_in['sW2'], 'L1_ffn_sb2': _L1_ffn_in['sb2'], 'L1_ffn_sW3': _L1_ffn_in['sW3'], 'L1_ffn_sb3': _L1_ffn_in['sb3'], 'L1_ffn_eW1': _L1_ffn_in['eW1'], 'L1_ffn_eb1': _L1_ffn_in['eb1'], 'L1_ffn_eW2': _L1_ffn_in['eW2'], 'L1_ffn_eb2': _L1_ffn_in['eb2'], 'L1_ffn_eW3': _L1_ffn_in['eW3'], 'L1_ffn_eb3': _L1_ffn_in['eb3'], 'L1_ffn_gW': _L1_ffn_in['gW'], 'L1_ffn_gb': _L1_ffn_in['gb']}

def reference(x, src, dst, edge_type_8, L0_gnn_basis, L0_gnn_comp, L0_gnn_loop_weight, L0_gnn_bias_param, L0_ffn_attention_mask, L0_ffn_wr, L0_ffn_br, L0_ffn_w1, L0_ffn_b1, L0_ffn_w2, L0_ffn_b2, L1_gnn_g0, L1_gnn_b0, L1_gnn_W1a, L1_gnn_b1a, L1_gnn_g1, L1_gnn_bt1, L1_gnn_W1b, L1_gnn_b1b, L1_gnn_W2a, L1_gnn_b2a, L1_gnn_g2, L1_gnn_bt2, L1_gnn_W2b, L1_gnn_b2b, L1_ffn_sW1, L1_ffn_sb1, L1_ffn_sW2, L1_ffn_sb2, L1_ffn_sW3, L1_ffn_sb3, L1_ffn_eW1, L1_ffn_eb1, L1_ffn_eW2, L1_ffn_eb2, L1_ffn_eW3, L1_ffn_eb3, L1_ffn_gW, L1_ffn_gb):
    import jax
    import jax.numpy as jnp

    def _L0_gnn_ref(x, src, dst, etypes, basis, comp, loop_weight, bias_param):
        import jax, jax.numpy as jnp
        import numpy as np
        N_NODES = 2500
        N_EDGES = 37500
        D = 256
        NUM_RELS = 8
        NUM_BASES = 4
        W = jnp.einsum('rb,bio->rio', comp, basis)
        H = jnp.einsum('ni,rio->nro', x, W)
        msg = H[src, etypes]
        agg = jax.ops.segment_sum(msg, dst, num_segments=N_NODES)
        out = agg + x @ loop_weight + bias_param
        return out

    def _L0_ffn_ref(x, attention_mask, wr, br, w1, b1, w2, b2):
        import jax, jax.numpy as jnp
        import numpy as np
        B, S, D = (8, 512, 256)
        H = 4 * D
        CAPACITY = 0.5
        b, s, d = x.shape
        weights = (jnp.einsum('bsd,do->bso', x, wr) + br)[..., 0]
        k = max(1, int(CAPACITY * s))
        kk = k - 1 if k > 1 else 1
        _, idx = jax.lax.top_k(weights, k)
        sel_idx = idx[:, :kk]
        sel = jnp.take_along_axis(x, sel_idx[:, :, None], axis=1)
        h = jax.nn.gelu(jnp.einsum('bkd,dh->bkh', sel, w1) + b1)
        y = jnp.einsum('bkh,hd->bkd', h, w2) + b2
        w_sel = jnp.take_along_axis(weights, sel_idx, axis=1)
        y = y * w_sel[..., None]
        batch_idx = jnp.arange(b)[:, None]
        processed = jnp.zeros_like(x).at[batch_idx, sel_idx].set(y)
        return processed + x

    def _L1_gnn_ref(x, edge_index, g0, b0, W1a, b1a, g1, bt1, W1b, b1b, W2a, b2a, g2, bt2, W2b, b2b):
        import jax, jax.numpy as jnp
        import numpy as np
        N = 12500
        E = 200000
        D = 256
        BN_EPS = 1e-05

        def _batchnorm(x, gamma, beta):
            mu = jnp.mean(x, axis=0)
            var = jnp.var(x, axis=0)
            return (x - mu) * jax.lax.rsqrt(var + BN_EPS) * gamma + beta

        def _gin_conv(x, src, dst, n, W1, b1, gamma, beta, W2, b2):
            agg = jax.ops.segment_sum(x[src], dst, num_segments=n)
            h = x + agg
            h = jax.nn.relu(_batchnorm(h @ W1 + b1, gamma, beta))
            return jax.nn.relu(h @ W2 + b2)
        n = x.shape[0]
        src, dst = (edge_index[0], edge_index[1])
        h = _batchnorm(x, g0, b0)
        h = _gin_conv(h, src, dst, n, W1a, b1a, g1, bt1, W1b, b1b)
        h = jax.nn.relu(h)
        h = _gin_conv(h, src, dst, n, W2a, b2a, g2, bt2, W2b, b2b)
        return jax.nn.relu(h)

    def _L1_ffn_ref(x, sW1, sb1, sW2, sb2, sW3, sb3, eW1, eb1, eW2, eb2, eW3, eb3, gW, gb):
        import jax, jax.numpy as jnp
        import numpy as np
        B, A = (512, 8)
        IN, OUT = (256, 256)
        SH1, SH2 = (256, 128)
        EH1, EH2 = (128, 64)
        E, TOPK = (4, 2)

        def _shared_mlp(x, W1, b1, W2, b2, W3, b3):
            h = jax.nn.relu(x @ W1 + b1)
            h = jax.nn.relu(h @ W2 + b2)
            return h @ W3 + b3

        def _experts_mlp(x, eW1, eb1, eW2, eb2, eW3, eb3):
            h = jax.nn.relu(jnp.einsum('baf,efh->ebah', x, eW1) + eb1[:, None, None, :])
            h = jax.nn.relu(jnp.einsum('ebah,ehg->ebag', h, eW2) + eb2[:, None, None, :])
            o = jnp.einsum('ebag,ego->ebao', h, eW3) + eb3[:, None, None, :]
            return jnp.moveaxis(o, 0, -1)
        all_out = _experts_mlp(x, eW1, eb1, eW2, eb2, eW3, eb3)
        shared = _shared_mlp(x, sW1, sb1, sW2, sb2, sW3, sb3)
        gates = jax.nn.softmax(x @ gW + gb, axis=-1)
        topv, topi = jax.lax.top_k(gates, TOPK)
        topw = jax.nn.softmax(topv, axis=-1)
        sel = jnp.take_along_axis(all_out, topi[:, :, None, :], axis=-1)
        gated = jnp.sum(sel * topw[:, :, None, :], axis=-1)
        return shared + gated
    edge_index = jnp.stack([src, dst])
    x = x + _L0_gnn_ref(_layernorm(x, axis=-1), src, dst, edge_type_8, L0_gnn_basis, L0_gnn_comp, L0_gnn_loop_weight, L0_gnn_bias_param)
    x = x + _L0_ffn_ref(_layernorm(x, axis=-1)[None], L0_ffn_attention_mask, L0_ffn_wr, L0_ffn_br, L0_ffn_w1, L0_ffn_b1, L0_ffn_w2, L0_ffn_b2)[0]
    x = x + _L1_gnn_ref(_layernorm(x, axis=-1), edge_index, L1_gnn_g0, L1_gnn_b0, L1_gnn_W1a, L1_gnn_b1a, L1_gnn_g1, L1_gnn_bt1, L1_gnn_W1b, L1_gnn_b1b, L1_gnn_W2a, L1_gnn_b2a, L1_gnn_g2, L1_gnn_bt2, L1_gnn_W2b, L1_gnn_b2b)
    x = x + _L1_ffn_ref(_layernorm(x, axis=-1)[None], L1_ffn_sW1, L1_ffn_sb1, L1_ffn_sW2, L1_ffn_sb2, L1_ffn_sW3, L1_ffn_sb3, L1_ffn_eW1, L1_ffn_eb1, L1_ffn_eW2, L1_ffn_eb2, L1_ffn_eW3, L1_ffn_eb3, L1_ffn_gW, L1_ffn_gb)[0]
    return x

_drawn_inputs = setup_inputs


def setup_inputs(seed=0):
    import zlib

    import numpy as np

    out = dict(_drawn_inputs(seed))
    spreads = {'L0_gnn_bias_param': (0.0, 0.8),
     'L0_ffn_b1': (0.0, 0.8),
     'L0_ffn_b2': (0.0, 0.8),
     'L1_gnn_g0': (1.0, 0.6),
     'L1_gnn_b0': (0.0, 0.8),
     'L1_gnn_b1a': (0.0, 2.0),
     'L1_gnn_g1': (1.0, 0.6),
     'L1_gnn_bt1': (0.0, 0.8),
     'L1_gnn_b1b': (0.0, 0.8),
     'L1_gnn_b2a': (0.0, 2.0),
     'L1_gnn_g2': (1.0, 0.6),
     'L1_gnn_bt2': (0.0, 0.8),
     'L1_gnn_b2b': (0.0, 0.8),
     'L1_ffn_sb1': (0.0, 0.8),
     'L1_ffn_sb2': (0.0, 2.0),
     'L1_ffn_sb3': (0.0, 2.0),
     'L1_ffn_eb1': (0.0, 0.8),
     'L1_ffn_eb2': (0.0, 2.0),
     'L1_ffn_eb3': (0.0, 2.0),
     'L1_ffn_gb': (0.0, 0.8)}
    factors = {'L0_ffn_wr': 8.0,
     'L0_ffn_w1': 8.0,
     'L0_ffn_w2': 8.0,
     'L1_gnn_W1a': 8.0,
     'L1_gnn_W1b': 8.0,
     'L1_gnn_W2a': 6.242,
     'L1_gnn_W2b': 4.958,
     'L1_ffn_sW1': 5.919,
     'L1_ffn_sW2': 5.35,
     'L1_ffn_sW3': 4.386,
     'L1_ffn_eW1': 8.0,
     'L1_ffn_eW2': 8.0,
     'L1_ffn_eW3': 8.0,
     'L1_ffn_gW': 8.0}
    for name, (base, spread) in spreads.items():
        noise = np.random.default_rng([zlib.crc32(name.encode()), seed]).standard_normal(out[name].shape)
        drawn = base * np.exp(spread * noise) if base else spread * noise
        out[name] = jnp.asarray(drawn.astype(out[name].dtype))
    for name, factor in factors.items():
        out[name] = (out[name] * factor).astype(out[name].dtype)
    return out
```

```python
from contextlib import ExitStack

import concourse.bass as bass
from concourse import mybir

F32 = mybir.dt.float32
BF16 = mybir.dt.bfloat16
I32 = mybir.dt.int32
ALU = mybir.AluOpType
ACT = mybir.ActivationFunctionType
AX = mybir.AxisListType.X

P = 128
N = 2500
D = 256
KD = D // P
E = 80000
TP = 125
NT = N // TP
TG = 4
G = NT // TG
GN = TP * TG
CH = E // P
CJ = CH // TP
U = 4
PAD = CH + U
R = 8
NB = 4
H = 1024
HM = H // P
KEEP = 1249
EPS = 1e-5
NE = 4
EH1, EH2 = 128, 64
FAR = 4096.0


class Count:

    def __init__(self, sem):
        self.sem, self.base, self.k, self.reg, self.per = sem, 0, 0, None, 0

    def step(self, ins):
        ins.then_inc(self.sem, 1)
        self.k += 1
        return self.at(self.k)

    def at(self, k):
        return self.base + k if self.reg is None else self.reg * self.per + (self.base + k)

    def enter(self, reg, per):
        self.base, self.k, self.reg, self.per = self.base + self.k, 0, reg, per

    def leave(self, trips):
        assert self.k == self.per, (self.k, self.per)
        self.base, self.k, self.reg = self.base + trips * self.per, 0, None


def gnn_ffn_kernel(nc, a, out, h_table, x_table):
    with ExitStack() as ctx:
        def sb(name, shape, dt=F32):
            return ctx.enter_context(nc.sbuf_tensor(name, shape, dt))

        def sem(name):
            return ctx.enter_context(nc.semaphore(name))

        bank = [ctx.enter_context(nc.psum_tensor(f"bank{i}", [P, 512], F32)) for i in range(8)]

        X = sb("X", [TP, NT, D])
        Y = sb("Y", [TP, NT, D])
        XT = sb("XT", [P, KD, N])
        ZT = sb("ZT", [P, KD, N])

        ident = sb("ident", [P, P])
        ones = sb("ones", [P, P])
        zeros = sb("zeros", [P, D], BF16)
        node_no = sb("node_no", [P, NT * P])
        below = sb("below", [TP, 2 * N], BF16)
        half = sb("half", [P, NT])
        chunk_no = sb("chunk_no", [NT, CH])
        tile_lo = sb("tile_lo", [NT, 1])
        tile_hi = sb("tile_hi", [NT, 1])
        earlier = sb("earlier", [TP, TG * NE * NE])

        src_of = sb("src_of", [P, PAD], I32)
        hrow_of = sb("hrow_of", [P, PAD], I32)
        dst_of = sb("dst_of", [P, PAD])
        rng = sb("rng", [1, 2 * NT], I32)
        slot = sb("slot", [P, U], I32)
        msg = sb("msg", [P, U, D])
        onehot = sb("onehot", [P, U, P])
        u_tile = sb("u_tile", [TP, D])

        nrm = sb("nrm", [TP, TG, D])
        stats = sb("stats", [TP, TG, 6])
        mv = sb("mv", [TP, TG, 2])
        veps = sb("veps", [TP, TG])
        rstd = sb("rstd", [TP, TG])
        pT = sb("pT", [P, KD, GN])

        bias_row = sb("bias_row", [1, D])
        b2_row = sb("b2_row", [1, D])
        b1b_row = sb("b1b_row", [1, D])
        b2b_row = sb("b2b_row", [1, D])
        sb3_row = sb("sb3_row", [1, D])
        gb_row = sb("gb_row", [1, NE])
        br_col = sb("br_col", [P, 1])
        wr_col = sb("wr_col", [P, KD])
        wr_rep = sb("wr_rep", [P, KD, P])
        b1_col = sb("b1_col", [P, HM])
        gin_col = sb("gin_col", [P, 8, KD])
        sb1_col = sb("sb1_col", [P, KD])
        sb2_col = sb("sb2_col", [P, 1])
        eb1_col = sb("eb1_col", [P, NE])
        eb2_col = sb("eb2_col", [EH2, NE])
        comp_bc = sb("comp_bc", [P, R * NB])
        bn_st = sb("bn_st", [P, KD, G, 6])
        bn_mv = sb("bn_mv", [P, KD, 2])
        bn_ve = sb("bn_ve", [P, KD])
        bn_rs = sb("bn_rs", [P, KD])
        bn_sc = sb("bn_sc", [P, KD])
        bn_ms = sb("bn_ms", [P, KD])
        bn_bi = sb("bn_bi", [P, KD])

        scratch = sb("scratch", [P, 11264])
        at = {"n": 0}

        def carve(width, parts=P):
            v = scratch[0:parts, at["n"]:at["n"] + width]
            at["n"] += width
            assert at["n"] <= 11264, at
            return v

        at["n"] = 0
        W0 = carve(KD * (R + 1) * D).rearrange("p (k n) -> p k n", k=KD)
        basis = carve(NB * KD * D).rearrange("p (b k o) -> p b k o", b=NB, k=KD)
        hst = carve(2 * R * D, TP).rearrange("p (u n) -> p u n", u=2)
        edge_i = XT[0:TP, 0, 0:3 * 640].bitcast(I32).rearrange("p (a n) -> p a n", a=3)
        edge_f = XT[0:TP, 1, 0:3 * 640 - 0].rearrange("p (a n) -> p a n", a=3)
        spread = ZT[0:TP, :, 0:CH]
        near = Y[0:NT, 0:5, :].rearrange("p a b -> p (a b)")
        cmax = sb("cmax", [TP, 2, CJ])
        lohi = sb("lohi", [NT, 2])
        at["n"] = 0
        w1 = carve(KD * H).rearrange("p (k n) -> p k n", k=KD)
        w2 = carve(HM * D).rearrange("p (k n) -> p k n", k=HM)
        hT = carve(HM * GN).rearrange("p (m n) -> p m n", m=HM)
        WB = carve(N)
        rank_tmp = ZT[0:TP, 0, :]
        rank_tmp2 = ZT[0:TP, 1, :]
        wcol = sb("wcol", [TP, NT])
        cnt = sb("cnt", [TP, 2, NT])
        rank = sb("rank", [TP, NT])
        gate_w = sb("gate_w", [TP, NT])
        at["n"] = 0
        gw = carve(4 * KD * D).rearrange("p (w k n) -> p w k n", w=4, k=KD)
        zs = carve(KD * GN).rearrange("p (k n) -> p k n", k=KD)
        bn_rep = carve(4 * P).rearrange("p (q n) -> p q n", q=4)
        bn_row = carve(4 * P, TP)
        at["n"] = 0
        sW1 = carve(KD * D).rearrange("p (k n) -> p k n", k=KD)
        sW2 = carve(KD * P).rearrange("p (k n) -> p k n", k=KD)
        sW3 = carve(D)
        eW1 = carve(NE * KD * EH1).rearrange("p (e k n) -> p e k n", e=NE, k=KD)
        eW2 = carve(NE * EH2).rearrange("p (e n) -> p e n", e=NE)
        eW3 = carve(NE * D, EH2 + 1).rearrange("p (e n) -> p e n", e=NE)
        gW = carve(KD * NE).rearrange("p (k n) -> p k n", k=KD)
        s1 = carve(KD * GN).rearrange("p (k n) -> p k n", k=KD)
        e1 = carve(NE * GN).rearrange("p (k n) -> p k n", k=NE)
        s2 = carve(GN)
        e2 = carve(NE * GN, EH2 + 1).rearrange("p (k n) -> p k n", k=NE)
        small = sb("small", [TP, 8, TG * NE])
        pair = sb("pair", [TP, 2, TG * NE * NE])
        gred = sb("gred", [TP, 4, TG])

        ld_edges, ld_x, ld_w0 = sem("ld_edges"), sem("ld_x"), sem("ld_w0")
        ld_small, ld_ffn, ld_gin, ld_moe = sem("ld_small"), sem("ld_ffn"), sem("ld_gin"), sem("ld_moe")
        consts = sem("consts")
        dve_order = sem("dve_order")
        dve_passed, sp_passed = sem("dve_passed"), sem("sp_passed")
        edges_f, edges_t, edges_ev = sem("edges_f"), sem("edges_t"), sem("edges_ev")
        spread_ok, spread_bc, lohi_ok, lohi_t, rng_ok = (sem(n) for n in (
            "spread_ok", "spread_bc", "lohi_ok", "lohi_t", "rng_ok"))
        ln_var, ln_rstd, ln_nrm, ln_t, ln_ev, ln_kept = (sem(n) for n in (
            "ln_var", "ln_rstd", "ln_nrm", "ln_t", "ln_ev", "ln_kept"))
        w0_ok, h_mm, h_act, h_dve, hst_free, h_stored, table_ok = (sem(n) for n in (
            "w0_ok", "h_mm", "h_act", "h_dve", "hst_free", "h_stored", "table_ok"))
        hst_dma = [sem(f"hst_dma{i}") for i in range(2)]
        used, hot, slot_ok = sem("used"), sem("hot"), sem("slot_ok")
        gathered = [sem(f"gathered{u}") for u in range(U)]
        tile_sum, tile_read, u_t, u_ev = sem("tile_sum"), sem("tile_read"), sem("u_t"), sem("u_ev")
        wr_ok, wb_mm, wb_ok, gate_ok, x_plus = (sem(n) for n in ("wr_ok", "wb_mm", "wb_ok", "gate_ok", "x_plus"))
        f1, f1e, f2, f2e = sem("f1"), sem("f1e"), sem("f2"), sem("f2e")
        bn_ve_ok, bn_rs_ok, bn_ok, bn_mm, bn_row_ok, y_ok, x_st = (sem(n) for n in (
            "bn_ve_ok", "bn_rs_ok", "bn_ok", "bn_mm", "bn_row_ok", "y_ok", "x_st"))
        c1, c1e, c1s, zs_ok, c2, c2e = (sem(n) for n in ("c1", "c1e", "c1s", "zs_ok", "c2", "c2e"))
        m1, m1e, m2, m2e, mg, mg_ev, mexp, mc, m3, m3e, o_ok, o_st, e2_ones = (sem(n) for n in (
            "m1", "m1e", "m2", "m2e", "mg", "mg_ev", "mexp", "mc", "m3", "m3e", "o_ok", "o_st", "e2_ones"))

        ctx.enter_context(nc.allow_non_contiguous_dma(reason="bias columns and per-tile rows"))
        block = ctx.enter_context(nc.Block())

        LN = {"stage0": 0, "stage1": 1, "stage2": 2, "stage3": 3}

        @block.sync
        def _(sp):
            def node_dma(dst, src, lo, hi, s):
                sp.dma_start(dst(0, lo), src(0, lo)).then_inc(s, 16)
                sp.dma_start(dst(lo, hi), src(lo, hi)).then_inc(s, 16)

            for i, name in enumerate(("src", "edge_type_8", "dst")):
                v = a[name].rearrange("(p n) -> p n", p=TP)
                node_dma(lambda l, h: edge_i[l:h, i, :], lambda l, h: v[l:h, :], 112, TP, ld_edges)
            xv = a["x"].rearrange("(t p) d -> p t d", p=TP)
            node_dma(lambda l, h: X[l:h, :, :], lambda l, h: xv[l:h, :, :], 112, TP, ld_x)
            sp.dma_start(basis, a["L0_gnn_basis"].rearrange("b (k p) o -> p b k o", p=P)).then_inc(ld_w0, 16)
            sp.dma_start(W0[:, :, R * D:(R + 1) * D],
                         a["L0_gnn_loop_weight"].rearrange("(k p) o -> p k o", p=P)).then_inc(ld_w0, 16)
            sp.dma_start(comp_bc[:, :], a["L0_gnn_comp"].rearrange("r b -> (r b)").partition_broadcast(P)).then_inc(ld_w0, 16)
            sp.dma_start(bias_row[:, :], a["L0_gnn_bias_param"].unsqueeze(0)).then_inc(ld_w0, 16)

            hv = h_table.rearrange("(t p r) o -> t p (r o)", p=TP, r=R)
            with sp.Fori(0, NT // 2) as g:
                for u in range(2):
                    sp.wait_ge(h_act, g * 4 + (2 * u + 4))
                    sp.sem_inc(sp_passed, 1)
                    sp.wait_ge(h_dve, g * 6 + (3 * u + 6))
                    sp.sem_inc(sp_passed, 1)
                    for lo, hi in ((0, 112), (112, TP)):
                        sp.dma_start(hv[bass.ds(g * 2 + u, 1), lo:hi, :].rearrange("a p n -> (a p) n"),
                                     hst[lo:hi, u, :]).then_inc(hst_dma[u], 16)
                    sp.wait_ge(hst_dma[u], g * 32 + 32)
                    sp.sem_inc(hst_free, 1)
            sp.sem_inc(table_ok, 1)

            sp.wait_ge(tile_read, 1 + NT)
            sp.dma_start(w1, a["L0_ffn_w1"].rearrange("(k p) n -> p k n", p=P)).then_inc(ld_ffn, 16)
            sp.dma_start(w2, a["L0_ffn_w2"].rearrange("(k p) n -> p k n", p=P)).then_inc(ld_ffn, 16)
            sp.wait_ge(f2e, 2 + NT)
            for i, name in enumerate(("L1_gnn_W1a", "L1_gnn_W1b", "L1_gnn_W2a", "L1_gnn_W2b")):
                sp.dma_start(gw[:, i, :, :], a[name].rearrange("(k p) n -> p k n", p=P)).then_inc(ld_gin, 16)
            tv = x_table.rearrange("(t p) o -> p t o", p=TP)
            for layer in range(2):
                sp.wait_ge(y_ok, 2 * (layer + 1))
                node_dma(lambda l, h: tv[l:h, :, :], lambda l, h: Y[l:h, :, :], 112, TP, x_st)
                sp.wait_ge(x_st, 32 * (layer + 1))
                sp.sem_inc(table_ok, 1)
            sp.wait_ge(c2e, 2 + 2 * NT)
            moe = [(sW1, a["L1_ffn_sW1"].rearrange("(k p) n -> p k n", p=P)),
                   (sW2, a["L1_ffn_sW2"].rearrange("(k p) n -> p k n", p=P)),
                   (sW3, a["L1_ffn_sW3"]),
                   (eW1, a["L1_ffn_eW1"].rearrange("e (k p) n -> p e k n", p=P)),
                   (eW2, a["L1_ffn_eW2"].rearrange("e p n -> p e n")),
                   (eW3[0:EH2, :, :], a["L1_ffn_eW3"].rearrange("e p n -> p e n")),
                   (eW3[EH2:EH2 + 1, :, :], a["L1_ffn_eb3"].unsqueeze(0)),
                   (gW, a["L1_ffn_gW"].rearrange("(k p) n -> p k n", p=P))]
            for dst, src in moe:
                sp.dma_start(dst, src).then_inc(ld_moe, 16)
            ov = out.rearrange("(t p) d -> p t d", p=TP)
            with sp.Fori(0, G) as g:
                sp.wait_ge(o_ok, g * TG + (TG + 1))
                sp.sem_inc(sp_passed, 1)
                for lo, hi in ((0, 112), (112, TP)):
                    sp.dma_start(ov[lo:hi, bass.ds(g * TG, TG), :], X[lo:hi, bass.ds(g * TG, TG), :]).then_inc(o_st, 16)
            sp.wait_ge(o_st, 32 * G)

        @block.gpsimd
        def _(pool):
            pool.memset(ident[:, :], 0.0).then_inc(consts, 1)
            pool.memset(ones[:, :], 1.0).then_inc(consts, 1)
            pool.memset(zeros[:, :], 0.0).then_inc(consts, 1)
            pool.memset(half[:, :], -0.5).then_inc(consts, 1)
            pool.memset(below[:, :], 1.0).then_inc(consts, 1)
            pool.memset(earlier[:, :], 1.0).then_inc(consts, 1)
            pool.memset(dst_of[:, CH:PAD], -1.0).then_inc(consts, 1)
            pool.memset(src_of[:, CH:PAD], 0).then_inc(consts, 1)
            pool.memset(hrow_of[:, CH:PAD], 0).then_inc(consts, 1)
            pool.iota(node_no[:, :], pattern=[[1, NT * P]], base=0, channel_multiplier=0,
                      allow_small_or_imprecise_dtypes=True).then_inc(consts, 1)
            pool.iota(chunk_no[:, :], pattern=[[1, CH]], base=0, channel_multiplier=0,
                      allow_small_or_imprecise_dtypes=True).then_inc(consts, 1)
            pool.iota(tile_lo[:, :], pattern=[[1, 1]], base=0, channel_multiplier=TP,
                      allow_small_or_imprecise_dtypes=True).then_inc(consts, 1)
            pool.iota(tile_hi[:, :], pattern=[[1, 1]], base=TP, channel_multiplier=TP,
                      allow_small_or_imprecise_dtypes=True).then_inc(consts, 1)
            pool.wait_ge(consts, 13)
            pool.affine_select(out=ident[:, :], in_=ident[:, :], compare_op=ALU.not_equal, fill=1.0,
                               base=0, pattern=[[-1, P]], channel_multiplier=1).then_inc(consts, 1)
            pool.affine_select(out=below[:, :], in_=below[:, :], compare_op=ALU.is_gt, fill=0.0,
                               base=N, pattern=[[-1, 2 * N]], channel_multiplier=1).then_inc(consts, 1)
            pool.affine_select(out=earlier[:, :].rearrange("p (t e j) -> p t e j", t=TG, e=NE),
                               in_=earlier[:, :].rearrange("p (t e j) -> p t e j", t=TG, e=NE),
                               compare_op=ALU.is_gt, fill=0.0, base=0,
                               pattern=[[0, TG], [1, NE], [-1, NE]], channel_multiplier=0).then_inc(consts, 1)
            def col(dst, name, **kw):
                pool.dma_start(dst, a[name].rearrange("(m p) -> p m", **kw)).then_inc(ld_small, 16)
            col(b1_col[:, :], "L0_ffn_b1", p=P)
            for i, name in enumerate(("L1_gnn_g0", "L1_gnn_b0", "L1_gnn_b1a", "L1_gnn_g1", "L1_gnn_bt1",
                                      "L1_gnn_b2a", "L1_gnn_g2", "L1_gnn_bt2")):
                col(gin_col[:, i, :], name, p=P)
            col(sb1_col[:, :], "L1_ffn_sb1", p=P)
            col(sb2_col[:, :], "L1_ffn_sb2", p=P)
            pool.dma_start(eb1_col[:, :], a["L1_ffn_eb1"].rearrange("e p -> p e")).then_inc(ld_small, 16)
            pool.dma_start(eb2_col[:, :], a["L1_ffn_eb2"].rearrange("e p -> p e")).then_inc(ld_small, 16)
            pool.dma_start(wr_col[:, :], a["L0_ffn_wr"].rearrange("(k p) o -> p (k o)", p=P)).then_inc(ld_small, 16)
            pool.dma_start(br_col[:, :], a["L0_ffn_br"].partition_broadcast(P)).then_inc(ld_small, 16)
            for dst, name in ((b2_row, "L0_ffn_b2"), (b1b_row, "L1_gnn_b1b"), (b2b_row, "L1_gnn_b2b"),
                              (sb3_row, "L1_ffn_sb3"), (gb_row, "L1_ffn_gb")):
                pool.dma_start(dst[:, :], a[name].unsqueeze(0)).then_inc(ld_small, 16)

            def ln_root(g, ln):
                pool.wait_ge(ln_var, g + (ln * G + 1))
                pool.tensor_tensor(rstd[:, :], veps[:, :], half[0:TP, 0:TG], ALU.pow).then_inc(ln_rstd, 1)

            sent = pool.alloc_register("sent")
            pool.reg_mov(sent, 0)

            def edge_pass(k, table, rows):
                pool.wait_ge(table_ok, k + 1)
                if k == 0:
                    pool.wait_ge(rng_ok, 1)
                with pool.Fori(0, NT) as t:
                    first = pool.value_load(rng[0:1, bass.ds(t, 1)], min_val=0, max_val=CH - 1)
                    end = pool.value_load(rng[0:1, bass.ds(t + NT, 1)], min_val=1, max_val=CH)
                    with pool.Fori(first, end, U) as c:
                        n = pool.snap(sent, min_val=0, max_val=3 * NT * PAD)
                        for u in range(U):
                            pool.wait_ge(used, n + (u + 1))
                            pool.tensor_copy(slot[:, u:u + 1], rows[:, bass.ds(c + u, 1)]).then_inc(slot_ok, 1)
                        for u in range(U):
                            pool.wait_ge(table_ok, k + 1)
                            if u == 0:
                                pool.wait_ge(slot_ok, n + U)
                            pool.indirect_dma_start(msg[:, u, :], None, table,
                                                    bass.IndirectOffsetOnAxis(slot[:, u:u + 1], 0)).then_inc(gathered[u], 16)
                        pool.reg_add(sent, sent, U)

            with pool.Fori(0, G) as g:
                ln_root(g, 0)
            edge_pass(0, h_table, hrow_of)

            with pool.Fori(0, G) as g:
                ln_root(g, 1)
                pool.wait_ge(ln_nrm, g * TG + (1 * NT + TG))
                pool.tensor_copy(Y[:, bass.ds(g * TG, TG), :], nrm[:, :, :]).then_inc(ln_kept, 1)
            pool.wait_ge(ln_kept, 1 + G)
            pool.tensor_tensor(X[:, :, :], X[:, :, :], Y[:, :, :], ALU.add).then_inc(x_plus, 1)

            with pool.Fori(0, G) as g:
                ln_root(g, 2)
                pool.wait_ge(ln_nrm, g * TG + (2 * NT + TG))
                pool.tensor_copy(Y[:, bass.ds(g * TG, TG), :], nrm[:, :, :]).then_inc(ln_kept, 1)
            for layer in range(2):
                if layer == 0:
                    pool.wait_ge(bn_ve_ok, 1)
                    pool.tensor_tensor(bn_rs[:, :], bn_ve[:, :], half[:, 0:KD], ALU.pow).then_inc(bn_rs_ok, 1)
                edge_pass(1 + layer, x_table, src_of)
                pool.wait_ge(bn_ve_ok, 2 + layer)
                pool.tensor_tensor(bn_rs[:, :], bn_ve[:, :], half[:, 0:KD], ALU.pow).then_inc(bn_rs_ok, 1)

            pool.wait_ge(ld_moe, 16 * 8)
            pool.memset(e2[EH2:EH2 + 1, :, :], 1.0).then_inc(e2_ones, 1)
            pool.wait_ge(e2_ones, 1)
            with pool.Fori(0, G) as g:
                ln_root(g, 3)

        @block.vector
        def _(dve):
            order = Count(dve_order)

            def link(ins):
                dve.wait_ge(dve_order, order.step(ins))

            dve.wait_ge(ld_edges, 96)
            order.step(nc.vector.tensor_copy(edge_f[:, 0, :], edge_i[:, 0, :]))
            order.step(nc.vector.tensor_copy(edge_f[:, 1, :], edge_i[:, 1, :]))
            link(nc.vector.tensor_copy(edge_f[:, 2, :], edge_i[:, 2, :]))
            nc.vector.scalar_tensor_tensor(out=edge_f[:, 1, :], in0=edge_f[:, 0, :], scalar=float(R),
                                           in1=edge_f[:, 1, :], op0=ALU.mult, op1=ALU.add).then_inc(edges_f, 1)
            targets = edge_f[:, 2, :].rearrange("p (j e) -> p j e", j=CJ)
            order.step(nc.vector.tensor_reduce(cmax[:, 0, :], targets, AX, ALU.max))
            link(nc.vector.tensor_reduce(cmax[:, 1, :], targets, AX, ALU.min))
            dve.wait_ge(consts, 16)
            for i in range(2):
                nc.vector.tensor_tensor(
                    spread[:, i, :].rearrange("p (q j) -> p q j", j=CJ),
                    ident[0:TP, 0:TP].unsqueeze(2).to_broadcast([TP, TP, CJ]),
                    cmax[:, i, :].unsqueeze(1).to_broadcast([TP, TP, CJ]), ALU.mult).then_inc(spread_ok, 1)
            for i, dst in enumerate((src_of, hrow_of, dst_of)):
                dve.wait_ge(edges_t, i + 1)
                v = dst[:, 0:CH].rearrange("p (q j) -> p j q", j=CJ)
                nc.vector.tensor_copy(v[:, 0:4, :], bank[2 * i][:, 0:4 * TP].rearrange("p (j q) -> p j q", j=4)).then_inc(edges_ev, 1)
                nc.vector.tensor_copy(v[:, 4, :], bank[2 * i + 1][:, 0:TP]).then_inc(edges_ev, 1)
            for i, (limit, op, far, red) in enumerate(((tile_lo, ALU.is_lt, FAR, ALU.min), (tile_hi, ALU.is_ge, -FAR, ALU.max))):
                dve.wait_ge(spread_bc, i + 1)
                for b, lo, hi in ((0, 0, 512), (1, 512, CH)):
                    src = bank[(6, 0)[i] + b][0:NT, 0:hi - lo]
                    link(nc.vector.tensor_scalar(near[:, lo:hi], src, limit[:, :], far, op, ALU.mult))
                link(nc.vector.tensor_tensor(near[:, 0:CH], near[:, 0:CH], chunk_no[:, :], ALU.add))
                link(nc.vector.tensor_reduce(lohi[:, i:i + 1], near[:, 0:CH], AX, red))
            link(nc.vector.tensor_scalar(lohi[:, 0:1], lohi[:, 0:1], float(CH - 1), None, ALU.min))
            link(nc.vector.tensor_tensor(lohi[:, 1:2], lohi[:, 1:2], lohi[:, 0:1], ALU.max))
            nc.vector.tensor_scalar(lohi[:, 1:2], lohi[:, 1:2], 1.0, None, ALU.add).then_inc(lohi_ok, 1)
            dve.wait_ge(lohi_t, 1)
            dve.wait_ge(edges_ev, 6)
            nc.vector.tensor_copy(rng[:, :], bank[2][0:1, 0:2 * NT]).then_inc(rng_ok, 1)

            dve.wait_ge(ld_w0, 64)
            for b in range(NB):
                for r in range(R):
                    w = W0[:, :, r * D:(r + 1) * D]
                    c = comp_bc[:, r * NB + b:r * NB + b + 1]
                    if b == 0:
                        order.step(nc.vector.tensor_scalar(w, basis[:, b, :, :], c, None, ALU.mult))
                    else:
                        dve.wait_ge(dve_order, order.at(order.k - R + 1))
                        order.step(nc.vector.scalar_tensor_tensor(out=w, in0=basis[:, b, :, :], scalar=c, in1=w,
                                                                  op0=ALU.mult, op1=ALU.add))
            dve.wait_ge(dve_order, order.at(order.k))
            dve.sem_inc(w0_ok, 1)

            def layernorm(g, ln):
                for j in range(TG):
                    s = order.step(nc.vector.bn_stats(stats[:, j, :], X[:, bass.ds(g * TG + j, 1), :].rearrange("p a d -> p (a d)")))
                dve.wait_ge(dve_order, s)
                dve.sem_inc(dve_passed, 1)
                for j in range(TG):
                    s = order.step(nc.vector.bn_aggr(mv[:, j, :], stats[:, j, :]))
                dve.wait_ge(dve_order, s)
                nc.vector.tensor_scalar(veps[:, :], mv[:, :, 1], EPS, None, ALU.add).then_inc(ln_var, 1)
                dve.wait_ge(ln_rstd, g + (ln * G + 1))
                dve.wait_ge(ln_t, g + (ln * G + 1))
                if ln == 3:
                    dve.wait_ge(ln_kept, 1 + 2 * G)
                elif ln:
                    dve.wait_ge(ln_kept, g + ((ln - 1) * G + 1))
                for j in range(TG):
                    nc.vector.tensor_scalar(nrm[:, j, :], X[:, bass.ds(g * TG + j, 1), :].rearrange("p a d -> p (a d)"),
                                            mv[:, j, 0:1], rstd[:, j:j + 1], ALU.subtract, ALU.mult).then_inc(ln_nrm, 1)

            dve.wait_ge(ld_x, 32)
            LN_STEPS = 2 * TG
            with dve.Fori(0, G) as g:
                order.enter(g, LN_STEPS)
                layernorm(g, 0)
                for j in range(TG):
                    dve.wait_ge(hst_free, g * TG + (j + 1))
                    for b in (2, 3):
                        dve.wait_ge(h_mm, g * (5 * TG) + (5 * j + b + 1))
                        nc.vector.tensor_copy(hst[:, j % 2, b * 512:(b + 1) * 512], bank[2 + b][0:TP, :]).then_inc(h_dve, 1)
                    dve.wait_ge(h_mm, g * (5 * TG) + (5 * j + 5))
                    xt = X[:, bass.ds(g * TG + j, 1), :].rearrange("p a d -> p (a d)")
                    nc.vector.tensor_tensor(xt, xt, bank[6][0:TP, 0:D], ALU.add).then_inc(h_dve, 1)
            order.leave(G)

            made = dve.alloc_register("made")
            dve.reg_mov(made, 0)

            def edge_pass(k, fold):
                with dve.Fori(0, NT) as t:
                    first = dve.value_load(rng[0:1, bass.ds(t, 1)], min_val=0, max_val=CH - 1)
                    end = dve.value_load(rng[0:1, bass.ds(t + NT, 1)], min_val=1, max_val=CH)
                    with dve.Fori(first, end, U) as c:
                        n = dve.snap(made, min_val=0, max_val=3 * NT * PAD)
                        for u in range(U):
                            dve.wait_ge(used, n + (u + 1))
                            nc.vector.tensor_scalar(onehot[:, u, :], node_no[:, bass.ds(t * TP, P)],
                                                    dst_of[:, bass.ds(c + u, 1)], None, ALU.is_equal).then_inc(hot, 1)
                        dve.reg_add(made, made, U)
                    dve.wait_ge(tile_sum, t + (k * NT + 1))
                    fold(t)

            dve.wait_ge(rng_ok, 1)
            dve.wait_ge(h_dve, 3 + 3 * NT)

            def into_x(t):
                xt = X[:, bass.ds(t, 1), :].rearrange("p a d -> p (a d)")
                nc.vector.tensor_tensor(xt, xt, bank[0][0:TP, 0:D], ALU.add).then_inc(tile_read, 1)

            edge_pass(0, into_x)
            dve.wait_ge(tile_read, 1 + NT)

            dve.wait_ge(ld_small, 16 * 20)
            for k in range(KD):
                nc.vector.tensor_scalar(wr_rep[:, k, :], ones[:, :], wr_col[:, k:k + 1], None, ALU.mult).then_inc(wr_ok, 1)
            with dve.Fori(0, G) as g:
                order.enter(g, LN_STEPS)
                layernorm(g, 1)
            order.leave(G)
            dve.wait_ge(wb_ok, 1 + G)
            link(nc.vector.tensor_tensor(rank_tmp.rearrange("p (t q) -> p t q", t=NT),
                                         WB[0:TP, :].rearrange("p (t q) -> p t q", t=NT),
                                         ident[0:TP, 0:TP].unsqueeze(1).to_broadcast([TP, NT, TP]), ALU.mult))
            link(nc.vector.tensor_reduce(wcol[:, :], rank_tmp.rearrange("p (t q) -> p t q", t=NT), AX, ALU.add))
            for t in range(NT):
                if t:
                    dve.wait_ge(dve_order, order.at(order.k - 1))
                order.step(nc.vector.tensor_scalar(rank_tmp, WB[0:TP, :], wcol[:, t:t + 1], None, ALU.is_gt, ALU.add,
                                                   accum_out=cnt[:, 0, t:t + 1]))
                if t:
                    dve.wait_ge(dve_order, order.at(order.k - 1))
                s = order.step(nc.vector.scalar_tensor_tensor(out=rank_tmp2, in0=WB[0:TP, :], scalar=wcol[:, t:t + 1],
                                                          in1=below[:, N - t * TP:2 * N - t * TP],
                                                          op0=ALU.is_equal, op1=ALU.mult,
                                                          accum_out=cnt[:, 1, t:t + 1]))
            dve.wait_ge(dve_order, s)
            link(nc.vector.tensor_tensor(rank[:, :], cnt[:, 0, :], cnt[:, 1, :], ALU.add))
            link(nc.vector.scalar_tensor_tensor(out=gate_w[:, :], in0=rank[:, :], scalar=float(KEEP), in1=wcol[:, :],
                                                op0=ALU.is_lt, op1=ALU.mult))
            dve.wait_ge(x_plus, 1)
            with dve.Fori(0, G) as g:
                for j in range(TG):
                    dve.wait_ge(f2, g * TG + (j + 1))
                    xt = X[:, bass.ds(g * TG + j, 1), :].rearrange("p a d -> p (a d)")
                    nc.vector.scalar_tensor_tensor(out=xt, in0=bank[4 + j % 2][0:TP, 0:D],
                                                   scalar=gate_w[:, bass.ds(g * TG + j, 1)], in1=xt,
                                                   op0=ALU.mult, op1=ALU.add).then_inc(f2e, 1)
            dve.wait_ge(f2e, 2 + NT)

            with dve.Fori(0, G) as g:
                order.enter(g, LN_STEPS)
                layernorm(g, 2)
                dve.wait_ge(ln_t, g + (2 * G + 2))
                for k in range(KD):
                    nc.vector.bn_stats(bn_st[:, k, bass.ds(g, 1), :].rearrange("p a s -> p (a s)"),
                                       bank[k][:, 0:GN]).then_inc(ln_ev, 1)
            order.leave(G)

            def bn_affine(i_gamma, i_beta, times):
                for k in range(KD):
                    s = order.step(nc.vector.bn_aggr(bn_mv[:, k, :], bn_st[:, k, :, :].rearrange("p g s -> p (g s)")))
                dve.wait_ge(dve_order, s)
                nc.vector.tensor_scalar(bn_ve[:, :], bn_mv[:, :, 1], EPS, None, ALU.add).then_inc(bn_ve_ok, 1)
                dve.wait_ge(bn_rs_ok, times)
                link(nc.vector.tensor_tensor(bn_sc[:, :], bn_rs[:, :], gin_col[:, i_gamma, :], ALU.mult))
                link(nc.vector.tensor_tensor(bn_ms[:, :], bn_mv[:, :, 0], bn_sc[:, :], ALU.mult))
                link(nc.vector.tensor_tensor(bn_bi[:, :], gin_col[:, i_beta, :], bn_ms[:, :], ALU.subtract))

            dve.wait_ge(ln_ev, 2 * 2 * G + 2 * G)
            bn_affine(0, 1, 1)
            dve.wait_ge(ld_gin, 64)
            for q in range(4):
                v = (bn_sc, bn_bi)[q // 2][:, q % 2:q % 2 + 1]
                nc.vector.tensor_scalar(bn_rep[:, q, :], ones[:, :], v, None, ALU.mult).then_inc(bn_ok, 1)
            dve.wait_ge(bn_mm, 1)
            link(nc.vector.tensor_copy(bn_row, bank[2][0:TP, :]))
            dve.wait_ge(ln_kept, 1 + 2 * G)
            for h, (lo, hi) in enumerate(((0, NT // 2), (NT // 2, NT))):
                link(nc.vector.tensor_tensor(Y[:, lo:hi, :], Y[:, lo:hi, :],
                                             bn_row[:, 0:D].unsqueeze(1).to_broadcast([TP, NT // 2, D]), ALU.mult))
                nc.vector.tensor_tensor(Y[:, lo:hi, :], Y[:, lo:hi, :],
                                        bn_row[:, D:2 * D].unsqueeze(1).to_broadcast([TP, NT // 2, D]), ALU.add).then_inc(y_ok, 1)
            dve.wait_ge(y_ok, 2)

            for layer in range(2):
                def into_u(t, layer=layer):
                    dve.wait_ge(u_t, t + (layer * NT + 1))
                    yt = Y[:, bass.ds(t, 1), :].rearrange("p a d -> p (a d)")
                    nc.vector.tensor_tensor(u_tile[:, :], yt, bank[0][0:TP, 0:D], ALU.add).then_inc(tile_read, 1)
                edge_pass(1 + layer, into_u)
                with dve.Fori(0, G) as g:
                    dve.wait_ge(c1e, g * KD + (layer * KD * G + KD + KD))
                    for k in range(KD):
                        nc.vector.bn_stats(bn_st[:, k, bass.ds(g, 1), :].rearrange("p a s -> p (a s)"),
                                           ZT[:, k, bass.ds(g * GN, GN)]).then_inc(c1s, 1)
                dve.wait_ge(c1s, KD * G * (layer + 1))
                bn_affine(3 + 3 * layer, 4 + 3 * layer, 2 + layer)
                dve.sem_inc(bn_ok, 1)
                if layer == 1:
                    with dve.Fori(0, G) as g:
                        for j in range(TG):
                            dve.wait_ge(c2, g * TG + (NT + TG + j + 1))
                            xt = X[:, bass.ds(g * TG + j, 1), :].rearrange("p a d -> p (a d)")
                            nc.vector.scalar_tensor_tensor(out=xt, in0=bank[2 + j % 2][0:TP, 0:D], scalar=0.0, in1=xt,
                                                           op0=ALU.max, op1=ALU.add).then_inc(c2e, 1)
                else:
                    dve.wait_ge(c2e, 2 + NT)
            dve.wait_ge(c2e, 2 + 2 * NT)

            def v3(i):
                return small[:, i, :].rearrange("p (t e) -> p t e", t=TG)

            def over_e(col):
                return col.unsqueeze(2).to_broadcast([TP, TG, NE])

            with dve.Fori(0, G) as g:
                order.enter(g, LN_STEPS + GATE_STEPS + TG * 4)
                layernorm(g, 3)
                dve.wait_ge(mg, g + 1)
                logits = bank[7][0:TP, 0:TG * NE].rearrange("p (t e) -> p t e", t=TG)
                link(nc.vector.tensor_reduce(gred[:, 0, :], logits, AX, ALU.max))
                nc.vector.tensor_tensor(v3(0), logits, over_e(gred[:, 0, :]), ALU.subtract).then_inc(mg_ev, 1)
                dve.wait_ge(mexp, g * 2 + 1)
                link(nc.vector.tensor_reduce(gred[:, 1, :], v3(1), AX, ALU.add))
                link(nc.vector.reciprocal(gred[:, 2, :], gred[:, 1, :]))
                link(nc.vector.tensor_tensor(v3(2), v3(1), over_e(gred[:, 2, :]), ALU.mult))
                pe_ = v3(2).unsqueeze(3).to_broadcast([TP, TG, NE, NE])
                pj_ = v3(2).unsqueeze(2).to_broadcast([TP, TG, NE, NE])
                q4 = [pair[:, i, :].rearrange("p (t e j) -> p t e j", t=TG, e=NE) for i in range(2)]
                order.step(nc.vector.tensor_tensor(q4[0], pj_, pe_, ALU.is_gt))
                link(nc.vector.tensor_tensor(q4[1], pj_, pe_, ALU.is_equal))
                link(nc.vector.tensor_tensor(pair[:, 1, :], pair[:, 1, :], earlier[:, :], ALU.mult))
                link(nc.vector.tensor_tensor(pair[:, 0, :], pair[:, 0, :], pair[:, 1, :], ALU.add))
                link(nc.vector.tensor_reduce(v3(3), q4[0], AX, ALU.add))
                order.step(nc.vector.tensor_scalar(v3(4), v3(3), 2.0, None, ALU.is_lt))
                link(nc.vector.tensor_reduce(gred[:, 3, :], v3(2), AX, ALU.max))
                nc.vector.tensor_tensor(v3(5), v3(2), over_e(gred[:, 3, :]), ALU.subtract).then_inc(mg_ev, 1)
                dve.wait_ge(mexp, g * 2 + 2)
                link(nc.vector.tensor_tensor(v3(6), v3(6), v3(4), ALU.mult))
                link(nc.vector.tensor_reduce(gred[:, 1, :], v3(6), AX, ALU.add))
                link(nc.vector.reciprocal(gred[:, 2, :], gred[:, 1, :]))
                link(nc.vector.tensor_tensor(v3(7), v3(6), over_e(gred[:, 2, :]), ALU.mult))
                for j in range(TG):
                    xt = X[:, bass.ds(g * TG + j, 1), :].rearrange("p a d -> p (a d)")
                    dve.wait_ge(m3, g * TG + (j + 1))
                    link(nc.vector.tensor_tensor(xt, xt, bank[2][0:TP, 0:D], ALU.add))
                    for e in range(NE):
                        o = bank[(3, 4)[e // 2]][0:TP, (e % 2) * D:(e % 2 + 1) * D]
                        ins = nc.vector.scalar_tensor_tensor(out=xt, in0=o, scalar=small[:, 7, NE * j + e:NE * j + e + 1],
                                                             in1=xt, op0=ALU.mult, op1=ALU.add)
                        if e < NE - 1:
                            link(ins)
                        else:
                            ins.then_inc(o_ok, 1)
            order.leave(G)

        @block.scalar
        def _(act):
            def ln_copy(g, ln, dst):
                act.wait_ge(ln_t, g + (ln * G + 2))
                for k in range(KD):
                    nc.scalar.activation(dst(k), bank[k][:, 0:GN], ACT.Copy).then_inc(ln_ev, 1)

            with act.Fori(0, G) as g:
                ln_copy(g, 0, lambda k: pT[:, k, :])
                for j in range(TG):
                    act.wait_ge(hst_free, g * TG + (j + 1))
                    for b in (0, 1):
                        act.wait_ge(h_mm, g * (5 * TG) + (5 * j + b + 1))
                        nc.scalar.activation(hst[:, j % 2, b * 512:(b + 1) * 512], bank[2 + b][0:TP, :], ACT.Copy).then_inc(h_act, 1)

            act.wait_ge(ld_small, 16 * 20)
            with act.Fori(0, G) as g:
                ln_copy(g, 1, lambda k: XT[:, k, bass.ds(g * GN, GN)])
                act.wait_ge(wb_mm, g + 1)
                nc.scalar.activation(WB[:, bass.ds(g * GN, GN)], bank[2][:, 0:GN], ACT.Identity, bias=br_col[:, :]).then_inc(wb_ok, 1)
            with act.Fori(0, G) as g:
                for m in range(HM):
                    act.wait_ge(f1, g * HM + (m + 1))
                    nc.scalar.activation(hT[:, m, :], bank[m % 4][:, 0:GN], ACT.Gelu_apprx_tanh,
                                         bias=b1_col[:, m:m + 1]).then_inc(f1e, 1)

            for layer in range(2):
                with act.Fori(0, NT) as t:
                    act.wait_ge(u_t, t + (layer * NT + 2))
                    nc.scalar.activation(XT[:, :, bass.ds(t * TP, TP)],
                                         bank[1][:, 0:KD * TP].rearrange("p (k n) -> p k n", k=KD), ACT.Copy).then_inc(u_ev, 1)
                with act.Fori(0, G) as g:
                    for k in range(KD):
                        act.wait_ge(c1, g * KD + (layer * KD * G + k + 1))
                        nc.scalar.activation(ZT[:, k, bass.ds(g * GN, GN)], bank[k][:, 0:GN], ACT.Identity,
                                             bias=gin_col[:, 2 + 3 * layer, k:k + 1]).then_inc(c1e, 1)
                act.wait_ge(bn_ok, 5 + layer)
                with act.Fori(0, G) as g:
                    act.wait_ge(c2, g * TG + (layer * NT + TG))
                    for k in range(KD):
                        nc.scalar.activation(zs[:, k, :], ZT[:, k, bass.ds(g * GN, GN)], ACT.Relu,
                                             bias=bn_bi[:, k:k + 1], scale=bn_sc[:, k:k + 1]).then_inc(zs_ok, 1)
                    if layer == 0:
                        for j in range(TG):
                            act.wait_ge(c2, g * TG + (TG + j + 1))
                            nc.scalar.activation(Y[:, bass.ds(g * TG + j, 1), :].rearrange("p a d -> p (a d)"),
                                                 bank[2 + j % 2][0:TP, 0:D], ACT.Relu).then_inc(c2e, 1)
                if layer == 0:
                    act.wait_ge(c2e, 2 + NT)
                    act.sem_inc(y_ok, 2)

            with act.Fori(0, G) as g:
                ln_copy(g, 3, lambda k: pT[:, k, :])
                act.wait_ge(mg_ev, g * 2 + 1)
                nc.scalar.activation(small[:, 1, :], small[:, 0, :], ACT.Exp).then_inc(mexp, 1)
                for m in range(6):
                    act.wait_ge(m1, g * 6 + (m + 1))
                    dst, bias = (s1[:, m, :], sb1_col[:, m:m + 1]) if m < 2 else (e1[:, m - 2, :], eb1_col[:, m - 2:m - 1])
                    nc.scalar.activation(dst, bank[(5, 6)[m % 2]][:, 0:GN], ACT.Relu, bias=bias).then_inc(m1e, 1)
                act.wait_ge(mg_ev, g * 2 + 2)
                nc.scalar.activation(small[:, 6, :], small[:, 5, :], ACT.Exp).then_inc(mexp, 1)
                for m in range(5):
                    act.wait_ge(m2, g * 5 + (m + 1))
                    src = bank[(5, 6)[m % 2]]
                    if m == 0:
                        nc.scalar.activation(s2, src[:, 0:GN], ACT.Relu, bias=sb2_col[:, :]).then_inc(m2e, 1)
                    else:
                        nc.scalar.activation(e2[0:EH2, m - 1, :], src[0:EH2, 0:GN], ACT.Relu,
                                             bias=eb2_col[:, m - 1:m]).then_inc(m2e, 1)

        @block.tensor
        def _(pe):
            mm = nc.tensor.matmul

            pe.sem_inc(used, U)
            pe.sem_inc(h_act, 2)
            pe.sem_inc(h_dve, 3)
            pe.sem_inc(hst_free, 2)
            pe.sem_inc(tile_read, 1)
            pe.sem_inc(f1e, 4)
            pe.sem_inc(f2e, 2)
            pe.sem_inc(c1e, KD)
            pe.sem_inc(c2e, 2)
            pe.sem_inc(u_t, 1)
            pe.sem_inc(u_ev, 1)
            pe.sem_inc(c2, TG)
            pe.sem_inc(m1e, 2)
            pe.sem_inc(o_ok, 1)
            pe.sem_inc(ln_t, 1)
            pe.sem_inc(ln_kept, 1)
            pe.sem_inc(wb_ok, 1)

            pe.wait_ge(consts, 16)
            pe.wait_ge(edges_f, 1)
            for i in range(3):
                for j in range(CJ):
                    dst = bank[2 * i + j // 4][:, (j % 4) * TP:(j % 4 + 1) * TP]
                    last = nc.tensor.transpose(dst, edge_f[:, i, j * P:(j + 1) * P], ident[0:TP, 0:TP])
                last.then_inc(edges_t, 1)
            for i in range(2):
                if i:
                    pe.wait_ge(edges_ev, 2)
                pe.wait_ge(spread_ok, i + 1)
                for b, lo, hi in ((0, 0, 512), (1, 512, CH)):
                    last = mm(bank[(6, 0)[i] + b][0:NT, 0:hi - lo], ones[0:TP, 0:NT], spread[:, i, lo:hi], start=True, stop=True)
                last.then_inc(spread_bc, 1)
            pe.wait_ge(lohi_ok, 1)
            pe.wait_ge(edges_ev, 3)
            for i in range(2):
                last = mm(bank[2][0:1, i * NT:(i + 1) * NT], lohi[:, i:i + 1], ident[0:NT, 0:NT], start=True, stop=True)
            last.then_inc(lohi_t, 1)
            pe.wait_ge(rng_ok, 1)

            def ln_transposes(g, ln, ev_before):
                pe.wait_ge(ln_nrm, g * TG + (ln * NT + TG))
                if ev_before is not None:
                    pe.wait_ge(ln_ev, ev_before)
                for k in range(KD):
                    for j in range(TG):
                        last = nc.tensor.transpose(bank[k][:, j * TP:(j + 1) * TP], nrm[:, j, k * P:(k + 1) * P], ident[0:TP, 0:TP])
                last.then_inc(ln_t, 1)

            pe.wait_ge(w0_ok, 1)
            with pe.Fori(0, G) as g:
                ln_transposes(g, 0, None)
                pe.wait_ge(ln_ev, g * KD + KD)
                for j in range(TG):
                    for b in range(5):
                        if b < 2:
                            pe.wait_ge(h_act, g * (2 * TG) + (2 * j + b + 1))
                        else:
                            pe.wait_ge(h_dve, g * (3 * TG) + (3 * j + b - 1))
                        w = 512 if b < 4 else D
                        for k in range(KD):
                            last = mm(bank[2 + b][0:TP, 0:w], pT[:, k, j * TP:(j + 1) * TP], W0[:, k, b * 512:b * 512 + w],
                                      start=(k == 0), stop=(k == KD - 1 and b < 4))
                        if b == 4:
                            last = mm(bank[2 + b][0:TP, 0:w], ones[0:1, 0:TP], bias_row[:, :], start=False, stop=True)
                        last.then_inc(h_mm, 1)

            summed = pe.alloc_register("summed")
            pe.reg_mov(summed, 1)
            landed = pe.alloc_register("landed")
            pe.reg_mov(landed, 16)

            def edge_pass(k, after):
                with pe.Fori(0, NT) as t:
                    first = pe.value_load(rng[0:1, bass.ds(t, 1)], min_val=0, max_val=CH - 1)
                    end = pe.value_load(rng[0:1, bass.ds(t + NT, 1)], min_val=1, max_val=CH)
                    pe.wait_ge(tile_read, t + (k * NT + 1))
                    mm(bank[0][:, 0:D], zeros[:, 0:P], zeros[:, :], start=True, stop=False)
                    with pe.Fori(first, end, U) as c:
                        n = pe.snap(summed, min_val=1, max_val=3 * NT * PAD)
                        l = pe.snap(landed, min_val=16, max_val=16 * 3 * NT * PAD)
                        for u in range(U):
                            pe.wait_ge(hot, n + u)
                            pe.wait_ge(gathered[u], l)
                            mm(bank[0][:, 0:D], onehot[:, u, :], msg[:, u, :], start=False, stop=False,
                               skip_group_check=True).then_inc(used, 1)
                        pe.reg_add(summed, summed, U)
                        pe.reg_add(landed, landed, 16)
                    mm(bank[0][:, 0:D], zeros[:, 0:P], zeros[:, :], start=False, stop=True).then_inc(tile_sum, 1)
                    after(t)

            edge_pass(0, lambda t: None)

            pe.wait_ge(wr_ok, KD)
            with pe.Fori(0, G) as g:
                ln_transposes(g, 1, g * KD + KD * G)
                pe.wait_ge(ln_ev, g * KD + (KD * G + KD))
                pe.wait_ge(wb_ok, g + 1)
                for k in range(KD):
                    last = mm(bank[2][:, 0:GN], wr_rep[:, k, :], XT[:, k, bass.ds(g * GN, GN)], start=(k == 0), stop=(k == KD - 1))
                last.then_inc(wb_mm, 1)
            pe.wait_ge(wb_ok, 1 + G)
            pe.wait_ge(ld_ffn, 32)
            pe.wait_ge(ld_small, 16 * 20)
            with pe.Fori(0, G) as g:
                for m in range(HM):
                    pe.wait_ge(f1e, g * HM + (m + 1))
                    for k in range(KD):
                        last = mm(bank[m % 4][:, 0:GN], w1[:, k, m * P:(m + 1) * P], XT[:, k, bass.ds(g * GN, GN)],
                                  start=(k == 0), stop=(k == KD - 1))
                    last.then_inc(f1, 1)
                pe.wait_ge(f1e, g * HM + (HM + 4))
                for j in range(TG):
                    pe.wait_ge(f2e, g * TG + (j + 1))
                    o = bank[4 + j % 2][0:TP, 0:D]
                    for m in range(HM):
                        mm(o, hT[:, m, j * TP:(j + 1) * TP], w2[:, m, :], start=(m == 0), stop=False)
                    mm(o, ones[0:1, 0:TP], b2_row[:, :], start=False, stop=True).then_inc(f2, 1)

            with pe.Fori(0, G) as g:
                ln_transposes(g, 2, g * KD + 2 * KD * G)
            pe.wait_ge(bn_ok, 4)
            for q in range(4):
                last = mm(bank[2][0:TP, q * P:(q + 1) * P], bn_rep[:, q, 0:TP], ident[:, :], start=True, stop=True)
            last.then_inc(bn_mm, 1)
            pe.wait_ge(ld_gin, 64)
            for layer in range(2):
                def transpose_u(t, layer=layer):
                    pe.wait_ge(tile_read, t + ((1 + layer) * NT + 2))
                    pe.wait_ge(u_ev, t + (layer * NT + 1))
                    for k in range(KD):
                        last = nc.tensor.transpose(bank[1][:, k * TP:(k + 1) * TP], u_tile[:, k * P:(k + 1) * P], ident[0:TP, 0:TP])
                    last.then_inc(u_t, 1)
                edge_pass(1 + layer, transpose_u)
                pe.wait_ge(u_ev, 1 + NT * (layer + 1))
                with pe.Fori(0, G) as g:
                    for m in range(KD):
                        pe.wait_ge(c1e, g * KD + (layer * KD * G + m + 1))
                        for k in range(KD):
                            last = mm(bank[m][:, 0:GN], gw[:, 2 * layer, k, m * P:(m + 1) * P], XT[:, k, bass.ds(g * GN, GN)],
                                      start=(k == 0), stop=(k == KD - 1))
                        last.then_inc(c1, 1)
                with pe.Fori(0, G) as g:
                    pe.wait_ge(zs_ok, g * KD + (layer * KD * G + KD))
                    for j in range(TG):
                        pe.wait_ge(c2e, g * TG + (layer * NT + j + 1))
                        o = bank[2 + j % 2][0:TP, 0:D]
                        for k in range(KD):
                            mm(o, zs[:, k, j * TP:(j + 1) * TP], gw[:, 2 * layer + 1, k, :], start=(k == 0), stop=False)
                        mm(o, ones[0:1, 0:TP], (b1b_row, b2b_row)[layer][:, :], start=False, stop=True).then_inc(c2, 1)

            pe.wait_ge(ld_moe, 16 * 8)
            pe.wait_ge(e2_ones, 1)
            with pe.Fori(0, G) as g:
                ln_transposes(g, 3, g * KD + 3 * KD * G)
                pe.wait_ge(ln_ev, g * KD + (3 * KD * G + KD))
                for j in range(TG):
                    o = bank[7][0:TP, j * NE:(j + 1) * NE]
                    for k in range(KD):
                        mm(o, pT[:, k, j * TP:(j + 1) * TP], gW[:, k, :], start=(k == 0), stop=False)
                    last = mm(o, ones[0:1, 0:TP], gb_row[:, :], start=False, stop=True)
                last.then_inc(mg, 1)
                for m in range(6):
                    pe.wait_ge(m1e, g * 6 + (m + 1))
                    for k in range(KD):
                        w = sW1[:, k, m * P:(m + 1) * P] if m < 2 else eW1[:, m - 2, k, :]
                        last = mm(bank[(5, 6)[m % 2]][:, 0:GN], w, pT[:, k, :], start=(k == 0), stop=(k == KD - 1))
                    last.then_inc(m1, 1)
                pe.wait_ge(m1e, g * 6 + 8)
                for m in range(5):
                    if m >= 2:
                        pe.wait_ge(m2e, g * 5 + (m - 1))
                    if m == 0:
                        for k in range(KD):
                            last = mm(bank[5][:, 0:GN], sW2[:, k, :], s1[:, k, :], start=(k == 0), stop=(k == KD - 1))
                    else:
                        last = mm(bank[(5, 6)[m % 2]][0:EH2, 0:GN], eW2[:, m - 1, :], e1[:, m - 1, :], start=True, stop=True)
                    last.then_inc(m2, 1)
                pe.wait_ge(m2e, g * 5 + 5)
                for j in range(TG):
                    pe.wait_ge(o_ok, g * TG + (j + 1))
                    o = bank[2][0:TP, 0:D]
                    mm(o, s2[:, j * TP:(j + 1) * TP], sW3, start=True, stop=False)
                    mm(o, ones[0:1, 0:TP], sb3_row[:, :], start=False, stop=True)
                    for e in range(NE):
                        last = mm(bank[(3, 4)[e // 2]][0:TP, (e % 2) * D:(e % 2 + 1) * D], e2[:, e, j * TP:(j + 1) * TP],
                                  eW3[:, e, :], start=True, stop=True)
                    last.then_inc(m3, 1)


GATE_STEPS = 15


_INS = ["x", "src", "dst", "edge_type_8", "L0_gnn_basis", "L0_gnn_comp", "L0_gnn_loop_weight", "L0_gnn_bias_param",
        "L0_ffn_wr", "L0_ffn_br", "L0_ffn_w1", "L0_ffn_b1", "L0_ffn_w2", "L0_ffn_b2",
        "L1_gnn_g0", "L1_gnn_b0", "L1_gnn_W1a", "L1_gnn_b1a", "L1_gnn_g1", "L1_gnn_bt1", "L1_gnn_W1b", "L1_gnn_b1b",
        "L1_gnn_W2a", "L1_gnn_b2a", "L1_gnn_g2", "L1_gnn_bt2", "L1_gnn_W2b", "L1_gnn_b2b",
        "L1_ffn_sW1", "L1_ffn_sb1", "L1_ffn_sW2", "L1_ffn_sb2", "L1_ffn_sW3", "L1_ffn_sb3",
        "L1_ffn_eW1", "L1_ffn_eb1", "L1_ffn_eW2", "L1_ffn_eb2", "L1_ffn_eW3", "L1_ffn_eb3", "L1_ffn_gW", "L1_ffn_gb"]


def kernel(**inputs):
    import numpy as _np
    import concourse.bacc as _bacc
    from concourse import mybir as _mybir
    from concourse.bass_utils import run_bass_kernel_spmd as _run

    nc = _bacc.Bacc("TRN2", target_bir_lowering=False, num_devices=1)
    arrays, args = {}, {}
    for name in _INS:
        v = _np.ascontiguousarray(inputs[name])
        arrays[f"in_{name}"] = v
        args[name] = nc.dram_tensor(f"in_{name}", v.shape, _mybir.dt.from_np(v.dtype), kind="ExternalInput").ap()
    out = nc.dram_tensor("out_dram", (N, D), _mybir.dt.float32, kind="ExternalOutput").ap()
    h_table = nc.dram_tensor("h_table", (N * R, D), _mybir.dt.float32, kind="Internal").ap()
    x_table = nc.dram_tensor("x_table", (N, D), _mybir.dt.float32, kind="Internal").ap()
    gnn_ffn_kernel(nc, args, out, h_table, x_table)
    r = _run(nc, [arrays], core_ids=[0])
    return r.results[0]["out_dram"]
```

```python
from contextlib import ExitStack

import concourse.bass as bass
from concourse import mybir

F32 = mybir.dt.float32
BF16 = mybir.dt.bfloat16
I32 = mybir.dt.int32
U16 = mybir.dt.uint16
ALU = mybir.AluOpType
ACT = mybir.ActivationFunctionType
AX = mybir.AxisListType.X

P = 128
N = 2500
D = 256
KD = D // P
E = 80000
TP = 125
NT = N // TP
TG = 4
G = NT // TG
GN = TP * TG
CH = E // P
CJ = CH // TP
U = 4
PRE = U
PAD = PRE + CH + 3 * U
R = 8
NB = 4
H = 1024
HM = H // P
KEEP = 1249
EPS = 1e-5
NE = 4
EH1, EH2 = 128, 64
FAR = 4096.0
PARTS = 3
EXACT = 254.0
AB_ACT, AB_DVE = (0, 2, 4), (1, 3)
AB = 5
TB = 8
M3 = ((7, 5, 6), (2, 3, 4))
BLOCKS = [(0, 8), (8, 16), (16, 20)]


class Count:

    def __init__(self, sem):
        self.sem, self.base, self.k, self.reg, self.per = sem, 0, 0, None, 0

    def step(self, ins):
        ins.then_inc(self.sem, 1)
        self.k += 1
        return self.at(self.k)

    def at(self, k):
        return self.base + k if self.reg is None else self.reg * self.per + (self.base + k)

    def enter(self, reg, per):
        self.base, self.k, self.reg, self.per = self.base + self.k, 0, reg, per

    def leave(self, trips):
        assert self.k == self.per, (self.k, self.per)
        self.base, self.k, self.reg = self.base + trips * self.per, 0, None


def gnn_ffn_kernel(nc, a, out, h_table, x_table):
    with ExitStack() as ctx:
        def sb(name, shape, dt=F32):
            return ctx.enter_context(nc.sbuf_tensor(name, shape, dt))

        def sem(name):
            return ctx.enter_context(nc.semaphore(name))

        bank = [ctx.enter_context(nc.psum_tensor(f"bank{i}", [P, 512], F32)) for i in range(8)]

        bank16 = [b[:, :].bitcast(BF16) for b in bank]
        class Area:
            def __init__(self, name, words):
                self.t, self.words, self.n = sb(name, [P, words]), words, 0

            def take(self, words, parts=P, dt=None):
                v = self.t[0:parts, self.n:self.n + words]
                self.n += words
                assert self.n <= self.words, (self.n, self.words)
                return v if dt is None else v.bitcast(dt)

            def anew(self, at=0):
                self.n = at
                return self

        NH = N // 2
        X = sb("X", [TP, NT, D])
        adj = Area("adj", NT * NH)
        rows = Area("rows", NT * D)
        mid = Area("mid", PARTS * NT * D // 2)
        low = Area("low", 6500)

        ident = sb("ident", [P, P])
        ident16 = sb("ident16", [P, P], BF16)
        ones = sb("ones", [P, P])
        zeros = sb("zeros", [P, P], BF16)
        node_no = sb("node_no", [P, NT * P], U16)
        tri = sb("tri", [TP, TP])
        half = sb("half", [P, TG])
        m_exact = sb("m_exact", [P, 1])
        tile_lo = sb("tile_lo", [NT, 1])
        tile_hi = sb("tile_hi", [NT, 1])
        earlier = sb("earlier", [TP, TG * NE * NE])

        src_of = sb("src_of", [P, PAD], I32)
        dst_of = sb("dst_of", [P, PAD])
        rng = sb("rng", [1, 3 * NT], I32)
        slot = sb("slot", [P, U], I32)

        stats = sb("stats", [TP, TG, 6])
        mv = sb("mv", [TP, TG, 2])
        veps = sb("veps", [TP, TG])
        rstd = sb("rstd", [TP, TG])
        br_col = sb("br_col", [P, 1])
        wr_col = sb("wr_col", [P, KD])
        b1_col = sb("b1_col", [P, HM])
        gin_col = sb("gin_col", [P, 8, KD])
        sb1_col = sb("sb1_col", [P, KD])
        sb2_col = sb("sb2_col", [P, 1])
        eb1_col = sb("eb1_col", [P, NE])
        eb2_col = sb("eb2_col", [EH2, NE])
        comp_bc = sb("comp_bc", [P, R * NB])
        bn_st = sb("bn_st", [P, KD, G, 6])
        bn_mv = sb("bn_mv", [P, KD, 2])
        bn_ve, bn_rs, bn_sc, bn_ms, bn_bi = (sb(n, [P, KD]) for n in ("bn_ve", "bn_rs", "bn_sc", "bn_ms", "bn_bi"))
        cmax = sb("cmax", [TP, 2, CJ])
        lohi = sb("lohi", [NT, 2])
        over = sb("over", [TP, NT])
        over_max = sb("over_max", [TP, 1])
        flag = sb("flag", [1, 1], I32)
        wcol = sb("wcol", [TP, NT])
        cnt = sb("cnt", [TP, 3, NT])
        rank = sb("rank", [TP, NT])
        gate_w = sb("gate_w", [TP, NT])
        gred = sb("gred", [TP, 4, TG])

        adj.anew()
        W0 = adj.take(KD * (R + 1) * D).rearrange("p (k n) -> p k n", k=KD)
        basis = adj.take(NB * KD * D).rearrange("p (b k o) -> p b k o", b=NB, k=KD)
        hst = adj.take(2 * R * D, TP).rearrange("p (u n) -> p u n", u=2)
        pT0 = adj.take(KD * GN).rearrange("p (k n) -> p k n", k=KD)
        edge_i = adj.take(3 * CJ * P, TP, I32).rearrange("p (a n) -> p a n", a=3)
        edge_f = adj.take(3 * CJ * P, TP).rearrange("p (a n) -> p a n", a=3)
        spread = adj.take(2 * CH, TP).rearrange("p (a n) -> p a n", a=2)
        near = adj.take(CH, NT)
        chunk_no = adj.take(CH, NT)
        bias_row = adj.take(D, 1)
        lo_row = adj.take(2 * NT, 1)
        nrm = low.anew(4100).take(TG * D, TP).rearrange("p (t d) -> p t d", t=TG)
        hot_src = rows.anew().take(U * NH, P, BF16).rearrange("p (u n) -> p u n", u=U)
        mid.anew()
        abf = mid.take(NH, TP, BF16)
        over_junk = mid.take(NH, TP, BF16)
        msg = mid.take(U * D).rearrange("p (u d) -> p u d", u=U)
        onehot = mid.take(U * P).rearrange("p (u n) -> p u n", u=U)
        hot16 = mid.take(U * P // 2, P, BF16).rearrange("p (u n) -> p u n", u=U)
        hrow_of = mid.take(PAD, P, I32)
        agg = low.anew().take(NT * D, TP).rearrange("p (t d) -> p t d", t=NT)
        AT = adj.anew().take(NT * NH, TP, BF16).rearrange("p (t n) -> p t n", t=NT)
        at_flat = adj.anew().take(NT * NH, TP, BF16)
        XT = rows.anew().take(KD * N).rearrange("p (k n) -> p k n", k=KD)
        mid.anew()
        WB = mid.take(N)
        w1 = mid.take(KD * H).rearrange("p (k n) -> p k n", k=KD)
        w2 = mid.take(HM * D).rearrange("p (k n) -> p k n", k=HM)
        wr_rep = mid.take(KD * P).rearrange("p (k n) -> p k n", k=KD)
        b2_row = mid.take(D, 1)
        rank_tri = mid.take(TP, TP)
        low.anew()
        hT = low.take(HM * GN).rearrange("p (m n) -> p m n", m=HM)
        rank_tmp = [low.take(NH, TP, BF16) for _ in range(2)]
        diag = hT[0:TP, 0:5, :].rearrange("p a n -> p (a n)")
        Y = rows.anew().take(NT * D, TP).rearrange("p (t d) -> p t d", t=NT)
        Ys = mid.anew().take(PARTS * NT * D // 2, TP, BF16).rearrange("p (s t d) -> p s t d", s=PARTS, t=NT)
        ZT = mid.anew().take(KD * N).rearrange("p (k n) -> p k n", k=KD)
        low.anew()
        gw = low.take(4 * KD * D).rearrange("p (w k n) -> p w k n", w=4, k=KD)
        zs = low.take(KD * GN).rearrange("p (k n) -> p k n", k=KD)
        bn_rep = low.take(4 * P).rearrange("p (q n) -> p q n", q=4)
        bn_row = low.take(4 * P, TP)
        low.anew(4100 + TG * D)
        b1b_row, b2b_row = low.take(D, 1), low.take(D, 1)
        adj.anew()
        few_msg = adj.take(U * D).rearrange("p (u d) -> p u d", u=U)
        few_hot = adj.take(U * P).rearrange("p (u n) -> p u n", u=U)
        few_tile = adj.take(D, TP)
        few_T = adj.take(KD * N).rearrange("p (k n) -> p k n", k=KD)
        adj.anew()
        sW1 = adj.take(KD * D).rearrange("p (k n) -> p k n", k=KD)
        sW2 = adj.take(KD * P).rearrange("p (k n) -> p k n", k=KD)
        sW3 = adj.take(D)
        eW1 = adj.take(NE * KD * EH1).rearrange("p (e k n) -> p e k n", e=NE, k=KD)
        eW2 = adj.take(NE * EH2).rearrange("p (e n) -> p e n", e=NE)
        eW3 = adj.take(NE * D, EH2 + 1).rearrange("p (e n) -> p e n", e=NE)
        gW = adj.take(KD * NE).rearrange("p (k n) -> p k n", k=KD)
        s1 = adj.take(KD * GN).rearrange("p (k n) -> p k n", k=KD)
        e1 = adj.take(NE * GN).rearrange("p (k n) -> p k n", k=NE)
        s2 = adj.take(GN)
        e2 = adj.take(NE * GN, EH2 + 1).rearrange("p (k n) -> p k n", k=NE)
        pT3 = adj.take(KD * GN).rearrange("p (k n) -> p k n", k=KD)
        sb3_row, gb_row = adj.take(D, 1), adj.take(NE, 1)
        small = adj.take(8 * TG * NE, TP).rearrange("p (i n) -> p i n", i=8)
        pair = adj.take(2 * TG * NE * NE, TP).rearrange("p (i n) -> p i n", i=2)

        ld_edges, ld_x, ld_w0 = sem("ld_edges"), sem("ld_x"), sem("ld_w0")
        ld_small, ld_ffn, ld_gin, ld_moe = sem("ld_small"), sem("ld_ffn"), sem("ld_gin"), sem("ld_moe")
        consts = sem("consts")
        dve_order = sem("dve_order")
        dve_passed, sp_passed, pool_passed = sem("dve_passed"), sem("sp_passed"), sem("pool_passed")
        edges_f, edges_t, edges_ev = sem("edges_f"), sem("edges_t"), sem("edges_ev")
        spread_ok, spread_bc, lohi_ok, lohi_t, rng_ok = (sem(n) for n in (
            "spread_ok", "spread_bc", "lohi_ok", "lohi_t", "rng_ok"))
        ln_var, ln_rstd, ln_nrm, ln_t, ln_ev, ln_kept = (sem(n) for n in (
            "ln_var", "ln_rstd", "ln_nrm", "ln_t", "ln_ev", "ln_kept"))
        w0_ok, h_mm, h_act, h_dve, hst_free, h_stored, table_ok = (sem(n) for n in (
            "w0_ok", "h_mm", "h_act", "h_dve", "hst_free", "h_stored", "table_ok"))
        hst_dma = [sem(f"hst_dma{i}") for i in range(2)]
        used, hot, slot_ok = sem("used"), sem("hot"), sem("slot_ok")
        gathered = [sem(f"gathered{u}") for u in range(U)]
        tile_sum, tile_read, a_act, a_dve, over_ok, at_t, at_ev, at_ok = (sem(n) for n in (
            "tile_sum", "tile_read", "a_act", "a_dve", "over_ok", "at_t", "at_ev", "at_ok"))
        split_a, split_d, u_mm, u_act, u_dve = (sem(n) for n in ("split_a", "split_d", "u_mm", "u_act", "u_dve"))
        over_max_ok, over_mm, flag_ok = sem("over_max_ok"), sem("over_mm"), sem("flag_ok")
        few_table, few_dma, few_slot, few_used, few_made, few_sum, few_read, few_t, few_ev, few_xt = (sem(n) for n in (
            "few_table", "few_dma", "few_slot", "few_used", "few_made", "few_sum", "few_read", "few_t", "few_ev", "few_xt"))
        few_landed = [sem(f"few_landed{u}") for u in range(U)]
        wr_ok, wb_mm, wb_ok, diag_ok, x_plus = (sem(n) for n in ("wr_ok", "wb_mm", "wb_ok", "diag_ok", "x_plus"))
        f1, f1e, f2, f2e = sem("f1"), sem("f1e"), sem("f2"), sem("f2e")
        bn_ve_ok, bn_rs_ok, bn_ok, bn_mm, bn_row_ok, y_ok, x_st = (sem(n) for n in (
            "bn_ve_ok", "bn_rs_ok", "bn_ok", "bn_mm", "bn_row_ok", "y_ok", "x_st"))
        c1, c1e, c1s, zs_ok, c2, c2e = (sem(n) for n in ("c1", "c1e", "c1s", "zs_ok", "c2", "c2e"))
        m1, m1e, m2, m2e, mg, mg_ev, mexp, mc, m3, m3e, o_ok, o_st, e2_ones = (sem(n) for n in (
            "m1", "m1e", "m2", "m2e", "mg", "mg_ev", "mexp", "mc", "m3", "m3e", "o_ok", "o_st", "e2_ones"))

        ctx.enter_context(nc.allow_non_contiguous_dma(reason="bias columns and per-tile rows"))
        block = ctx.enter_context(nc.Block())

        LN = {"stage0": 0, "stage1": 1, "stage2": 2, "stage3": 3}

        @block.sync
        def _(sp):
            def node_dma(dst, src, lo, hi, s):
                sp.dma_start(dst(0, lo), src(0, lo)).then_inc(s, 16)
                sp.dma_start(dst(lo, hi), src(lo, hi)).then_inc(s, 16)

            for i, name in enumerate(("src", "edge_type_8", "dst")):
                v = a[name].rearrange("(p n) -> p n", p=TP)
                node_dma(lambda l, h: edge_i[l:h, i, :], lambda l, h: v[l:h, :], 112, TP, ld_edges)
            xv = a["x"].rearrange("(t p) d -> p t d", p=TP)
            node_dma(lambda l, h: X[l:h, :, :], lambda l, h: xv[l:h, :, :], 112, TP, ld_x)
            sp.dma_start(basis, a["L0_gnn_basis"].rearrange("b (k p) o -> p b k o", p=P)).then_inc(ld_w0, 16)
            sp.dma_start(W0[:, :, R * D:(R + 1) * D],
                         a["L0_gnn_loop_weight"].rearrange("(k p) o -> p k o", p=P)).then_inc(ld_w0, 16)
            sp.dma_start(comp_bc[:, :], a["L0_gnn_comp"].rearrange("r b -> (r b)").partition_broadcast(P)).then_inc(ld_w0, 16)
            sp.dma_start(bias_row, a["L0_gnn_bias_param"].unsqueeze(0)).then_inc(ld_w0, 16)

            hv = h_table.rearrange("(t p r) o -> t p (r o)", p=TP, r=R)
            with sp.Fori(0, NT // 2) as g:
                for u in range(2):
                    sp.wait_ge(h_act, g * 4 + (2 * u + 4))
                    sp.sem_inc(sp_passed, 1)
                    sp.wait_ge(h_dve, g * 6 + (3 * u + 6))
                    sp.sem_inc(sp_passed, 1)
                    for lo, hi in ((0, 112), (112, TP)):
                        sp.dma_start(hv[bass.ds(g * 2 + u, 1), lo:hi, :].rearrange("a p n -> (a p) n"),
                                     hst[lo:hi, u, :]).then_inc(hst_dma[u], 16)
                    sp.wait_ge(hst_dma[u], g * 32 + 32)
                    sp.sem_inc(hst_free, 1)
            sp.sem_inc(table_ok, 1)

            sp.wait_ge(at_ok, 1)
            sp.dma_start(w1, a["L0_ffn_w1"].rearrange("(k p) n -> p k n", p=P)).then_inc(ld_ffn, 16)
            sp.dma_start(w2, a["L0_ffn_w2"].rearrange("(k p) n -> p k n", p=P)).then_inc(ld_ffn, 16)
            sp.dma_start(b2_row, a["L0_ffn_b2"].unsqueeze(0)).then_inc(ld_ffn, 16)
            sp.wait_ge(f2e, 4 + NT)
            for i, name in enumerate(("L1_gnn_W1a", "L1_gnn_W1b", "L1_gnn_W2a", "L1_gnn_W2b")):
                sp.dma_start(gw[:, i, :, :], a[name].rearrange("(k p) n -> p k n", p=P)).then_inc(ld_gin, 16)
            for dst, name in ((b1b_row, "L1_gnn_b1b"), (b2b_row, "L1_gnn_b2b")):
                sp.dma_start(dst, a[name].unsqueeze(0)).then_inc(ld_gin, 16)
            sp.wait_ge(flag_ok, 1)
            inexact = sp.value_load(flag[0:1, 0:1], min_val=0, max_val=1)
            with sp.If(inexact > 0):
                tv = x_table.rearrange("(t p) o -> p t o", p=TP)
                for layer in range(2):
                    sp.wait_ge(y_ok, 2 * (layer + 1))
                    node_dma(lambda l, h: tv[l:h, :, :], lambda l, h: Y[l:h, :, :], 112, TP, few_dma)
                    sp.wait_ge(few_dma, 32 * (layer + 1))
                    sp.sem_inc(few_table, 1)
            sp.wait_ge(c2e, 2 + 2 * NT)
            moe = [(sW1, a["L1_ffn_sW1"].rearrange("(k p) n -> p k n", p=P)),
                   (sW2, a["L1_ffn_sW2"].rearrange("(k p) n -> p k n", p=P)),
                   (sW3, a["L1_ffn_sW3"]),
                   (eW1, a["L1_ffn_eW1"].rearrange("e (k p) n -> p e k n", p=P)),
                   (eW2, a["L1_ffn_eW2"].rearrange("e p n -> p e n")),
                   (eW3[0:EH2, :, :], a["L1_ffn_eW3"].rearrange("e p n -> p e n")),
                   (eW3[EH2:EH2 + 1, :, :], a["L1_ffn_eb3"].unsqueeze(0)),
                   (gW, a["L1_ffn_gW"].rearrange("(k p) n -> p k n", p=P)),
                   (sb3_row, a["L1_ffn_sb3"].unsqueeze(0)), (gb_row, a["L1_ffn_gb"].unsqueeze(0))]
            for dst, src in moe:
                sp.dma_start(dst, src).then_inc(ld_moe, 16)
            ov = out.rearrange("(t p) d -> p t d", p=TP)
            with sp.Fori(0, G) as g:
                sp.wait_ge(o_ok, g * TG + (TG + 2))
                sp.sem_inc(sp_passed, 1)
                for lo, hi in ((0, 112), (112, TP)):
                    sp.dma_start(ov[lo:hi, bass.ds(g * TG, TG), :], X[lo:hi, bass.ds(g * TG, TG), :]).then_inc(o_st, 16)
            sp.wait_ge(o_st, 32 * G)

        @block.gpsimd
        def _(pool):
            pool.memset(ident[:, :], 0.0).then_inc(consts, 1)
            pool.memset(ones[:, :], 1.0).then_inc(consts, 1)
            pool.memset(zeros[:, :], 0.0).then_inc(consts, 1)
            pool.memset(m_exact[:, :], -EXACT).then_inc(consts, 1)
            pool.memset(half[:, :], -0.5).then_inc(consts, 1)
            pool.memset(tri[:, :], 1.0).then_inc(consts, 1)
            pool.memset(earlier[:, :], 1.0).then_inc(consts, 1)
            pool.memset(dst_of[:, :], -1.0).then_inc(consts, 1)
            pool.memset(src_of[:, :], 0).then_inc(consts, 1)
            pool.memset(hrow_of[:, :], 0).then_inc(consts, 1)
            pool.iota(node_no[:, :], pattern=[[1, NT * P]], base=0, channel_multiplier=0,
                      allow_small_or_imprecise_dtypes=True).then_inc(consts, 1)
            pool.iota(chunk_no, pattern=[[1, CH]], base=0, channel_multiplier=0,
                      allow_small_or_imprecise_dtypes=True).then_inc(consts, 1)
            pool.iota(tile_lo[:, :], pattern=[[1, 1]], base=0, channel_multiplier=TP,
                      allow_small_or_imprecise_dtypes=True).then_inc(consts, 1)
            pool.iota(tile_hi[:, :], pattern=[[1, 1]], base=TP, channel_multiplier=TP,
                      allow_small_or_imprecise_dtypes=True).then_inc(consts, 1)
            pool.wait_ge(consts, 14)
            pool.affine_select(out=ident[:, :], in_=ident[:, :], compare_op=ALU.not_equal, fill=1.0,
                               base=0, pattern=[[-1, P]], channel_multiplier=1).then_inc(consts, 1)
            pool.affine_select(out=tri[:, :], in_=tri[:, :], compare_op=ALU.is_gt, fill=0.0,
                               base=0, pattern=[[-1, TP]], channel_multiplier=1).then_inc(consts, 1)
            pool.affine_select(out=earlier[:, :].rearrange("p (t e j) -> p t e j", t=TG, e=NE),
                               in_=earlier[:, :].rearrange("p (t e j) -> p t e j", t=TG, e=NE),
                               compare_op=ALU.is_gt, fill=0.0, base=0,
                               pattern=[[0, TG], [1, NE], [-1, NE]], channel_multiplier=0).then_inc(consts, 1)
            def col(dst, name, **kw):
                pool.dma_start(dst, a[name].rearrange("(m p) -> p m", **kw)).then_inc(ld_small, 16)
            col(b1_col[:, :], "L0_ffn_b1", p=P)
            for i, name in enumerate(("L1_gnn_g0", "L1_gnn_b0", "L1_gnn_b1a", "L1_gnn_g1", "L1_gnn_bt1",
                                      "L1_gnn_b2a", "L1_gnn_g2", "L1_gnn_bt2")):
                col(gin_col[:, i, :], name, p=P)
            col(sb1_col[:, :], "L1_ffn_sb1", p=P)
            col(sb2_col[:, :], "L1_ffn_sb2", p=P)
            pool.dma_start(eb1_col[:, :], a["L1_ffn_eb1"].rearrange("e p -> p e")).then_inc(ld_small, 16)
            pool.dma_start(eb2_col[:, :], a["L1_ffn_eb2"].rearrange("e p -> p e")).then_inc(ld_small, 16)
            pool.dma_start(wr_col[:, :], a["L0_ffn_wr"].rearrange("(k p) o -> p (k o)", p=P)).then_inc(ld_small, 16)
            pool.dma_start(br_col[:, :], a["L0_ffn_br"].partition_broadcast(P)).then_inc(ld_small, 16)
            def ln_root(g, ln):
                pool.wait_ge(ln_var, g + (ln * G + 1))
                pool.tensor_tensor(rstd[:, :], veps[:, :], half[0:TP, 0:TG], ALU.pow).then_inc(ln_rstd, 1)

            with pool.Fori(0, G) as g:
                ln_root(g, 0)

            sent = pool.alloc_register("sent")
            pool.reg_mov(sent, 0)
            pool.wait_ge(rng_ok, 1)
            with pool.Fori(0, NT) as t:
                first = pool.value_load(rng[0:1, bass.ds(t, 1)], min_val=1, max_val=PRE + CH - 1)
                end = pool.value_load(rng[0:1, bass.ds(t + NT, 1)], min_val=PRE + 1, max_val=PRE + CH + 2 * U)
                with pool.Fori(first, end, U) as c:
                    n = pool.snap(sent, min_val=0, max_val=NT * PAD)
                    for u in range(U):
                        pool.wait_ge(slot_ok, n + (u + 1))
                        pool.sem_inc(pool_passed, 1)
                        pool.wait_ge(table_ok, 1)
                        pool.indirect_dma_start(msg[:, u, :], None, h_table,
                                                bass.IndirectOffsetOnAxis(slot[:, u:u + 1], 0)).then_inc(gathered[u], 16)
                    pool.reg_add(sent, sent, U)

            with pool.Fori(0, G) as g:
                ln_root(g, 1)
                pool.wait_ge(ln_nrm, g * TG + (1 * NT + TG))
                xg = X[:, bass.ds(g * TG, TG), :]
                pool.tensor_tensor(xg, xg, nrm, ALU.add).then_inc(ln_kept, 1)

            with pool.Fori(0, G) as g:
                ln_root(g, 2)
                pool.wait_ge(ln_nrm, g * TG + (2 * NT + TG))
                pool.tensor_copy(Y[:, bass.ds(g * TG, TG), :], nrm).then_inc(ln_kept, 1)
            pool.wait_ge(flag_ok, 1)
            inexact = pool.value_load(flag[0:1, 0:1], min_val=0, max_val=1)
            pool.reg_mov(sent, 0)
            for times in range(3):
                pool.wait_ge(bn_ve_ok, 1 + times)
                pool.tensor_tensor(bn_rs[:, :], bn_ve[:, :], half[:, 0:KD], ALU.pow).then_inc(bn_rs_ok, 1)
                if times == 2:
                    break
                with pool.If(inexact > 0):
                    pool.wait_ge(few_table, 1 + times)
                    with pool.Fori(0, NT) as t:
                        first = pool.value_load(rng[0:1, bass.ds(t, 1)], min_val=1, max_val=PRE + CH - 1)
                        end = pool.value_load(rng[0:1, bass.ds(t + NT, 1)], min_val=PRE + 1, max_val=PRE + CH + 2 * U)
                        with pool.Fori(first, end, U) as c:
                            n = pool.snap(sent, min_val=0, max_val=4 * NT * PAD)
                            for u in range(U):
                                pool.wait_ge(few_slot, n + (u + 1))
                                pool.sem_inc(pool_passed, 1)
                                pool.wait_ge(few_table, 1 + times)
                                pool.indirect_dma_start(few_msg[:, u, :], None, x_table,
                                                        bass.IndirectOffsetOnAxis(slot[:, u:u + 1], 0)).then_inc(few_landed[u], 16)
                            pool.reg_add(sent, sent, U)

            pool.wait_ge(ld_moe, 16 * 10)
            pool.memset(e2[EH2:EH2 + 1, :, :], 1.0).then_inc(e2_ones, 1)
            pool.wait_ge(e2_ones, 1)
            with pool.Fori(0, G) as g:
                ln_root(g, 3)

        @block.vector
        def _(dve):
            order = Count(dve_order)

            def link(ins):
                dve.wait_ge(dve_order, order.step(ins))

            dve.wait_ge(ld_edges, 96)
            order.step(nc.vector.tensor_copy(edge_f[:, 0, :], edge_i[:, 0, :]))
            order.step(nc.vector.tensor_copy(edge_f[:, 1, :], edge_i[:, 1, :]))
            link(nc.vector.tensor_copy(edge_f[:, 2, :], edge_i[:, 2, :]))
            nc.vector.scalar_tensor_tensor(out=edge_f[:, 1, :], in0=edge_f[:, 0, :], scalar=float(R),
                                           in1=edge_f[:, 1, :], op0=ALU.mult, op1=ALU.add).then_inc(edges_f, 1)
            targets = edge_f[:, 2, :].rearrange("p (j e) -> p j e", j=CJ)
            order.step(nc.vector.tensor_reduce(cmax[:, 0, :], targets, AX, ALU.max))
            link(nc.vector.tensor_reduce(cmax[:, 1, :], targets, AX, ALU.min))
            dve.wait_ge(consts, 17)
            order.step(nc.vector.tensor_copy(ident16[:, :], ident[:, :]))
            for i in range(2):
                nc.vector.tensor_tensor(
                    spread[:, i, :].rearrange("p (q j) -> p q j", j=CJ),
                    ident[0:TP, 0:TP].unsqueeze(2).to_broadcast([TP, TP, CJ]),
                    cmax[:, i, :].unsqueeze(1).to_broadcast([TP, TP, CJ]), ALU.mult).then_inc(spread_ok, 1)
            for i, dst in enumerate((src_of, hrow_of, dst_of)):
                dve.wait_ge(edges_t, i + 1)
                v = dst[:, PRE:PRE + CH].rearrange("p (q j) -> p j q", j=CJ)
                nc.vector.tensor_copy(v[:, 0:4, :], bank[2 * i][:, 0:4 * TP].rearrange("p (j q) -> p j q", j=4)).then_inc(edges_ev, 1)
                nc.vector.tensor_copy(v[:, 4, :], bank[2 * i + 1][:, 0:TP]).then_inc(edges_ev, 1)
            for i, (limit, op, far, red) in enumerate(((tile_lo, ALU.is_lt, FAR, ALU.min), (tile_hi, ALU.is_ge, -FAR, ALU.max))):
                dve.wait_ge(spread_bc, i + 1)
                for b, lo, hi in ((0, 0, 512), (1, 512, CH)):
                    src = bank[(6, 0)[i] + b][0:NT, 0:hi - lo]
                    link(nc.vector.tensor_scalar(near[:, lo:hi], src, limit[:, :], far, op, ALU.mult))
                link(nc.vector.tensor_tensor(near[:, 0:CH], near[:, 0:CH], chunk_no, ALU.add))
                link(nc.vector.tensor_reduce(lohi[:, i:i + 1], near[:, 0:CH], AX, red))
            link(nc.vector.tensor_scalar(lohi[:, 0:1], lohi[:, 0:1], float(CH - 1), None, ALU.min))
            link(nc.vector.tensor_tensor(lohi[:, 1:2], lohi[:, 1:2], lohi[:, 0:1], ALU.max))
            link(nc.vector.tensor_scalar(lohi[:, 1:2], lohi[:, 1:2], 1.0, None, ALU.add))
            nc.vector.scalar_tensor_tensor(out=lohi[:, 1:2], in0=lohi[:, 0:1], scalar=float(2 * U + 1), in1=lohi[:, 1:2],
                                           op0=ALU.add, op1=ALU.max).then_inc(lohi_ok, 1)
            dve.wait_ge(lohi_t, 1)
            dve.wait_ge(edges_ev, 6)
            link(nc.vector.tensor_copy(lo_row, bank[2][0:1, 0:2 * NT]))
            firsts, ends, skips = (rng[:, i * NT:(i + 1) * NT] for i in range(3))
            link(nc.vector.tensor_tensor(skips, lo_row[:, 0:NT], lo_row[:, NT:2 * NT], ALU.subtract))
            link(nc.vector.tensor_scalar(skips, skips, U - 1, None, ALU.bitwise_and))
            order.step(nc.vector.tensor_scalar(ends, lo_row[:, NT:2 * NT], float(PRE), None, ALU.add))
            link(nc.vector.tensor_scalar(firsts, lo_row[:, 0:NT], float(PRE), None, ALU.add))
            nc.vector.tensor_tensor(firsts, firsts, skips, ALU.subtract).then_inc(rng_ok, 1)

            dve.wait_ge(ld_w0, 64)
            for b in range(NB):
                for r in range(R):
                    w = W0[:, :, r * D:(r + 1) * D]
                    c = comp_bc[:, r * NB + b:r * NB + b + 1]
                    if b == 0:
                        order.step(nc.vector.tensor_scalar(w, basis[:, b, :, :], c, None, ALU.mult))
                    else:
                        dve.wait_ge(dve_order, order.at(order.k - R + 1))
                        order.step(nc.vector.scalar_tensor_tensor(out=w, in0=basis[:, b, :, :], scalar=c, in1=w,
                                                                  op0=ALU.mult, op1=ALU.add))
            dve.wait_ge(dve_order, order.at(order.k))
            dve.sem_inc(w0_ok, 1)

            def layernorm(g, ln):
                for j in range(TG):
                    s = order.step(nc.vector.bn_stats(stats[:, j, :], X[:, bass.ds(g * TG + j, 1), :].rearrange("p a d -> p (a d)")))
                dve.wait_ge(dve_order, s)
                dve.sem_inc(dve_passed, 1)
                for j in range(TG):
                    s = order.step(nc.vector.bn_aggr(mv[:, j, :], stats[:, j, :]))
                dve.wait_ge(dve_order, s)
                nc.vector.tensor_scalar(veps[:, :], mv[:, :, 1], EPS, None, ALU.add).then_inc(ln_var, 1)
                dve.wait_ge(ln_rstd, g + (ln * G + 1))
                dve.wait_ge(ln_t, g + (ln * G + 1))
                if ln == 3:
                    dve.wait_ge(ln_kept, 1 + 2 * G)
                elif ln:
                    dve.wait_ge(ln_kept, g + ((ln - 1) * G + 1))
                for j in range(TG):
                    nc.vector.tensor_scalar(nrm[:, j, :], X[:, bass.ds(g * TG + j, 1), :].rearrange("p a d -> p (a d)"),
                                            mv[:, j, 0:1], rstd[:, j:j + 1], ALU.subtract, ALU.mult).then_inc(ln_nrm, 1)

            dve.wait_ge(ld_x, 32)
            LN_STEPS = 2 * TG
            with dve.Fori(0, G) as g:
                order.enter(g, LN_STEPS)
                layernorm(g, 0)
                for j in range(TG):
                    dve.wait_ge(hst_free, g * TG + (j + 1))
                    for b in (2, 3):
                        dve.wait_ge(h_mm, g * (5 * TG) + (5 * j + b + 1))
                        nc.vector.tensor_copy(hst[:, j % 2, b * 512:(b + 1) * 512], bank[2 + b][0:TP, :]).then_inc(h_dve, 1)
                    dve.wait_ge(h_mm, g * (5 * TG) + (5 * j + 5))
                    xt = X[:, bass.ds(g * TG + j, 1), :].rearrange("p a d -> p (a d)")
                    nc.vector.tensor_tensor(xt, xt, bank[6][0:TP, 0:D], ALU.add).then_inc(h_dve, 1)
            order.leave(G)

            made = dve.alloc_register("made")
            dve.reg_mov(made, 0)

            dve.wait_ge(rng_ok, 1)

            def hots(t, col, offset, rows_of=None):
                n = dve.snap(made, min_val=0, max_val=NT * PAD)
                for u in range(U):
                    c = col + (u + offset) % U
                    if u == U - 1 and rows_of is not None:
                        read_rows(rows_of)
                    dve.wait_ge(used, n + (u + 1))
                    nc.vector.tensor_copy(slot[:, u:u + 1], hrow_of[:, bass.ds(c, 1)]).then_inc(slot_ok, 1)
                    targets = node_no[:, bass.ds(t * TP, P)]
                    nc.vector.tensor_scalar(hot16[:, u, :], targets, dst_of[:, bass.ds(c, 1)], None, ALU.is_equal).then_inc(hot, 1)
                    nc.vector.tensor_scalar(hot_src[:, u, :], node_no[:, 0:N], src_of[:, bass.ds(c, 1)], None, ALU.is_equal).then_inc(hot, 1)
                    nc.vector.tensor_scalar(onehot[:, u, :], targets, dst_of[:, bass.ds(c, 1)], None, ALU.is_equal).then_inc(hot, 1)
                dve.reg_add(made, made, U)

            def read_rows(t):
                dve.wait_ge(tile_sum, t + 1)
                dve.wait_ge(at_t, t * len(BLOCKS) + 1)
                dve.wait_ge(over_ok, t + 1)
                for i in AB_DVE:
                    nc.vector.tensor_copy(abf[:, i * GN:(i + 1) * GN], bank[1 + i][0:TP, 0:GN]).then_inc(a_dve, 1)

            def hot_tile(t, before):
                first = dve.value_load(rng[0:1, bass.ds(t, 1)], min_val=1, max_val=PRE + CH - 1)
                end = dve.value_load(rng[0:1, bass.ds(t + NT, 1)], min_val=PRE + 1, max_val=PRE + CH + 2 * U)
                hots(t, first, U - 1, t - 1 if before else None)
                with dve.Fori(first + U, end, U) as c:
                    hots(t, c, 0)

            hot_tile(0, False)
            with dve.Fori(1, NT) as t:
                hot_tile(t, True)
            read_rows(NT - 1)
            dve.wait_ge(h_dve, 3 + 3 * NT)
            dve.wait_ge(tile_read, 1 + NT)
            link(nc.vector.tensor_tensor(X[:, :, :], X[:, :, :], agg, ALU.add))
            dve.wait_ge(at_ev, 2 + len(BLOCKS) * NT)
            step = N + TP
            own = at_flat[:, 0:(NT - 1) * step].rearrange("p (t q) -> p t q", q=step)[:, :, 0:TP]
            last = at_flat[:, (NT - 1) * step:NT * N]
            nc.vector.tensor_tensor(own, own, ident16[0:TP, 0:TP].unsqueeze(1).to_broadcast([TP, NT - 1, TP]), ALU.add).then_inc(at_ok, 1)
            nc.vector.tensor_tensor(last, last, ident16[0:TP, 0:TP], ALU.add).then_inc(at_ok, 1)

            dve.wait_ge(over_ok, 1 + NT)
            nc.vector.tensor_reduce(over_max[:, :], over[:, :], AX, ALU.max).then_inc(over_max_ok, 1)
            dve.wait_ge(over_mm, 1)
            nc.vector.tensor_scalar(flag[:, :], bank[7][0:1, 0:1], 0.0, None, ALU.is_gt).then_inc(flag_ok, 1)
            dve.wait_ge(flag_ok, 1)
            inexact = dve.value_load(flag[0:1, 0:1], min_val=0, max_val=1)
            dve.reg_mov(made, 0)

            dve.wait_ge(ld_small, 16 * 15)
            for k in range(KD):
                nc.vector.tensor_scalar(wr_rep[:, k, :], ones[:, :], wr_col[:, k:k + 1], None, ALU.mult).then_inc(wr_ok, 1)
            with dve.Fori(0, G) as g:
                order.enter(g, LN_STEPS)
                layernorm(g, 1)
            order.leave(G)
            dve.wait_ge(wb_ok, 1 + G)
            dve.wait_ge(ln_kept, 1 + G)
            wb_t = WB[0:TP, :].rearrange("p (t q) -> p t q", t=NT)
            diag_t = diag.rearrange("p (t q) -> p t q", t=NT)
            link(nc.vector.tensor_tensor(diag_t, wb_t, ident[0:TP, 0:TP].unsqueeze(1).to_broadcast([TP, NT, TP]), ALU.mult))
            link(nc.vector.tensor_reduce(wcol[:, :], diag_t, AX, ALU.add))
            dve.sem_inc(diag_ok, 1)
            order.step(nc.vector.memset(cnt[:, 0, 0:1], 0.0))
            for t in range(NT):
                at, w = t * TP, wcol[:, t:t + 1]
                if t:
                    dve.wait_ge(dve_order, order.at(order.k - 2))
                    order.step(nc.vector.tensor_scalar(rank_tmp[0][:, 0:at], WB[0:TP, 0:at], w, None, ALU.is_ge, ALU.add,
                                                       accum_out=cnt[:, 0, t:t + 1]))
                    dve.wait_ge(dve_order, order.at(order.k - 2))
                order.step(nc.vector.tensor_scalar(rank_tmp[1][:, at:N], WB[0:TP, at:N], w, None, ALU.is_gt, ALU.add,
                                                   accum_out=cnt[:, 1, t:t + 1]))
                if t:
                    dve.wait_ge(dve_order, order.at(order.k - 2))
                s = order.step(nc.vector.scalar_tensor_tensor(out=rank_tri, in0=WB[0:TP, at:at + TP], scalar=w,
                                                              in1=tri[:, :], op0=ALU.is_equal, op1=ALU.mult,
                                                              accum_out=cnt[:, 2, t:t + 1]))
            dve.wait_ge(dve_order, s)
            link(nc.vector.tensor_tensor(rank[:, :], cnt[:, 0, :], cnt[:, 1, :], ALU.add))
            link(nc.vector.tensor_tensor(rank[:, :], rank[:, :], cnt[:, 2, :], ALU.add))
            link(nc.vector.scalar_tensor_tensor(out=gate_w[:, :], in0=rank[:, :], scalar=float(KEEP), in1=wcol[:, :],
                                                op0=ALU.is_lt, op1=ALU.mult))
            with dve.Fori(0, G) as g:
                for j in range(TG):
                    dve.wait_ge(f2, g * TG + (2 * (j // 2) + 2))
                    xt = X[:, bass.ds(g * TG + j, 1), :].rearrange("p a d -> p (a d)")
                    nc.vector.scalar_tensor_tensor(out=xt, in0=bank[4 + j // 2][0:TP, j % 2 * D:(j % 2 + 1) * D],
                                                   scalar=gate_w[:, bass.ds(g * TG + j, 1)], in1=xt,
                                                   op0=ALU.mult, op1=ALU.add).then_inc(f2e, 1)
            dve.wait_ge(f2e, 4 + NT)

            with dve.Fori(0, G) as g:
                order.enter(g, LN_STEPS)
                layernorm(g, 2)
                dve.wait_ge(ln_t, g + (2 * G + 2))
                for k in range(KD):
                    nc.vector.bn_stats(bn_st[:, k, bass.ds(g, 1), :].rearrange("p a s -> p (a s)"),
                                       bank[k][:, 0:GN]).then_inc(ln_ev, 1)
            order.leave(G)

            def bn_affine(i_gamma, i_beta, times):
                for k in range(KD):
                    s = order.step(nc.vector.bn_aggr(bn_mv[:, k, :], bn_st[:, k, :, :].rearrange("p g s -> p (g s)")))
                dve.wait_ge(dve_order, s)
                nc.vector.tensor_scalar(bn_ve[:, :], bn_mv[:, :, 1], EPS, None, ALU.add).then_inc(bn_ve_ok, 1)
                dve.wait_ge(bn_rs_ok, times)
                link(nc.vector.tensor_tensor(bn_sc[:, :], bn_rs[:, :], gin_col[:, i_gamma, :], ALU.mult))
                link(nc.vector.tensor_tensor(bn_ms[:, :], bn_mv[:, :, 0], bn_sc[:, :], ALU.mult))
                link(nc.vector.tensor_tensor(bn_bi[:, :], gin_col[:, i_beta, :], bn_ms[:, :], ALU.subtract))

            dve.wait_ge(ln_ev, 2 * 2 * G + 2 * G)
            bn_affine(0, 1, 1)
            dve.wait_ge(ld_gin, 96)
            for q in range(4):
                v = (bn_sc, bn_bi)[q // 2][:, q % 2:q % 2 + 1]
                nc.vector.tensor_scalar(bn_rep[:, q, :], ones[:, :], v, None, ALU.mult).then_inc(bn_ok, 1)
            dve.wait_ge(bn_mm, 1)
            link(nc.vector.tensor_copy(bn_row, bank[2][0:TP, :]))
            dve.wait_ge(ln_kept, 1 + 2 * G)
            for h, (lo, hi) in enumerate(((0, NT // 2), (NT // 2, NT))):
                link(nc.vector.tensor_tensor(Y[:, lo:hi, :], Y[:, lo:hi, :],
                                             bn_row[:, 0:D].unsqueeze(1).to_broadcast([TP, NT // 2, D]), ALU.mult))
                nc.vector.tensor_tensor(Y[:, lo:hi, :], Y[:, lo:hi, :],
                                        bn_row[:, D:2 * D].unsqueeze(1).to_broadcast([TP, NT // 2, D]), ALU.add).then_inc(y_ok, 1)
            dve.wait_ge(y_ok, 2)

            for layer in range(2):
                with dve.If(inexact > 0):
                    dve.wait_ge(at_ok, 2)
                    with dve.Fori(0, NT) as t:
                        first = dve.value_load(rng[0:1, bass.ds(t, 1)], min_val=1, max_val=PRE + CH - 1)
                        end = dve.value_load(rng[0:1, bass.ds(t + NT, 1)], min_val=PRE + 1, max_val=PRE + CH + 2 * U)
                        with dve.Fori(first, end, U) as c:
                            n = dve.snap(made, min_val=0, max_val=4 * NT * PAD)
                            for u in range(U):
                                dve.wait_ge(few_used, n + (u + 1))
                                nc.vector.tensor_copy(slot[:, u:u + 1], src_of[:, bass.ds(c + u, 1)]).then_inc(few_slot, 1)
                                nc.vector.tensor_scalar(few_hot[:, u, :], node_no[:, bass.ds(t * TP, P)],
                                                        dst_of[:, bass.ds(c + u, 1)], None, ALU.is_equal).then_inc(few_made, 1)
                            dve.reg_add(made, made, U)
                        dve.wait_ge(few_sum, t + (layer * NT + 1))
                        dve.wait_ge(few_t, t + (layer * NT + 1))
                        yt = Y[:, bass.ds(t, 1), :].rearrange("p a d -> p (a d)")
                        nc.vector.tensor_tensor(few_tile, yt, bank[0][0:TP, 0:D], ALU.add).then_inc(few_read, 1)
                with dve.Else():
                    for h in range(2):
                        ts = slice(h * NT // 2, (h + 1) * NT // 2)
                        dve.wait_ge(split_a, layer * 4 + 2 * h + 1)
                        nc.vector.tensor_tensor(Y[:, ts, :], Y[:, ts, :], Ys[:, 0, ts, :], ALU.subtract).then_inc(split_d, 1)
                        dve.wait_ge(split_d, layer * 4 + 2 * h + 1)
                        dve.wait_ge(split_a, layer * 4 + 2 * h + 2)
                        nc.vector.tensor_tensor(Ys[:, 2, ts, :], Y[:, ts, :], Ys[:, 1, ts, :], ALU.subtract).then_inc(split_d, 1)
                    dve.wait_ge(split_d, layer * 4 + 4)
                    for f in range(KD):
                        dve.wait_ge(u_mm, (layer * KD + f + 1) * NT)
                        for i in (1, 3):
                            nc.vector.tensor_copy(XT[:, f, i * GN:(i + 1) * GN], bank[(5 * f + i) % 8][:, 0:GN]).then_inc(u_dve, 1)
                with dve.Fori(0, G) as g:
                    dve.wait_ge(c1e, g * KD + (layer * KD * G + KD + KD))
                    for k in range(KD):
                        nc.vector.bn_stats(bn_st[:, k, bass.ds(g, 1), :].rearrange("p a s -> p (a s)"),
                                           ZT[:, k, bass.ds(g * GN, GN)]).then_inc(c1s, 1)
                dve.wait_ge(c1s, KD * G * (layer + 1))
                bn_affine(3 + 3 * layer, 4 + 3 * layer, 2 + layer)
                dve.sem_inc(bn_ok, 1)
                if layer == 1:
                    with dve.Fori(0, G) as g:
                        for j in range(TG):
                            dve.wait_ge(c2, g * TG + (NT + TG + j + 1))
                            xt = X[:, bass.ds(g * TG + j, 1), :].rearrange("p a d -> p (a d)")
                            nc.vector.scalar_tensor_tensor(out=xt, in0=bank[4 + j % 2][0:TP, 0:D], scalar=0.0, in1=xt,
                                                           op0=ALU.max, op1=ALU.add).then_inc(c2e, 1)
                else:
                    dve.wait_ge(c2e, 2 + NT)
            dve.wait_ge(c2e, 2 + 2 * NT)

            def v3(i):
                return small[:, i, :].rearrange("p (t e) -> p t e", t=TG)

            def over_e(col):
                return col.unsqueeze(2).to_broadcast([TP, TG, NE])

            layernorm(0, 3)

            def second_ffn(g, more):
                if more:
                    layernorm(g + 1, 3)
                dve.wait_ge(mg, g + 1)
                logits = bank[7][0:TP, 0:TG * NE].rearrange("p (t e) -> p t e", t=TG)
                link(nc.vector.tensor_reduce(gred[:, 0, :], logits, AX, ALU.max))
                nc.vector.tensor_tensor(v3(0), logits, over_e(gred[:, 0, :]), ALU.subtract).then_inc(mg_ev, 1)
                dve.wait_ge(mexp, g * 2 + 1)
                link(nc.vector.tensor_reduce(gred[:, 1, :], v3(1), AX, ALU.add))
                link(nc.vector.reciprocal(gred[:, 2, :], gred[:, 1, :]))
                link(nc.vector.tensor_tensor(v3(2), v3(1), over_e(gred[:, 2, :]), ALU.mult))
                pe_ = v3(2).unsqueeze(3).to_broadcast([TP, TG, NE, NE])
                pj_ = v3(2).unsqueeze(2).to_broadcast([TP, TG, NE, NE])
                q4 = [pair[:, i, :].rearrange("p (t e j) -> p t e j", t=TG, e=NE) for i in range(2)]
                order.step(nc.vector.tensor_tensor(q4[0], pj_, pe_, ALU.is_gt))
                link(nc.vector.tensor_tensor(q4[1], pj_, pe_, ALU.is_equal))
                link(nc.vector.tensor_tensor(pair[:, 1, :], pair[:, 1, :], earlier[:, :], ALU.mult))
                link(nc.vector.tensor_tensor(pair[:, 0, :], pair[:, 0, :], pair[:, 1, :], ALU.add))
                link(nc.vector.tensor_reduce(v3(3), q4[0], AX, ALU.add))
                order.step(nc.vector.tensor_scalar(v3(4), v3(3), 2.0, None, ALU.is_lt))
                link(nc.vector.tensor_reduce(gred[:, 3, :], v3(2), AX, ALU.max))
                nc.vector.tensor_tensor(v3(5), v3(2), over_e(gred[:, 3, :]), ALU.subtract).then_inc(mg_ev, 1)
                dve.wait_ge(mexp, g * 2 + 2)
                link(nc.vector.tensor_tensor(v3(6), v3(6), v3(4), ALU.mult))
                link(nc.vector.tensor_reduce(gred[:, 1, :], v3(6), AX, ALU.add))
                link(nc.vector.reciprocal(gred[:, 2, :], gred[:, 1, :]))
                link(nc.vector.tensor_tensor(v3(7), v3(6), over_e(gred[:, 2, :]), ALU.mult))
                for j in range(TG):
                    xt = X[:, bass.ds(g * TG + j, 1), :].rearrange("p a d -> p (a d)")
                    dve.wait_ge(m3, g * TG + (j + 1))
                    shared, first, second = M3[j % 2]
                    link(nc.vector.tensor_tensor(xt, xt, bank[shared][0:TP, 0:D], ALU.add))
                    for e in range(NE):
                        o = bank[(first, second)[e // 2]][0:TP, (e % 2) * D:(e % 2 + 1) * D]
                        ins = nc.vector.scalar_tensor_tensor(out=xt, in0=o, scalar=small[:, 7, NE * j + e:NE * j + e + 1],
                                                             in1=xt, op0=ALU.mult, op1=ALU.add)
                        if e < NE - 1:
                            link(ins)
                        else:
                            ins.then_inc(o_ok, 1)

            with dve.Fori(0, G - 1) as g:
                order.enter(g, LN_STEPS + GATE_STEPS + TG * 4)
                second_ffn(g, True)
            order.leave(G - 1)
            second_ffn(G - 1, False)

        @block.scalar
        def _(act):
            def ln_copy(g, ln, dst):
                act.wait_ge(ln_t, g + (ln * G + 2))
                for k in range(KD):
                    nc.scalar.activation(dst(k), bank[k][:, 0:GN], ACT.Copy).then_inc(ln_ev, 1)

            with act.Fori(0, G) as g:
                ln_copy(g, 0, lambda k: pT0[:, k, :])
                for j in range(TG):
                    act.wait_ge(hst_free, g * TG + (j + 1))
                    for b in (0, 1):
                        act.wait_ge(h_mm, g * (5 * TG) + (5 * j + b + 1))
                        nc.scalar.activation(hst[:, j % 2, b * 512:(b + 1) * 512], bank[2 + b][0:TP, :], ACT.Copy).then_inc(h_act, 1)

            act.wait_ge(consts, 17)
            with act.Fori(0, NT) as t:
                act.wait_ge(tile_sum, t + 1)
                act.wait_ge(at_t, t * len(BLOCKS) + 1)
                act.wait_ge(over_ok, t + 1)
                for i in AB_ACT:
                    nc.scalar.activation(abf[:, i * GN:(i + 1) * GN], bank[1 + i][0:TP, 0:GN], ACT.Copy).then_inc(a_act, 1)
                    if i == 0:
                        nc.scalar.activation(agg[:, bass.ds(t, 1), :].rearrange("p a d -> p (a d)"), bank[0][0:TP, 0:D], ACT.Copy).then_inc(tile_read, 1)
                for b, (lo, hi) in enumerate(BLOCKS):
                    act.wait_ge(at_t, t * len(BLOCKS) + (b + 2))
                    nc.scalar.activation(AT[:, lo:hi, bass.ds(t * TP, TP)],
                                         bank16[6 + b % 2][0:TP, :].rearrange("p (s n) -> p s n", n=P)[:, 0:hi - lo, 0:TP],
                                         ACT.Copy).then_inc(at_ev, 1)
                act.wait_ge(a_act, t * 3 + 6)
                act.wait_ge(a_dve, t * 2 + 4)
                nc.scalar.activation(over_junk, abf, ACT.Relu, bias=m_exact[0:TP, :],
                                     accum_out=over[:, bass.ds(t, 1)]).then_inc(over_ok, 1)

            act.wait_ge(ld_small, 16 * 15)
            with act.Fori(0, G) as g:
                ln_copy(g, 1, lambda k: XT[:, k, bass.ds(g * GN, GN)])
                act.wait_ge(wb_mm, g + 1)
                nc.scalar.activation(WB[:, bass.ds(g * GN, GN)], bank[2][:, 0:GN], ACT.Identity, bias=br_col[:, :]).then_inc(wb_ok, 1)
            with act.Fori(0, G) as g:
                act.wait_ge(diag_ok, 1)
                for m in range(HM):
                    act.wait_ge(f1, g * HM + (m + 1))
                    nc.scalar.activation(hT[:, m, :], bank[m % 4][:, 0:GN], ACT.Gelu_apprx_tanh,
                                         bias=b1_col[:, m:m + 1]).then_inc(f1e, 1)

            act.wait_ge(flag_ok, 1)
            inexact = act.value_load(flag[0:1, 0:1], min_val=0, max_val=1)
            for layer in range(2):
                act.wait_ge(y_ok, 2 * (layer + 1))
                with act.If(inexact > 0):
                    act.wait_ge(at_ok, 2)
                    with act.Fori(0, NT) as t:
                        act.wait_ge(few_t, t + (layer * NT + 2))
                        nc.scalar.activation(few_T[:, :, bass.ds(t * TP, TP)],
                                             bank[1][:, 0:KD * TP].rearrange("p (k n) -> p k n", k=KD), ACT.Copy).then_inc(few_ev, 1)
                    act.wait_ge(few_ev, 1 + (layer + 1) * NT)
                    act.wait_ge(few_dma, 32 * (layer + 1))
                    nc.scalar.activation(XT[:, :, :], few_T, ACT.Copy).then_inc(few_xt, 1)
                with act.Else():
                    for h in range(2):
                        ts = slice(h * NT // 2, (h + 1) * NT // 2)
                        nc.scalar.activation(Ys[:, 0, ts, :], Y[:, ts, :], ACT.Copy).then_inc(split_a, 1)
                        act.wait_ge(split_d, layer * 4 + 2 * h + 1)
                        nc.scalar.activation(Ys[:, 1, ts, :], Y[:, ts, :], ACT.Copy).then_inc(split_a, 1)
                    act.wait_ge(split_d, layer * 4 + 4)
                    for f in range(KD):
                        act.wait_ge(u_mm, (layer * KD + f + 1) * NT)
                        for i in (0, 2, 4):
                            nc.scalar.activation(XT[:, f, i * GN:(i + 1) * GN], bank[(5 * f + i) % 8][:, 0:GN], ACT.Copy).then_inc(u_act, 1)
                with act.Fori(0, G) as g:
                    for k in range(KD):
                        act.wait_ge(c1, g * KD + (layer * KD * G + k + 1))
                        nc.scalar.activation(ZT[:, k, bass.ds(g * GN, GN)], bank[2 + k][:, 0:GN], ACT.Identity,
                                             bias=gin_col[:, 2 + 3 * layer, k:k + 1]).then_inc(c1e, 1)
                act.wait_ge(bn_ok, 5 + layer)
                with act.Fori(0, G) as g:
                    act.wait_ge(c2, g * TG + (layer * NT + TG))
                    for k in range(KD):
                        nc.scalar.activation(zs[:, k, :], ZT[:, k, bass.ds(g * GN, GN)], ACT.Relu,
                                             bias=bn_bi[:, k:k + 1], scale=bn_sc[:, k:k + 1]).then_inc(zs_ok, 1)
                    if layer == 0:
                        for j in range(TG):
                            act.wait_ge(c2, g * TG + (TG + j + 1))
                            nc.scalar.activation(Y[:, bass.ds(g * TG + j, 1), :].rearrange("p a d -> p (a d)"),
                                                 bank[4 + j % 2][0:TP, 0:D], ACT.Relu).then_inc(c2e, 1)
                if layer == 0:
                    act.wait_ge(c2e, 2 + NT)
                    act.sem_inc(y_ok, 2)

            ln_copy(0, 3, lambda k: pT3[:, k, :])

            def second_ffn(g, more):
                for m in range(6):
                    act.wait_ge(m1, g * 6 + (m + 1))
                    dst, bias = (s1[:, m, :], sb1_col[:, m:m + 1]) if m < 2 else (e1[:, m - 2, :], eb1_col[:, m - 2:m - 1])
                    nc.scalar.activation(dst, bank[(5, 6)[m % 2]][:, 0:GN], ACT.Relu, bias=bias).then_inc(m1e, 1)
                act.wait_ge(mg_ev, g * 2 + 1)
                nc.scalar.activation(small[:, 1, :], small[:, 0, :], ACT.Exp).then_inc(mexp, 1)
                if more:
                    ln_copy(g + 1, 3, lambda k: pT3[:, k, :])
                act.wait_ge(mg_ev, g * 2 + 2)
                nc.scalar.activation(small[:, 6, :], small[:, 5, :], ACT.Exp).then_inc(mexp, 1)
                for m in range(5):
                    act.wait_ge(m2, g * 5 + (m + 1))
                    src = bank[(5, 6)[m % 2]]
                    if m == 0:
                        nc.scalar.activation(s2, src[:, 0:GN], ACT.Relu, bias=sb2_col[:, :]).then_inc(m2e, 1)
                    else:
                        nc.scalar.activation(e2[0:EH2, m - 1, :], src[0:EH2, 0:GN], ACT.Relu,
                                             bias=eb2_col[:, m - 1:m]).then_inc(m2e, 1)

            with act.Fori(0, G - 1) as g:
                second_ffn(g, True)
            second_ffn(G - 1, False)

        @block.tensor
        def _(pe):
            mm = nc.tensor.matmul

            pe.sem_inc(used, U)
            pe.sem_inc(few_used, U)
            pe.sem_inc(few_read, 1)
            pe.sem_inc(few_t, 1)
            pe.sem_inc(few_ev, 1)
            pe.sem_inc(h_act, 2)
            pe.sem_inc(h_dve, 3)
            pe.sem_inc(hst_free, 2)
            pe.sem_inc(tile_read, 1)
            pe.sem_inc(f1e, 4)
            pe.sem_inc(f2e, 4)
            pe.sem_inc(c1e, KD)
            pe.sem_inc(c2e, 2)
            pe.sem_inc(a_act, 3)
            pe.sem_inc(a_dve, 2)
            pe.sem_inc(over_ok, 1)
            pe.sem_inc(at_t, 1)
            pe.sem_inc(at_ev, 2)
            pe.sem_inc(c2, TG)
            pe.sem_inc(m1e, 2)
            pe.sem_inc(o_ok, 2)
            pe.sem_inc(ln_t, 1)
            pe.sem_inc(ln_kept, 1)
            pe.sem_inc(wb_ok, 1)

            pe.wait_ge(consts, 17)
            pe.wait_ge(edges_f, 1)
            for i in range(3):
                for j in range(CJ):
                    dst = bank[2 * i + j // 4][:, (j % 4) * TP:(j % 4 + 1) * TP]
                    last = nc.tensor.transpose(dst, edge_f[:, i, j * P:(j + 1) * P], ident[0:TP, 0:TP])
                last.then_inc(edges_t, 1)
            for i in range(2):
                if i:
                    pe.wait_ge(edges_ev, 2)
                pe.wait_ge(spread_ok, i + 1)
                for b, lo, hi in ((0, 0, 512), (1, 512, CH)):
                    last = mm(bank[(6, 0)[i] + b][0:NT, 0:hi - lo], ones[0:TP, 0:NT], spread[:, i, lo:hi], start=True, stop=True)
                last.then_inc(spread_bc, 1)
            pe.wait_ge(lohi_ok, 1)
            pe.wait_ge(edges_ev, 3)
            for i in range(2):
                last = mm(bank[2][0:1, i * NT:(i + 1) * NT], lohi[:, i:i + 1], ident[0:NT, 0:NT], start=True, stop=True)
            last.then_inc(lohi_t, 1)
            pe.wait_ge(rng_ok, 1)

            def ln_transposes(g, ln, ev_before):
                pe.wait_ge(ln_nrm, g * TG + (ln * NT + TG))
                if ev_before is not None:
                    pe.wait_ge(ln_ev, ev_before)
                for k in range(KD):
                    for j in range(TG):
                        last = nc.tensor.transpose(bank[k][:, j * TP:(j + 1) * TP], nrm[:, j, k * P:(k + 1) * P], ident[0:TP, 0:TP])
                last.then_inc(ln_t, 1)

            pe.wait_ge(w0_ok, 1)
            with pe.Fori(0, G) as g:
                ln_transposes(g, 0, None)
                pe.wait_ge(ln_ev, g * KD + KD)
                for j in range(TG):
                    for b in range(5):
                        if b < 2:
                            pe.wait_ge(h_act, g * (2 * TG) + (2 * j + b + 1))
                        else:
                            pe.wait_ge(h_dve, g * (3 * TG) + (3 * j + b - 1))
                        w = 512 if b < 4 else D
                        for k in range(KD):
                            last = mm(bank[2 + b][0:TP, 0:w], pT0[:, k, j * TP:(j + 1) * TP], W0[:, k, b * 512:b * 512 + w],
                                      start=(k == 0), stop=(k == KD - 1 and b < 4))
                        if b == 4:
                            last = mm(bank[2 + b][0:TP, 0:w], ones[0:1, 0:TP], bias_row, start=False, stop=True)
                        last.then_inc(h_mm, 1)

            summed = pe.alloc_register("summed")
            pe.reg_mov(summed, 1)
            landed = pe.alloc_register("landed")
            pe.reg_mov(landed, 16)

            def chunk(t, u, n, l, new=False):
                pe.wait_ge(hot, (n - 1) * 3 + (3 * u + 2))
                for i in range(AB):
                    if new:
                        if i in AB_ACT:
                            pe.wait_ge(a_act, t * 3 + (AB_ACT.index(i) + 1))
                        else:
                            pe.wait_ge(a_dve, t * 2 + (AB_DVE.index(i) + 1))
                    mm(bank[1 + i][:, 0:GN], hot16[:, u, :], hot_src[:, u, i * GN:(i + 1) * GN],
                       start=new, stop=True, skip_group_check=True)
                if new:
                    pe.wait_ge(tile_read, t + 1)
                pe.wait_ge(hot, (n - 1) * 3 + (3 * u + 3))
                pe.wait_ge(gathered[u], l)
                mm(bank[0][:, 0:D], onehot[:, u, :], msg[:, u, :], start=new, stop=True,
                   skip_group_check=True).then_inc(used, 1)

            def counters():
                return (pe.snap(summed, min_val=1, max_val=4 * NT * PAD),
                        pe.snap(landed, min_val=16, max_val=4 * 16 * NT * PAD))

            def count_round():
                pe.reg_add(summed, summed, U)
                pe.reg_add(landed, landed, 16)

            def transpose_rows(t, banks):
                pe.wait_ge(a_act, t * 3 + 6)
                pe.wait_ge(a_dve, t * 2 + 4)
                for b in banks:
                    lo, hi = BLOCKS[b]
                    pe.wait_ge(at_ev, t * len(BLOCKS) + (b + 1))
                    for s in range(lo, hi):
                        last = nc.tensor.transpose(bank16[6 + b % 2][0:TP, (s - lo) * P:(s - lo) * P + TP],
                                                   abf[:, s * TP:(s + 1) * TP], ident16[0:TP, 0:TP])
                    last.then_inc(at_t, 1)

            def tile(t, before):
                first = pe.value_load(rng[0:1, bass.ds(t, 1)], min_val=1, max_val=PRE + CH - 1)
                end = pe.value_load(rng[0:1, bass.ds(t + NT, 1)], min_val=PRE + 1, max_val=PRE + CH + 2 * U)
                skip = pe.value_load(rng[0:1, bass.ds(t + 2 * NT, 1)], min_val=0, max_val=U - 1)
                n, l = counters()
                chunk(t, 0, n, l, new=True)
                for u in range(1, U):
                    with pe.If(skip < u):
                        chunk(t, u, n, l)
                    with pe.Else():
                        pe.wait_ge(hot, (n - 1) * 3 + (3 * u + 3))
                        pe.wait_ge(gathered[u], l)
                        mm(bank[0][:, 0:2], zeros[:, :], zeros[:, 0:2], start=False, stop=True, skip_group_check=True).then_inc(used, 1)
                count_round()
                if before:
                    transpose_rows(t - 1, (0, 1))

                def whole_round():
                    n, l = counters()
                    for u in range(U):
                        chunk(t, u, n, l)
                    count_round()

                whole_round()
                if before:
                    transpose_rows(t - 1, (2,))
                with pe.Fori(first + 2 * U, end, U):
                    whole_round()
                mm(bank[0][:, 0:2], zeros[:, :], zeros[:, 0:2], start=False, stop=True, skip_group_check=True).then_inc(tile_sum, 1)

            pe.wait_ge(h_act, 2 + 2 * NT)
            pe.wait_ge(h_dve, 3 + 3 * NT)
            tile(0, False)
            with pe.Fori(1, NT) as t:
                tile(t, True)
            transpose_rows(NT - 1, (0, 1, 2))
            pe.wait_ge(over_max_ok, 1)
            pe.wait_ge(at_ev, 2 + len(BLOCKS) * NT)
            mm(bank[7][0:1, 0:1], over_max[:, :], ones[0:TP, 0:1], start=True, stop=True).then_inc(over_mm, 1)
            pe.wait_ge(flag_ok, 1)
            inexact = pe.value_load(flag[0:1, 0:1], min_val=0, max_val=1)
            pe.reg_mov(summed, 1)
            pe.reg_mov(landed, 16)

            pe.wait_ge(wr_ok, KD)
            with pe.Fori(0, G) as g:
                ln_transposes(g, 1, g * KD + KD * G)
                pe.wait_ge(ln_ev, g * KD + (KD * G + KD))
                pe.wait_ge(wb_ok, g + 1)
                for k in range(KD):
                    last = mm(bank[2][:, 0:GN], wr_rep[:, k, :], XT[:, k, bass.ds(g * GN, GN)], start=(k == 0), stop=(k == KD - 1))
                last.then_inc(wb_mm, 1)
            pe.wait_ge(wb_ok, 1 + G)
            pe.wait_ge(ld_ffn, 48)
            pe.wait_ge(ld_small, 16 * 15)
            with pe.Fori(0, G) as g:
                for m in range(HM):
                    pe.wait_ge(f1e, g * HM + (m + 1))
                    for k in range(KD):
                        last = mm(bank[m % 4][:, 0:GN], w1[:, k, m * P:(m + 1) * P], XT[:, k, bass.ds(g * GN, GN)],
                                  start=(k == 0), stop=(k == KD - 1))
                    last.then_inc(f1, 1)
                pe.wait_ge(f1e, g * HM + (HM + 4))
                for j in range(TG):
                    pe.wait_ge(f2e, g * TG + (2 * (j // 2) + 2))
                    o = bank[4 + j // 2][0:TP, j % 2 * D:(j % 2 + 1) * D]
                    for m in range(HM):
                        mm(o, hT[:, m, j * TP:(j + 1) * TP], w2[:, m, :], start=(m == 0), stop=False)
                    mm(o, ones[0:1, 0:TP], b2_row, start=False, stop=True).then_inc(f2, 1)

            with pe.Fori(0, G) as g:
                ln_transposes(g, 2, g * KD + 2 * KD * G)
            pe.wait_ge(bn_ok, 4)
            for q in range(4):
                last = mm(bank[2][0:TP, q * P:(q + 1) * P], bn_rep[:, q, 0:TP], ident[:, :], start=True, stop=True)
            last.then_inc(bn_mm, 1)
            pe.wait_ge(ld_gin, 96)
            for layer in range(2):
                def few_round(new):
                    n = pe.snap(summed, min_val=1, max_val=4 * NT * PAD)
                    l = pe.snap(landed, min_val=16, max_val=4 * 16 * NT * PAD)
                    for u in range(U):
                        pe.wait_ge(few_made, n + u)
                        pe.wait_ge(few_landed[u], l)
                        mm(bank[0][:, 0:D], few_hot[:, u, :], few_msg[:, u, :], start=new and u == 0, stop=True,
                           skip_group_check=True).then_inc(few_used, 1)
                    pe.reg_add(summed, summed, U)
                    pe.reg_add(landed, landed, 16)

                with pe.If(inexact > 0):
                    pe.wait_ge(ln_ev, 3 * KD * G)
                    with pe.Fori(0, NT) as t:
                        first = pe.value_load(rng[0:1, bass.ds(t, 1)], min_val=1, max_val=PRE + CH - 1)
                        end = pe.value_load(rng[0:1, bass.ds(t + NT, 1)], min_val=PRE + 1, max_val=PRE + CH + 2 * U)
                        pe.wait_ge(few_read, t + (layer * NT + 1))
                        few_round(True)
                        with pe.Fori(first + U, end, U):
                            few_round(False)
                        mm(bank[0][:, 0:2], zeros[:, :], zeros[:, 0:2], start=False, stop=True,
                           skip_group_check=True).then_inc(few_sum, 1)
                        pe.wait_ge(few_read, t + (layer * NT + 2))
                        pe.wait_ge(few_ev, t + (layer * NT + 1))
                        for k in range(KD):
                            last = nc.tensor.transpose(bank[1][:, k * TP:(k + 1) * TP], few_tile[:, k * P:(k + 1) * P], ident[0:TP, 0:TP])
                        last.then_inc(few_t, 1)
                    pe.wait_ge(few_xt, layer + 1)
                with pe.Else():
                    pe.wait_ge(split_d, layer * 4 + 4)
                    pe.wait_ge(at_ok, 2)
                    for f in range(KD):
                        def neighbours(s, start):
                            for part in range(PARTS):
                                for i in range(AB):
                                    if start and part == 0 and f == 1 and i >= 3:
                                        pe.wait_ge(u_act, layer * 6 + 1)
                                        pe.wait_ge(u_dve, layer * 4 + 1)
                                    w = Ys[:, part, bass.ds(s, 1), f * P:(f + 1) * P].rearrange("p a n -> p (a n)")
                                    v = AT[:, bass.ds(s, 1), i * GN:(i + 1) * GN].rearrange("p a n -> p (a n)")
                                    last = mm(bank[(5 * f + i) % 8][:, 0:GN], w, v, start=start and part == 0, stop=True,
                                              skip_group_check=True)
                            last.then_inc(u_mm, 1)
                        neighbours(0, True)
                        with pe.Fori(1, NT) as s:
                            neighbours(s, False)
                    pe.wait_ge(u_act, layer * 6 + 6)
                    pe.wait_ge(u_dve, layer * 4 + 4)
                with pe.Fori(0, G) as g:
                    for m in range(KD):
                        pe.wait_ge(c1e, g * KD + (layer * KD * G + m + 1))
                        for k in range(KD):
                            last = mm(bank[2 + m][:, 0:GN], gw[:, 2 * layer, k, m * P:(m + 1) * P], XT[:, k, bass.ds(g * GN, GN)],
                                      start=(k == 0), stop=(k == KD - 1))
                        last.then_inc(c1, 1)
                with pe.Fori(0, G) as g:
                    pe.wait_ge(zs_ok, g * KD + (layer * KD * G + KD))
                    for j in range(TG):
                        pe.wait_ge(c2e, g * TG + (layer * NT + j + 1))
                        o = bank[4 + j % 2][0:TP, 0:D]
                        for k in range(KD):
                            mm(o, zs[:, k, j * TP:(j + 1) * TP], gw[:, 2 * layer + 1, k, :], start=(k == 0), stop=False)
                        mm(o, ones[0:1, 0:TP], (b1b_row, b2b_row)[layer], start=False, stop=True).then_inc(c2, 1)

            pe.wait_ge(ld_moe, 16 * 10)
            pe.wait_ge(e2_ones, 1)
            ln_transposes(0, 3, 3 * KD * G)

            def second_ffn(g, more):
                pe.wait_ge(ln_ev, g * KD + (3 * KD * G + KD))
                pe.wait_ge(o_ok, g * TG + 1)
                for j in range(TG):
                    o = bank[7][0:TP, j * NE:(j + 1) * NE]
                    for k in range(KD):
                        mm(o, pT3[:, k, j * TP:(j + 1) * TP], gW[:, k, :], start=(k == 0), stop=False)
                    last = mm(o, ones[0:1, 0:TP], gb_row, start=False, stop=True)
                last.then_inc(mg, 1)
                for m in range(6):
                    pe.wait_ge(m1e, g * 6 + (m + 1))
                    for k in range(KD):
                        w = sW1[:, k, m * P:(m + 1) * P] if m < 2 else eW1[:, m - 2, k, :]
                        last = mm(bank[(5, 6)[m % 2]][:, 0:GN], w, pT3[:, k, :], start=(k == 0), stop=(k == KD - 1))
                    last.then_inc(m1, 1)
                if more:
                    ln_transposes(g + 1, 3, g * KD + (3 * KD * G + KD))
                pe.wait_ge(m1e, g * 6 + 8)
                for m in range(5):
                    if m >= 2:
                        pe.wait_ge(m2e, g * 5 + (m - 1))
                    if m == 0:
                        for k in range(KD):
                            last = mm(bank[5][:, 0:GN], sW2[:, k, :], s1[:, k, :], start=(k == 0), stop=(k == KD - 1))
                    else:
                        last = mm(bank[(5, 6)[m % 2]][0:EH2, 0:GN], eW2[:, m - 1, :], e1[:, m - 1, :], start=True, stop=True)
                    last.then_inc(m2, 1)
                pe.wait_ge(m2e, g * 5 + 5)
                pe.wait_ge(mg_ev, g * 2 + 1)
                for j in range(TG):
                    shared, first, second = M3[j % 2]
                    pe.wait_ge(o_ok, g * TG + (j + 1))
                    o = bank[shared][0:TP, 0:D]
                    mm(o, s2[:, j * TP:(j + 1) * TP], sW3, start=True, stop=False)
                    mm(o, ones[0:1, 0:TP], sb3_row, start=False, stop=True)
                    for e in range(NE):
                        last = mm(bank[(first, second)[e // 2]][0:TP, (e % 2) * D:(e % 2 + 1) * D], e2[:, e, j * TP:(j + 1) * TP],
                                  eW3[:, e, :], start=True, stop=True)
                    last.then_inc(m3, 1)

            with pe.Fori(0, G - 1) as g:
                second_ffn(g, True)
            second_ffn(G - 1, False)


GATE_STEPS = 15


_INS = ["x", "src", "dst", "edge_type_8", "L0_gnn_basis", "L0_gnn_comp", "L0_gnn_loop_weight", "L0_gnn_bias_param",
        "L0_ffn_wr", "L0_ffn_br", "L0_ffn_w1", "L0_ffn_b1", "L0_ffn_w2", "L0_ffn_b2",
        "L1_gnn_g0", "L1_gnn_b0", "L1_gnn_W1a", "L1_gnn_b1a", "L1_gnn_g1", "L1_gnn_bt1", "L1_gnn_W1b", "L1_gnn_b1b",
        "L1_gnn_W2a", "L1_gnn_b2a", "L1_gnn_g2", "L1_gnn_bt2", "L1_gnn_W2b", "L1_gnn_b2b",
        "L1_ffn_sW1", "L1_ffn_sb1", "L1_ffn_sW2", "L1_ffn_sb2", "L1_ffn_sW3", "L1_ffn_sb3",
        "L1_ffn_eW1", "L1_ffn_eb1", "L1_ffn_eW2", "L1_ffn_eb2", "L1_ffn_eW3", "L1_ffn_eb3", "L1_ffn_gW", "L1_ffn_gb"]


def kernel(**inputs):
    import numpy as _np
    import concourse.bacc as _bacc
    from concourse import mybir as _mybir
    from concourse.bass_utils import run_bass_kernel_spmd as _run

    nc = _bacc.Bacc("TRN2", target_bir_lowering=False, num_devices=1)
    arrays, args = {}, {}
    for name in _INS:
        v = _np.ascontiguousarray(inputs[name])
        arrays[f"in_{name}"] = v
        args[name] = nc.dram_tensor(f"in_{name}", v.shape, _mybir.dt.from_np(v.dtype), kind="ExternalInput").ap()
    out = nc.dram_tensor("out_dram", (N, D), _mybir.dt.float32, kind="ExternalOutput").ap()
    h_table = nc.dram_tensor("h_table", (N * R, D), _mybir.dt.float32, kind="Internal").ap()
    x_table = nc.dram_tensor("x_table", (N, D), _mybir.dt.float32, kind="Internal").ap()
    gnn_ffn_kernel(nc, args, out, h_table, x_table)
    r = _run(nc, [arrays], core_ids=[0])
    return r.results[0]["out_dram"]
```

```python
from contextlib import ExitStack

import concourse.bass as bass
from concourse import mybir

F32 = mybir.dt.float32
BF16 = mybir.dt.bfloat16
I32 = mybir.dt.int32
U16 = mybir.dt.uint16
ALU = mybir.AluOpType
ACT = mybir.ActivationFunctionType
AX = mybir.AxisListType.X

P = 128
N = 2500
D = 256
KD = D // P
E = 80000
TP = 125
NT = N // TP
TG = 4
G = NT // TG
GN = TP * TG
CH = E // P
CJ = CH // TP
U = 4
PRE = U
PAD = PRE + CH + 3 * U
R = 8
NB = 4
H = 1024
HM = H // P
KEEP = 1249
EPS = 1e-5
NE = 4
EH1, EH2 = 128, 64
FAR = 4096.0
EDGE_BANKS = (7, 0, 7)
SPREAD_BANKS = (((7, 0), (0, 0)), ((1, 0), (0, P)))
PARTS = 3
EXACT = 254.0
AB_ACT, AB_DVE = (0, 2, 4), (1, 3)
AB = 5
M3 = ((7, 5, 6), (2, 3, 4))
BLOCKS = [(0, 8), (8, 16), (16, 20)]


class Count:

    def __init__(self, sem):
        self.sem, self.base, self.k, self.reg, self.per = sem, 0, 0, None, 0

    def step(self, ins):
        ins.then_inc(self.sem, 1)
        self.k += 1
        return self.at(self.k)

    def at(self, k):
        return self.base + k if self.reg is None else self.reg * self.per + (self.base + k)

    def enter(self, reg, per):
        self.base, self.k, self.reg, self.per = self.base + self.k, 0, reg, per

    def leave(self, trips):
        assert self.k == self.per, (self.k, self.per)
        self.base, self.k, self.reg = self.base + trips * self.per, 0, None


def gnn_ffn_kernel(nc, a, out, h_table, x_table):
    with ExitStack() as ctx:
        def sb(name, shape, dt=F32):
            return ctx.enter_context(nc.sbuf_tensor(name, shape, dt))

        def sem(name):
            return ctx.enter_context(nc.semaphore(name))

        bank = [ctx.enter_context(nc.psum_tensor(f"bank{i}", [P, 512], F32)) for i in range(8)]

        bank16 = [b[:, :].bitcast(BF16) for b in bank]
        class Area:
            def __init__(self, name, words):
                self.t, self.words, self.n = sb(name, [P, words]), words, 0

            def take(self, words, parts=P, dt=None):
                v = self.t[0:parts, self.n:self.n + words]
                self.n += words
                assert self.n <= self.words, (self.n, self.words)
                return v if dt is None else v.bitcast(dt)

            def anew(self, at=0):
                self.n = at
                return self

        NH = N // 2
        X = sb("X", [TP, NT, D])
        adj = Area("adj", NT * NH)
        rows = Area("rows", NT * D)
        mid = Area("mid", PARTS * NT * D // 2)
        low = Area("low", 6500)

        ident = sb("ident", [P, P])
        ident16 = sb("ident16", [P, P], BF16)
        ones = sb("ones", [P, P])
        zeros = sb("zeros", [P, P], BF16)
        node_no = sb("node_no", [P, NT * P], U16)
        tri = sb("tri", [TP, TP])
        half = sb("half", [P, TG])
        m_exact = sb("m_exact", [P, 1])
        tile_lo = sb("tile_lo", [NT, 1])
        tile_hi = sb("tile_hi", [NT, 1])
        earlier = sb("earlier", [TP, TG * NE * NE])

        src_of = sb("src_of", [P, PAD], I32)
        dst_of = sb("dst_of", [P, PAD])
        rng = sb("rng", [1, 3 * NT], I32)
        slot = sb("slot", [P, U], I32)

        stats = sb("stats", [TP, TG, 6])
        mv = sb("mv", [TP, TG, 2])
        means = sb("means", [TP, NT])
        veps = sb("veps", [TP, TG])
        rstd = sb("rstd", [TP, NT])
        br_col = sb("br_col", [P, 1])
        wr_col = sb("wr_col", [P, KD])
        b1_col = sb("b1_col", [P, HM])
        gin_col = sb("gin_col", [P, 8, KD])
        sb1_col = sb("sb1_col", [P, KD])
        sb2_col = sb("sb2_col", [P, 1])
        eb1_col = sb("eb1_col", [P, NE])
        eb2_col = sb("eb2_col", [EH2, NE])
        comp_bc = sb("comp_bc", [P, R * NB])
        bn_st = sb("bn_st", [P, KD, G, 6])
        bn_mv = sb("bn_mv", [P, KD, 2])
        bn_ve, bn_rs, bn_sc, bn_ms, bn_bi = (sb(n, [P, KD]) for n in ("bn_ve", "bn_rs", "bn_sc", "bn_ms", "bn_bi"))
        cmax = sb("cmax", [TP, 2, CJ])
        lohi = sb("lohi", [NT, 2])
        over = sb("over", [TP, NT])
        over_max = sb("over_max", [TP, 1])
        flag = sb("flag", [1, 1], I32)
        wcol = sb("wcol", [TP, NT])
        cnt = sb("cnt", [TP, 3, NT])
        rank = sb("rank", [TP, NT])
        gate_w = sb("gate_w", [TP, NT])
        gred = sb("gred", [TP, 4, TG])

        adj.anew()
        W0 = adj.take(KD * (R + 1) * D).rearrange("p (k n) -> p k n", k=KD)
        basis = adj.take(NB * KD * D).rearrange("p (b k o) -> p b k o", b=NB, k=KD)
        hst = adj.take(2 * R * D, TP).rearrange("p (u n) -> p u n", u=2)
        pT0 = adj.take(KD * GN).rearrange("p (k n) -> p k n", k=KD)
        edge_i = adj.take(3 * CJ * P, TP, I32).rearrange("p (a n) -> p a n", a=3)
        edge_f = adj.take(3 * CJ * P, TP).rearrange("p (a n) -> p a n", a=3)
        spread = adj.take(2 * CH, TP).rearrange("p (a n) -> p a n", a=2)
        near = adj.take(CH, NT)
        chunk_no = adj.take(CH, NT)
        bias_rows = adj.take(D, TP)
        lo_row = adj.take(2 * NT, 1)
        nrm = low.anew(4100).take(TG * D, TP).rearrange("p (t d) -> p t d", t=TG)
        hot_src = rows.anew().take(U * NH, P, BF16).rearrange("p (u n) -> p u n", u=U)
        mid.anew()
        abf = mid.take(NH, TP, BF16)
        over_junk = mid.take(NH, TP, BF16)
        msg = mid.take(U * D).rearrange("p (u d) -> p u d", u=U)
        onehot = mid.take(U * P).rearrange("p (u n) -> p u n", u=U)
        hot16 = mid.take(U * P // 2, P, BF16).rearrange("p (u n) -> p u n", u=U)
        hrow_of = mid.take(PAD, P, I32)
        AT = adj.anew().take(NT * NH, TP, BF16).rearrange("p (t n) -> p t n", t=NT)
        at_flat = adj.anew().take(NT * NH, TP, BF16)
        XT = rows.anew().take(KD * N).rearrange("p (k n) -> p k n", k=KD)
        mid.anew()
        WB = mid.take(N)
        w1 = mid.take(KD * H).rearrange("p (k n) -> p k n", k=KD)
        w2 = mid.take(HM * D).rearrange("p (k n) -> p k n", k=HM)
        wr_rep = mid.take(KD * P).rearrange("p (k n) -> p k n", k=KD)
        b2_rows = mid.take(D, TP)
        rank_tri = mid.take(TP, TP)
        low.anew()
        hT = low.take(HM * GN).rearrange("p (m n) -> p m n", m=HM)
        rank_tmp = [low.take(NH, TP, BF16) for _ in range(2)]
        diag = hT[0:TP, 0:5, :].rearrange("p a n -> p (a n)")
        Y = rows.anew().take(NT * D, TP).rearrange("p (t d) -> p t d", t=NT)
        Ys = mid.anew().take(PARTS * NT * D // 2, TP, BF16).rearrange("p (t s d) -> p t s d", s=PARTS, t=NT)
        ZT = mid.anew(mid.words - KD * N).take(KD * N).rearrange("p (g k n) -> p g k n", g=G, k=KD)
        low.anew()
        gw = low.take(4 * KD * D).rearrange("p (w k n) -> p w k n", w=4, k=KD)
        zs = low.take(KD * GN).rearrange("p (h k n) -> p h k n", h=2, k=KD)
        bn_rep = low.take(4 * P).rearrange("p (q n) -> p q n", q=4)
        bn_row = low.take(4 * P, TP)
        res = low.anew(4100).take(TG * D, TP).rearrange("p (t d) -> p t d", t=TG)
        b1b_row, b2b_row = low.take(D, 1), low.take(D, 1)
        adj.anew()
        few_msg = adj.take(U * D).rearrange("p (u d) -> p u d", u=U)
        few_hot = adj.take(U * P).rearrange("p (u n) -> p u n", u=U)
        few_tile = adj.take(D, TP)
        few_T = adj.take(KD * N).rearrange("p (k n) -> p k n", k=KD)
        adj.anew()
        sW1 = adj.take(KD * D).rearrange("p (k n) -> p k n", k=KD)
        sW2 = adj.take(KD * P).rearrange("p (k n) -> p k n", k=KD)
        sW3 = adj.take(D)
        eW1 = adj.take(NE * KD * EH1).rearrange("p (e k n) -> p e k n", e=NE, k=KD)
        eW2 = adj.take(NE * EH2).rearrange("p (e n) -> p e n", e=NE)
        eW3 = adj.take(NE * D, EH2 + 1).rearrange("p (e n) -> p e n", e=NE)
        gW = adj.take(KD * NE).rearrange("p (k n) -> p k n", k=KD)
        s1 = adj.take(KD * GN).rearrange("p (k n) -> p k n", k=KD)
        e1 = adj.take(NE * GN).rearrange("p (k n) -> p k n", k=NE)
        s2 = adj.take(GN)
        e2 = adj.take(NE * GN, EH2 + 1).rearrange("p (k n) -> p k n", k=NE)
        pT3 = adj.take(KD * GN).rearrange("p (k n) -> p k n", k=KD)
        sb3_rows, gb_row = adj.take(D, TP), adj.take(NE, 1)
        small = adj.take(8 * TG * NE, TP).rearrange("p (i n) -> p i n", i=8)
        pair = adj.take(2 * TG * NE * NE, TP).rearrange("p (i n) -> p i n", i=2)

        ld_edges, ld_x0, ld_x, ld_w0 = sem("ld_edges"), sem("ld_x0"), sem("ld_x"), sem("ld_w0")
        ld_small, ld_ffn, ld_gin, ld_moe = sem("ld_small"), sem("ld_ffn"), sem("ld_gin"), sem("ld_moe")
        consts = sem("consts")
        dve_order = sem("dve_order")
        dve_passed, sp_passed, pool_passed = sem("dve_passed"), sem("sp_passed"), sem("pool_passed")
        edges_f, edges_t, edges_ev = sem("edges_f"), sem("edges_t"), sem("edges_ev")
        spread_ok, spread_bc, lohi_ok, lohi_t, rng_ok = (sem(n) for n in (
            "spread_ok", "spread_bc", "lohi_ok", "lohi_t", "rng_ok"))
        ln_var, ln_rstd, ln_nrm, ln_t, ln_ev = (sem(n) for n in (
            "ln_var", "ln_rstd", "ln_nrm", "ln_t", "ln_ev"))
        early_cols = sem("early_cols")
        w0_ok, h_mm, h_act, h_dve, hst_free, table_ok = (sem(n) for n in (
            "w0_ok", "h_mm", "h_act", "h_dve", "hst_free", "table_ok"))
        hst_dma = [sem(f"hst_dma{i}") for i in range(2)]
        used, hot, slot_ok = sem("used"), sem("hot"), sem("slot_ok")
        gathered = [sem(f"gathered{u}") for u in range(U)]
        tile_sum, tile_read, a_act, a_dve, over_ok, at_t, at_ev, at_ok = (sem(n) for n in (
            "tile_sum", "tile_read", "a_act", "a_dve", "over_ok", "at_t", "at_ev", "at_ok"))
        split_a, split_d, u_mm, u_act, u_dve = (sem(n) for n in ("split_a", "split_d", "u_mm", "u_act", "u_dve"))
        over_max_ok, over_mm, flag_ok = sem("over_max_ok"), sem("over_mm"), sem("flag_ok")
        few_table, few_dma, few_slot, few_used, few_made, few_sum, few_read, few_t, few_ev, few_xt = (sem(n) for n in (
            "few_table", "few_dma", "few_slot", "few_used", "few_made", "few_sum", "few_read", "few_t", "few_ev", "few_xt"))
        few_landed = [sem(f"few_landed{u}") for u in range(U)]
        wr_ok, wb_mm, wb_ok, diag_ok = (sem(n) for n in ("wr_ok", "wb_mm", "wb_ok", "diag_ok"))
        f1, f1e, f2, f2e = sem("f1"), sem("f1e"), sem("f2"), sem("f2e")
        bn_ve_ok, bn_rs_ok, bn_ok, bn_mm, y_ok = (sem(n) for n in (
            "bn_ve_ok", "bn_rs_ok", "bn_ok", "bn_mm", "y_ok"))
        c1, c1e, c1s, zs_ok, c2, c2e = (sem(n) for n in ("c1", "c1e", "c1s", "zs_ok", "c2", "c2e"))
        m1, m1e, m2, m2e, mg, mg_ev, mexp, m3, o_ok, o_st, e2_ones = (sem(n) for n in (
            "m1", "m1e", "m2", "m2e", "mg", "mg_ev", "mexp", "m3", "o_ok", "o_st", "e2_ones"))

        ctx.enter_context(nc.allow_non_contiguous_dma(reason="bias columns and per-tile rows"))
        block = ctx.enter_context(nc.Block())


        @block.sync
        def _(sp):
            def node_dma(dst, src, lo, hi, s):
                sp.dma_start(dst(0, lo), src(0, lo)).then_inc(s, 16)
                sp.dma_start(dst(lo, hi), src(lo, hi)).then_inc(s, 16)

            xv = a["x"].rearrange("(t p) d -> p t d", p=TP)
            node_dma(lambda l, h: X[l:h, 0:TG, :], lambda l, h: xv[l:h, 0:TG, :], 112, TP, ld_x0)
            sp.dma_start(comp_bc[:, :], a["L0_gnn_comp"].rearrange("r b -> (r b)").partition_broadcast(P)).then_inc(ld_w0, 16)
            sp.dma_start(basis, a["L0_gnn_basis"].rearrange("b (k p) o -> p b k o", p=P)).then_inc(ld_w0, 16)
            sp.dma_start(W0[:, :, R * D:(R + 1) * D],
                         a["L0_gnn_loop_weight"].rearrange("(k p) o -> p k o", p=P)).then_inc(ld_w0, 16)
            sp.dma_start(bias_rows, a["L0_gnn_bias_param"].partition_broadcast(TP)).then_inc(ld_w0, 16)
            node_dma(lambda l, h: X[l:h, TG:NT, :], lambda l, h: xv[l:h, TG:NT, :], 112, TP, ld_x)
            for i, name in enumerate(("src", "edge_type_8", "dst")):
                v = a[name].rearrange("(p n) -> p n", p=TP)
                node_dma(lambda l, h: edge_i[l:h, i, :], lambda l, h: v[l:h, :], 112, TP, ld_edges)

            hv = h_table.rearrange("(t p r) o -> t p (r o)", p=TP, r=R)
            with sp.Fori(0, NT // 2) as g:
                for u in range(2):
                    sp.wait_ge(h_act, g * 4 + (2 * u + 4))
                    sp.sem_inc(sp_passed, 1)
                    sp.wait_ge(h_dve, g * 6 + (3 * u + 6))
                    sp.sem_inc(sp_passed, 1)
                    for lo, hi in ((0, 112), (112, TP)):
                        sp.dma_start(hv[bass.ds(g * 2 + u, 1), lo:hi, :].rearrange("a p n -> (a p) n"),
                                     hst[lo:hi, u, :]).then_inc(hst_dma[u], 16)
                    sp.wait_ge(hst_dma[u], g * 32 + 32)
                    sp.sem_inc(hst_free, 1)
            sp.sem_inc(table_ok, 1)

            sp.wait_ge(over_ok, 1 + NT)
            sp.wait_ge(at_ev, 2 + len(BLOCKS) * NT)
            sp.dma_start(w1, a["L0_ffn_w1"].rearrange("(k p) n -> p k n", p=P)).then_inc(ld_ffn, 16)
            sp.dma_start(w2, a["L0_ffn_w2"].rearrange("(k p) n -> p k n", p=P)).then_inc(ld_ffn, 16)
            sp.dma_start(b2_rows, a["L0_ffn_b2"].partition_broadcast(TP)).then_inc(ld_ffn, 16)
            sp.wait_ge(f2e, 8 + NT)
            for i, name in enumerate(("L1_gnn_W1a", "L1_gnn_W1b", "L1_gnn_W2a", "L1_gnn_W2b")):
                sp.dma_start(gw[:, i, :, :], a[name].rearrange("(k p) n -> p k n", p=P)).then_inc(ld_gin, 16)
            for dst, name in ((b1b_row, "L1_gnn_b1b"), (b2b_row, "L1_gnn_b2b")):
                sp.dma_start(dst, a[name].unsqueeze(0)).then_inc(ld_gin, 16)
            sp.wait_ge(flag_ok, 1)
            inexact = sp.value_load(flag[0:1, 0:1], min_val=0, max_val=1)
            with sp.If(inexact > 0):
                tv = x_table.rearrange("(t p) o -> p t o", p=TP)
                for layer in range(2):
                    if layer == 0:
                        sp.wait_ge(y_ok, NT)
                    else:
                        sp.wait_ge(c2e, 4 + NT)
                    node_dma(lambda l, h: tv[l:h, :, :], lambda l, h: Y[l:h, :, :], 112, TP, few_dma)
                    sp.wait_ge(few_dma, 32 * (layer + 1))
                    sp.sem_inc(few_table, 1)
            sp.wait_ge(c1s, 2 * KD * G)
            moe = [(sW1, a["L1_ffn_sW1"].rearrange("(k p) n -> p k n", p=P)),
                   (sW2, a["L1_ffn_sW2"].rearrange("(k p) n -> p k n", p=P)),
                   (sW3, a["L1_ffn_sW3"]),
                   (eW1, a["L1_ffn_eW1"].rearrange("e (k p) n -> p e k n", p=P)),
                   (eW2, a["L1_ffn_eW2"].rearrange("e p n -> p e n")),
                   (eW3[0:EH2, :, :], a["L1_ffn_eW3"].rearrange("e p n -> p e n")),
                   (eW3[EH2:EH2 + 1, :, :], a["L1_ffn_eb3"].unsqueeze(0)),
                   (gW, a["L1_ffn_gW"].rearrange("(k p) n -> p k n", p=P)),
                   (sb3_rows, a["L1_ffn_sb3"].partition_broadcast(TP)), (gb_row, a["L1_ffn_gb"].unsqueeze(0))]
            for dst, src in moe:
                sp.dma_start(dst, src).then_inc(ld_moe, 16)
            ov = out.rearrange("(t p) d -> p t d", p=TP)
            with sp.Fori(0, G) as g:
                sp.wait_ge(o_ok, g * TG + (TG + 2))
                sp.sem_inc(sp_passed, 1)
                for lo, hi in ((0, 112), (112, TP)):
                    sp.dma_start(ov[lo:hi, bass.ds(g * TG, TG), :], X[lo:hi, bass.ds(g * TG, TG), :]).then_inc(o_st, 16)
            sp.wait_ge(o_st, 32 * G)

        @block.gpsimd
        def _(pool):
            pool.memset(ident[:, :], 0.0).then_inc(consts, 1)
            pool.memset(ones[:, :], 1.0).then_inc(consts, 1)
            pool.memset(zeros[:, :], 0.0).then_inc(consts, 1)
            pool.memset(m_exact[:, :], -EXACT).then_inc(consts, 1)
            pool.memset(half[:, :], -0.5).then_inc(consts, 1)
            pool.memset(tri[:, :], 1.0).then_inc(consts, 1)
            pool.memset(earlier[:, :], 1.0).then_inc(consts, 1)
            pool.memset(dst_of[:, :], -1.0).then_inc(consts, 1)
            pool.memset(src_of[:, :], 0).then_inc(consts, 1)
            pool.memset(hrow_of[:, :], 0).then_inc(consts, 1)
            pool.iota(node_no[:, :], pattern=[[1, NT * P]], base=0, channel_multiplier=0,
                      allow_small_or_imprecise_dtypes=True).then_inc(consts, 1)
            pool.iota(chunk_no, pattern=[[1, CH]], base=0, channel_multiplier=0,
                      allow_small_or_imprecise_dtypes=True).then_inc(consts, 1)
            pool.iota(tile_lo[:, :], pattern=[[1, 1]], base=0, channel_multiplier=TP,
                      allow_small_or_imprecise_dtypes=True).then_inc(consts, 1)
            pool.iota(tile_hi[:, :], pattern=[[1, 1]], base=TP, channel_multiplier=TP,
                      allow_small_or_imprecise_dtypes=True).then_inc(consts, 1)
            pool.wait_ge(consts, 14)
            pool.affine_select(out=ident[:, :], in_=ident[:, :], compare_op=ALU.not_equal, fill=1.0,
                               base=0, pattern=[[-1, P]], channel_multiplier=1).then_inc(consts, 1)
            pool.affine_select(out=tri[:, :], in_=tri[:, :], compare_op=ALU.is_gt, fill=0.0,
                               base=0, pattern=[[-1, TP]], channel_multiplier=1).then_inc(consts, 1)
            pool.affine_select(out=earlier[:, :].rearrange("p (t e j) -> p t e j", t=TG, e=NE),
                               in_=earlier[:, :].rearrange("p (t e j) -> p t e j", t=TG, e=NE),
                               compare_op=ALU.is_gt, fill=0.0, base=0,
                               pattern=[[0, TG], [1, NE], [-1, NE]], channel_multiplier=0).then_inc(consts, 1)
            def ln_root(g, ln):
                pool.wait_ge(ln_var, g + (ln * G + 1))
                pool.tensor_tensor(rstd[:, bass.ds(g * TG, TG)], veps[:, :], half[0:TP, 0:TG], ALU.pow).then_inc(ln_rstd, 1)

            with pool.Fori(0, G) as g:
                ln_root(g, 0)

            def col(dst, name, **kw):
                pool.dma_start(dst, a[name].rearrange("(m p) -> p m", **kw)).then_inc(ld_small, 16)
            col(b1_col[:, :], "L0_ffn_b1", p=P)
            for i, name in enumerate(("L1_gnn_g0", "L1_gnn_b0", "L1_gnn_b1a", "L1_gnn_g1", "L1_gnn_bt1",
                                      "L1_gnn_b2a", "L1_gnn_g2", "L1_gnn_bt2")):
                col(gin_col[:, i, :], name, p=P)
            col(sb1_col[:, :], "L1_ffn_sb1", p=P)
            col(sb2_col[:, :], "L1_ffn_sb2", p=P)
            pool.dma_start(eb1_col[:, :], a["L1_ffn_eb1"].rearrange("e p -> p e")).then_inc(ld_small, 16)
            pool.dma_start(eb2_col[:, :], a["L1_ffn_eb2"].rearrange("e p -> p e")).then_inc(ld_small, 16)
            pool.dma_start(wr_col[:, :], a["L0_ffn_wr"].rearrange("(k p) o -> p (k o)", p=P)).then_inc(ld_small, 16)
            pool.dma_start(br_col[:, :], a["L0_ffn_br"].partition_broadcast(P)).then_inc(ld_small, 16)

            sent = pool.alloc_register("sent")
            pool.reg_mov(sent, 0)
            pool.wait_ge(rng_ok, 1)
            with pool.Fori(0, NT) as t:
                first = pool.value_load(rng[0:1, bass.ds(t, 1)], min_val=1, max_val=PRE + CH - 1)
                end = pool.value_load(rng[0:1, bass.ds(t + NT, 1)], min_val=PRE + 1, max_val=PRE + CH + 2 * U)
                with pool.Fori(first, end, U) as c:
                    n = pool.snap(sent, min_val=0, max_val=NT * PAD)
                    for u in range(U):
                        pool.wait_ge(slot_ok, n + (u + 1))
                        pool.sem_inc(pool_passed, 1)
                        pool.wait_ge(table_ok, 1)
                        pool.indirect_dma_start(msg[:, u, :], None, h_table,
                                                bass.IndirectOffsetOnAxis(slot[:, u:u + 1], 0)).then_inc(gathered[u], 16)
                    pool.reg_add(sent, sent, U)

            with pool.Fori(0, G) as g:
                ln_root(g, 1)
            pool.wait_ge(at_ev, 2 + len(BLOCKS) * NT)
            step = N + TP
            own = at_flat[:, 0:(NT - 1) * step].rearrange("p (t q) -> p t q", q=step)[:, :, 0:TP]
            last = at_flat[:, (NT - 1) * step:NT * N]
            pool.tensor_tensor(own, own, ident16[0:TP, 0:TP].unsqueeze(1).to_broadcast([TP, NT - 1, TP]), ALU.add).then_inc(at_ok, 1)
            pool.tensor_tensor(last, last, ident16[0:TP, 0:TP], ALU.add).then_inc(at_ok, 1)
            with pool.Fori(0, G) as g:
                ln_root(g, 2)
            pool.wait_ge(flag_ok, 1)
            inexact = pool.value_load(flag[0:1, 0:1], min_val=0, max_val=1)
            pool.reg_mov(sent, 0)
            for times in range(3):
                pool.wait_ge(bn_ve_ok, 1 + times)
                pool.tensor_tensor(bn_rs[:, :], bn_ve[:, :], half[:, 0:KD], ALU.pow).then_inc(bn_rs_ok, 1)
                if times == 2:
                    break
                with pool.If(inexact > 0):
                    pool.wait_ge(few_table, 1 + times)
                    with pool.Fori(0, NT) as t:
                        first = pool.value_load(rng[0:1, bass.ds(t, 1)], min_val=1, max_val=PRE + CH - 1)
                        end = pool.value_load(rng[0:1, bass.ds(t + NT, 1)], min_val=PRE + 1, max_val=PRE + CH + 2 * U)
                        with pool.Fori(first, end, U) as c:
                            n = pool.snap(sent, min_val=0, max_val=4 * NT * PAD)
                            for u in range(U):
                                pool.wait_ge(few_slot, n + (u + 1))
                                pool.sem_inc(pool_passed, 1)
                                pool.wait_ge(few_table, 1 + times)
                                pool.indirect_dma_start(few_msg[:, u, :], None, x_table,
                                                        bass.IndirectOffsetOnAxis(slot[:, u:u + 1], 0)).then_inc(few_landed[u], 16)
                            pool.reg_add(sent, sent, U)

            ln_root(0, 3)
            pool.wait_ge(ln_rstd, 3 * G + 1)
            pool.wait_ge(ld_moe, 16 * 10)
            pool.memset(e2[EH2:EH2 + 1, :, :], 1.0).then_inc(e2_ones, 1)
            pool.wait_ge(e2_ones, 1)
            with pool.Fori(1, G) as g:
                ln_root(g, 3)

        @block.vector
        def _(dve):
            order = Count(dve_order)

            def link(ins):
                dve.wait_ge(dve_order, order.step(ins))

            def add_rows(g, row):
                xg = X[:, bass.ds(g * TG, TG), :]
                link(nc.vector.tensor_tensor(xg, xg, row.unsqueeze(1).to_broadcast([TP, TG, D]), ALU.add))

            def mean_of(g, j):
                return means[:, bass.ds(g * TG + j, 1)]

            def ln_stats(g, ln):
                for j in range(TG):
                    s = order.step(nc.vector.bn_stats(stats[:, j, :], X[:, bass.ds(g * TG + j, 1), :].rearrange("p a d -> p (a d)")))
                dve.wait_ge(dve_order, s)
                dve.sem_inc(dve_passed, 1)
                for j in range(TG):
                    s = order.step(nc.vector.bn_aggr(mv[:, j, :], stats[:, j, :]))
                dve.wait_ge(dve_order, s)
                if ln == 1:
                    dve.wait_ge(ln_rstd, g + ln * G)
                nc.vector.tensor_scalar(veps[:, :], mv[:, :, 1], EPS, None, ALU.add).then_inc(ln_var, 1)
                link(nc.vector.tensor_copy(means[:, bass.ds(g * TG, TG)], mv[:, :, 0]))

            def ln_apply(g, ln):
                dve.wait_ge(ln_rstd, g + (ln * G + 1))
                dve.wait_ge(ln_t, g + (ln * G + 1))
                for j in range(TG):
                    nc.vector.tensor_scalar(nrm[:, j, :], X[:, bass.ds(g * TG + j, 1), :].rearrange("p a d -> p (a d)"),
                                            mean_of(g, j), rstd[:, bass.ds(g * TG + j, 1)], ALU.subtract, ALU.mult).then_inc(ln_nrm, 1)

            def layernorm(g, ln):
                ln_stats(g, ln)
                ln_apply(g, ln)

            LN_STEPS = 2 * TG + 1
            dve.wait_ge(ld_x0, 32)
            layernorm(0, 0)

            dve.wait_ge(ld_w0, 64)
            for r2 in range(0, R, 2):
                for b in range(NB):
                    for r in (r2, r2 + 1):
                        w = W0[:, :, r * D:(r + 1) * D]
                        c = comp_bc[:, r * NB + b:r * NB + b + 1]
                        if b == 0:
                            order.step(nc.vector.tensor_scalar(w, basis[:, b, :, :], c, None, ALU.mult))
                        else:
                            dve.wait_ge(dve_order, order.at(order.k - 1))
                            order.step(nc.vector.scalar_tensor_tensor(out=w, in0=basis[:, b, :, :], scalar=c, in1=w,
                                                                      op0=ALU.mult, op1=ALU.add))
                dve.wait_ge(dve_order, order.at(order.k))
                dve.sem_inc(w0_ok, 1)

            def prepare_edges():
                dve.wait_ge(ld_edges, 96)
                order.step(nc.vector.tensor_copy(edge_f[:, 0, :], edge_i[:, 0, :]))
                order.step(nc.vector.tensor_copy(edge_f[:, 1, :], edge_i[:, 1, :]))
                link(nc.vector.tensor_copy(edge_f[:, 2, :], edge_i[:, 2, :]))
                nc.vector.scalar_tensor_tensor(out=edge_f[:, 1, :], in0=edge_f[:, 0, :], scalar=float(R),
                                               in1=edge_f[:, 1, :], op0=ALU.mult, op1=ALU.add).then_inc(edges_f, 1)
                targets = edge_f[:, 2, :].rearrange("p (j e) -> p j e", j=CJ)
                order.step(nc.vector.tensor_reduce(cmax[:, 0, :], targets, AX, ALU.max))
                link(nc.vector.tensor_reduce(cmax[:, 1, :], targets, AX, ALU.min))
                dve.wait_ge(consts, 17)
                order.step(nc.vector.tensor_copy(ident16[:, :], ident[:, :]))
                for i in range(2):
                    nc.vector.tensor_tensor(
                        spread[:, i, :].rearrange("p (q j) -> p q j", j=CJ),
                        ident[0:TP, 0:TP].unsqueeze(2).to_broadcast([TP, TP, CJ]),
                        cmax[:, i, :].unsqueeze(1).to_broadcast([TP, TP, CJ]), ALU.mult).then_inc(spread_ok, 1)

            def edge_columns(i):
                dve.wait_ge(edges_t, max(i + 1, 2))
                dst = (src_of, hrow_of, dst_of)[i]
                v = dst[:, PRE:PRE + CH].rearrange("p (q j) -> p j q", j=CJ)
                nc.vector.tensor_copy(v[:, 0:4, :], bank[EDGE_BANKS[i]][:, 0:4 * TP].rearrange("p (j q) -> p j q", j=4)).then_inc(edges_ev, 1)
                nc.vector.tensor_copy(v[:, 4, :], bank[1][:, i * TP:(i + 1) * TP]).then_inc(edges_ev, 1)

            def chunk_limits():
                for i, (limit, op, far, red) in enumerate(((tile_lo, ALU.is_lt, FAR, ALU.min), (tile_hi, ALU.is_ge, -FAR, ALU.max))):
                    dve.wait_ge(spread_bc, 1)
                    for (b, at), lo, hi in zip(SPREAD_BANKS[i], (0, 512), (512, CH)):
                        src = bank[b][0:NT, at:at + hi - lo]
                        link(nc.vector.tensor_scalar(near[:, lo:hi], src, limit[:, :], far, op, ALU.mult))
                    link(nc.vector.tensor_tensor(near[:, 0:CH], near[:, 0:CH], chunk_no, ALU.add))
                    link(nc.vector.tensor_reduce(lohi[:, i:i + 1], near[:, 0:CH], AX, red))
                link(nc.vector.tensor_scalar(lohi[:, 0:1], lohi[:, 0:1], float(CH - 1), None, ALU.min))
                link(nc.vector.tensor_tensor(lohi[:, 1:2], lohi[:, 1:2], lohi[:, 0:1], ALU.max))
                link(nc.vector.tensor_scalar(lohi[:, 1:2], lohi[:, 1:2], 1.0, None, ALU.add))
                nc.vector.scalar_tensor_tensor(out=lohi[:, 1:2], in0=lohi[:, 0:1], scalar=float(2 * U + 1), in1=lohi[:, 1:2],
                                               op0=ALU.add, op1=ALU.max).then_inc(lohi_ok, 1)

            def ranges():
                dve.wait_ge(lohi_t, 1)
                link(nc.vector.tensor_copy(lo_row, bank[0][0:1, 0:2 * NT]))
                firsts, ends, skips = (rng[:, i * NT:(i + 1) * NT] for i in range(3))
                link(nc.vector.tensor_tensor(skips, lo_row[:, 0:NT], lo_row[:, NT:2 * NT], ALU.subtract))
                link(nc.vector.tensor_scalar(skips, skips, U - 1, None, ALU.bitwise_and))
                order.step(nc.vector.tensor_scalar(ends, lo_row[:, NT:2 * NT], float(PRE), None, ALU.add))
                link(nc.vector.tensor_scalar(firsts, lo_row[:, 0:NT], float(PRE), None, ALU.add))
                nc.vector.tensor_tensor(firsts, firsts, skips, ALU.subtract).then_inc(rng_ok, 1)

            def stage0(g, more, between=None):
                add_rows(g, bias_rows)
                for j in range(TG):
                    dve.wait_ge(hst_free, g * TG + (j + 1))
                    for b in (2, 3):
                        dve.wait_ge(h_mm, g * (5 * TG) + (5 * j + b + 1))
                        nc.vector.tensor_copy(hst[:, j % 2, b * 512:(b + 1) * 512], bank[2 + b][0:TP, :]).then_inc(h_dve, 1)
                    dve.wait_ge(h_mm, g * (5 * TG) + (5 * j + 5))
                    xt = X[:, bass.ds(g * TG + j, 1), :].rearrange("p a d -> p (a d)")
                    nc.vector.tensor_tensor(xt, xt, bank[6][0:TP, 0:D], ALU.add).then_inc(h_dve, 1)
                    if j == 0 and more:
                        layernorm(g + 1, 0)
                    if between is not None:
                        between(j)

            dve.wait_ge(ld_x, 32)

            def group0(j):
                if j == 1:
                    prepare_edges()

            def group1(j):
                if j == 0:
                    edge_columns(0)
                    edge_columns(1)
                elif j == 1:
                    edge_columns(2)

            def last_group(j):
                if j == 0:
                    chunk_limits()
                elif j == 2:
                    ranges()

            stage0(0, True, group0)
            stage0(1, True, group1)
            with dve.Fori(2, G - 1) as g:
                order.enter(g - 2, LN_STEPS + 1)
                stage0(g, True)
            order.leave(G - 3)
            stage0(G - 1, False, last_group)

            made = dve.alloc_register("made")
            dve.reg_mov(made, 0)

            dve.wait_ge(rng_ok, 1)
            dve.wait_ge(h_dve, 3 + 3 * NT)

            def hots(t, col, offset, rows_of=None):
                n = dve.snap(made, min_val=0, max_val=NT * PAD)
                for u in range(U):
                    c = col + (u + offset) % U
                    if u == U - 1 and rows_of is not None:
                        read_rows(rows_of)
                    dve.wait_ge(used, n + (u + 1))
                    nc.vector.tensor_copy(slot[:, u:u + 1], hrow_of[:, bass.ds(c, 1)]).then_inc(slot_ok, 1)
                    targets = node_no[:, bass.ds(t * TP, P)]
                    nc.vector.tensor_scalar(hot16[:, u, :], targets, dst_of[:, bass.ds(c, 1)], None, ALU.is_equal).then_inc(hot, 1)
                    nc.vector.tensor_scalar(hot_src[:, u, :], node_no[:, 0:N], src_of[:, bass.ds(c, 1)], None, ALU.is_equal).then_inc(hot, 1)
                    nc.vector.tensor_scalar(onehot[:, u, :], targets, dst_of[:, bass.ds(c, 1)], None, ALU.is_equal).then_inc(hot, 1)
                dve.reg_add(made, made, U)

            def read_rows(t):
                dve.wait_ge(tile_sum, t + 1)
                dve.wait_ge(at_t, t * len(BLOCKS) + 1)
                dve.wait_ge(over_ok, t + 1)
                for i in AB_DVE:
                    if i == AB_DVE[1]:
                        xt = X[:, bass.ds(t, 1), :].rearrange("p a d -> p (a d)")
                        nc.vector.tensor_tensor(xt, xt, bank[0][0:TP, 0:D], ALU.add).then_inc(tile_read, 1)
                    nc.vector.tensor_copy(abf[:, i * GN:(i + 1) * GN], bank[1 + i][0:TP, 0:GN]).then_inc(a_dve, 1)

            def hot_tile(t, before):
                first = dve.value_load(rng[0:1, bass.ds(t, 1)], min_val=1, max_val=PRE + CH - 1)
                end = dve.value_load(rng[0:1, bass.ds(t + NT, 1)], min_val=PRE + 1, max_val=PRE + CH + 2 * U)
                hots(t, first, U - 1, t - 1 if before else None)
                with dve.Fori(first + U, end, U) as c:
                    hots(t, c, 0)

            hot_tile(0, False)
            with dve.Fori(1, NT) as t:
                hot_tile(t, True)
            read_rows(NT - 1)
            dve.wait_ge(tile_read, 1 + NT)

            dve.wait_ge(ld_small, 16 * 15)
            for k in range(KD):
                nc.vector.tensor_scalar(wr_rep[:, k, :], ones[:, :], wr_col[:, k:k + 1], None, ALU.mult).then_inc(wr_ok, 1)

            def normalise_rows(g):
                ln_apply(g, 1)
                dve.wait_ge(ln_nrm, g * TG + (NT + TG))
                xg = X[:, bass.ds(g * TG, TG), :]
                return order.step(nc.vector.tensor_tensor(xg, xg, nrm, ALU.add))

            ln_stats(0, 1)
            with dve.Fori(0, G - 1) as g:
                order.enter(g, LN_STEPS + 1)
                ln_stats(g + 1, 1)
                normalise_rows(g)
            order.leave(G - 1)
            dve.wait_ge(dve_order, order.at(order.k))
            x_complete = normalise_rows(G - 1)
            dve.wait_ge(over_ok, 1 + NT)
            nc.vector.tensor_reduce(over_max[:, :], over[:, :], AX, ALU.max).then_inc(over_max_ok, 1)
            dve.wait_ge(over_mm, 1)
            nc.vector.tensor_scalar(flag[:, :], bank[7][0:1, 0:1], 0.0, None, ALU.is_gt).then_inc(flag_ok, 1)
            dve.wait_ge(flag_ok, 1)
            inexact = dve.value_load(flag[0:1, 0:1], min_val=0, max_val=1)
            dve.reg_mov(made, 0)
            dve.wait_ge(wb_ok, 1 + G)
            dve.wait_ge(dve_order, x_complete)
            dve.wait_ge(ln_t, 1 + 2 * G)
            wb_t = WB[0:TP, :].rearrange("p (t q) -> p t q", t=NT)
            diag_t = diag.rearrange("p (t q) -> p t q", t=NT)
            link(nc.vector.tensor_tensor(diag_t, wb_t, ident[0:TP, 0:TP].unsqueeze(1).to_broadcast([TP, NT, TP]), ALU.mult))
            link(nc.vector.tensor_reduce(wcol[:, :], diag_t, AX, ALU.add))
            dve.sem_inc(diag_ok, 1)
            order.step(nc.vector.memset(cnt[:, 0, 0:1], 0.0))
            for t in range(NT):
                at, w = t * TP, wcol[:, t:t + 1]
                if t:
                    dve.wait_ge(dve_order, order.at(order.k - 2))
                    order.step(nc.vector.tensor_scalar(rank_tmp[0][:, 0:at], WB[0:TP, 0:at], w, None, ALU.is_ge, ALU.add,
                                                       accum_out=cnt[:, 0, t:t + 1]))
                    dve.wait_ge(dve_order, order.at(order.k - 2))
                order.step(nc.vector.tensor_scalar(rank_tmp[1][:, at:N], WB[0:TP, at:N], w, None, ALU.is_gt, ALU.add,
                                                   accum_out=cnt[:, 1, t:t + 1]))
                if t:
                    dve.wait_ge(dve_order, order.at(order.k - 2))
                s = order.step(nc.vector.scalar_tensor_tensor(out=rank_tri, in0=WB[0:TP, at:at + TP], scalar=w,
                                                              in1=tri[:, :], op0=ALU.is_equal, op1=ALU.mult,
                                                              accum_out=cnt[:, 2, t:t + 1]))
            dve.wait_ge(dve_order, s)
            link(nc.vector.tensor_tensor(rank[:, :], cnt[:, 0, :], cnt[:, 1, :], ALU.add))
            link(nc.vector.tensor_tensor(rank[:, :], rank[:, :], cnt[:, 2, :], ALU.add))
            link(nc.vector.scalar_tensor_tensor(out=gate_w[:, :], in0=rank[:, :], scalar=float(KEEP), in1=wcol[:, :],
                                                op0=ALU.is_lt, op1=ALU.mult))

            def first_ffn(g, odd):
                for j in range(TG):
                    xt = X[:, bass.ds(g * TG + j, 1), :].rearrange("p a d -> p (a d)")
                    s = order.step(nc.vector.scalar_tensor_tensor(
                        out=xt, in0=b2_rows, scalar=gate_w[:, bass.ds(g * TG + j, 1)], in1=xt, op0=ALU.mult, op1=ALU.add))
                dve.wait_ge(dve_order, s)
                for j in range(TG):
                    dve.wait_ge(f2, g * TG + (2 * (j // 2) + 2))
                    xt = X[:, bass.ds(g * TG + j, 1), :].rearrange("p a d -> p (a d)")
                    s = order.step(nc.vector.scalar_tensor_tensor(
                        out=xt, in0=bank[4 + 2 * odd + j // 2][0:TP, j % 2 * D:(j % 2 + 1) * D],
                        scalar=gate_w[:, bass.ds(g * TG + j, 1)], in1=xt, op0=ALU.mult, op1=ALU.add))
                dve.wait_ge(dve_order, s)
                dve.sem_inc(f2e, TG)

            def bn_group(g):
                dve.wait_ge(ln_t, g + (2 * G + 2))
                for k in range(KD):
                    nc.vector.bn_stats(bn_st[:, k, bass.ds(g, 1), :].rearrange("p a s -> p (a s)"),
                                       bank[k][:, 0:GN]).then_inc(ln_ev, 1)

            dve.wait_ge(ld_ffn, 48)
            first_ffn(0, 0)
            layernorm(0, 2)
            with dve.Fori(0, (G - 1) // 2) as pair_no:
                order.enter(pair_no, 2 * (2 * TG + LN_STEPS))
                for odd, g in ((1, pair_no * 2 + 1), (0, pair_no * 2 + 2)):
                    first_ffn(g, odd)
                    bn_group(pair_no * 2 + 1 - odd)
                    layernorm(g, 2)
            order.leave((G - 1) // 2)
            bn_group(G - 1)

            def bn_affine(i_gamma, i_beta, times):
                for k in range(KD):
                    s = order.step(nc.vector.bn_aggr(bn_mv[:, k, :], bn_st[:, k, :, :].rearrange("p g s -> p (g s)")))
                dve.wait_ge(dve_order, s)
                nc.vector.tensor_scalar(bn_ve[:, :], bn_mv[:, :, 1], EPS, None, ALU.add).then_inc(bn_ve_ok, 1)
                dve.wait_ge(bn_rs_ok, times)
                link(nc.vector.tensor_tensor(bn_sc[:, :], bn_rs[:, :], gin_col[:, i_gamma, :], ALU.mult))
                link(nc.vector.tensor_tensor(bn_ms[:, :], bn_mv[:, :, 0], bn_sc[:, :], ALU.mult))
                link(nc.vector.tensor_tensor(bn_bi[:, :], gin_col[:, i_beta, :], bn_ms[:, :], ALU.subtract))

            dve.wait_ge(ln_ev, 2 * 2 * G + 2 * G)
            bn_affine(0, 1, 1)
            dve.wait_ge(ld_gin, 96)
            for q in range(4):
                v = (bn_sc, bn_bi)[q // 2][:, q % 2:q % 2 + 1]
                nc.vector.tensor_scalar(bn_rep[:, q, :], ones[:, :], v, None, ALU.mult).then_inc(bn_ok, 1)
            dve.wait_ge(bn_mm, 1)
            link(nc.vector.tensor_copy(bn_row, bank[2][0:TP, :]))

            def beyond_first(g, layer):
                n, ts = 2 * G * layer, bass.ds(g * TG, TG)
                if layer:
                    dve.wait_ge(split_d, g * 2 + n)
                dve.wait_ge(split_a, g * 2 + (n + 1))
                nc.vector.tensor_tensor(res, Y[:, ts, :], Ys[:, ts, 0, :], ALU.subtract).then_inc(split_d, 1)

            def beyond_second(g, layer):
                n, ts = 2 * G * layer, bass.ds(g * TG, TG)
                dve.wait_ge(split_d, g * 2 + (n + 1))
                dve.wait_ge(split_a, g * 2 + (n + 2))
                nc.vector.tensor_tensor(Ys[:, ts, 2, :], res, Ys[:, ts, 1, :], ALU.subtract).then_inc(split_d, 1)

            with dve.Fori(0, G) as g:
                order.enter(g, TG)
                for j in range(TG):
                    t = bass.ds(g * TG + j, 1)
                    s = order.step(nc.vector.scalar_tensor_tensor(
                        out=Y[:, t, :].rearrange("p a d -> p (a d)"), in0=X[:, t, :].rearrange("p a d -> p (a d)"),
                        scalar=mean_of(g, j), in1=bn_row[:, 0:D], op0=ALU.subtract, op1=ALU.mult))
                dve.wait_ge(dve_order, s)
                for j in range(TG):
                    yt = Y[:, bass.ds(g * TG + j, 1), :].rearrange("p a d -> p (a d)")
                    nc.vector.scalar_tensor_tensor(out=yt, in0=yt, scalar=rstd[:, bass.ds(g * TG + j, 1)], in1=bn_row[:, D:2 * D],
                                                   op0=ALU.mult, op1=ALU.add).then_inc(y_ok, 1)
                beyond_first(g, 0)
                beyond_second(g, 0)
            order.leave(G)

            for layer in range(2):
                with dve.If(inexact > 0):
                    dve.wait_ge(at_ok, 2)
                    with dve.Fori(0, NT) as t:
                        first = dve.value_load(rng[0:1, bass.ds(t, 1)], min_val=1, max_val=PRE + CH - 1)
                        end = dve.value_load(rng[0:1, bass.ds(t + NT, 1)], min_val=PRE + 1, max_val=PRE + CH + 2 * U)
                        with dve.Fori(first, end, U) as c:
                            n = dve.snap(made, min_val=0, max_val=4 * NT * PAD)
                            for u in range(U):
                                dve.wait_ge(few_used, n + (u + 1))
                                nc.vector.tensor_copy(slot[:, u:u + 1], src_of[:, bass.ds(c + u, 1)]).then_inc(few_slot, 1)
                                nc.vector.tensor_scalar(few_hot[:, u, :], node_no[:, bass.ds(t * TP, P)],
                                                        dst_of[:, bass.ds(c + u, 1)], None, ALU.is_equal).then_inc(few_made, 1)
                            dve.reg_add(made, made, U)
                        dve.wait_ge(few_sum, t + (layer * NT + 1))
                        dve.wait_ge(few_t, t + (layer * NT + 1))
                        yt = Y[:, bass.ds(t, 1), :].rearrange("p a d -> p (a d)")
                        nc.vector.tensor_tensor(few_tile, yt, bank[0][0:TP, 0:D], ALU.add).then_inc(few_read, 1)
                with dve.Else():
                    dve.wait_ge(split_d, (layer + 1) * 2 * G)
                    for f in range(KD):
                        dve.wait_ge(u_mm, (layer * KD + f + 1) * NT)
                        for i in (1, 3):
                            nc.vector.tensor_copy(XT[:, f, i * GN:(i + 1) * GN], bank[(5 * f + i) % 8][:, 0:GN]).then_inc(u_dve, 1)
                with dve.Fori(0, G) as g:
                    dve.wait_ge(c1e, g * KD + (layer * KD * G + KD + KD))
                    for k in range(KD):
                        nc.vector.bn_stats(bn_st[:, k, bass.ds(g, 1), :].rearrange("p a s -> p (a s)"),
                                           ZT[:, bass.ds(g, 1), k, :].rearrange("p a n -> p (a n)")).then_inc(c1s, 1)
                dve.wait_ge(c1s, KD * G * (layer + 1))
                bn_affine(3 + 3 * layer, 4 + 3 * layer, 2 + layer)
                dve.sem_inc(bn_ok, 1)
                if layer == 1:
                    with dve.Fori(0, G) as g:
                        for j in range(TG):
                            dve.wait_ge(c2, g * TG + (NT + TG + j + 1))
                            xt = X[:, bass.ds(g * TG + j, 1), :].rearrange("p a d -> p (a d)")
                            nc.vector.scalar_tensor_tensor(out=xt, in0=bank[4 + j][0:TP, 0:D], scalar=0.0, in1=xt,
                                                           op0=ALU.max, op1=ALU.add).then_inc(c2e, 1)
                else:
                    def next_rows(g, behind):
                        for j in range(TG):
                            if j == 2 and behind:
                                beyond_first(g - 1, 1)
                            dve.wait_ge(c2, g * TG + (TG + j + 1))
                            nc.vector.tensor_scalar(Y[:, bass.ds(g * TG + j, 1), :].rearrange("p a d -> p (a d)"),
                                                    bank[4 + j][0:TP, 0:D], 0.0, None, ALU.max).then_inc(c2e, 1)
                        if behind:
                            beyond_second(g - 1, 1)

                    next_rows(0, False)
                    with dve.Fori(1, G) as g:
                        next_rows(g, True)
                    beyond_first(G - 1, 1)
                    beyond_second(G - 1, 1)
            dve.wait_ge(c2e, 4 + 2 * NT)

            def v3(i):
                return small[:, i, :].rearrange("p (t e) -> p t e", t=TG)

            def over_e(col):
                return col.unsqueeze(2).to_broadcast([TP, TG, NE])

            layernorm(0, 3)
            dve.wait_ge(ld_moe, 16 * 10)

            def second_ffn(g, more):
                if more:
                    layernorm(g + 1, 3)
                add_rows(g, sb3_rows)
                dve.wait_ge(mg, g + 1)
                logits = bank[7][0:TP, 0:TG * NE].rearrange("p (t e) -> p t e", t=TG)
                link(nc.vector.tensor_reduce(gred[:, 0, :], logits, AX, ALU.max))
                nc.vector.tensor_tensor(v3(0), logits, over_e(gred[:, 0, :]), ALU.subtract).then_inc(mg_ev, 1)
                dve.wait_ge(mexp, g * 2 + 1)
                link(nc.vector.tensor_reduce(gred[:, 1, :], v3(1), AX, ALU.add))
                link(nc.vector.reciprocal(gred[:, 2, :], gred[:, 1, :]))
                link(nc.vector.tensor_tensor(v3(2), v3(1), over_e(gred[:, 2, :]), ALU.mult))
                pe_ = v3(2).unsqueeze(3).to_broadcast([TP, TG, NE, NE])
                pj_ = v3(2).unsqueeze(2).to_broadcast([TP, TG, NE, NE])
                q4 = [pair[:, i, :].rearrange("p (t e j) -> p t e j", t=TG, e=NE) for i in range(2)]
                order.step(nc.vector.tensor_tensor(q4[0], pj_, pe_, ALU.is_gt))
                link(nc.vector.tensor_tensor(q4[1], pj_, pe_, ALU.is_equal))
                link(nc.vector.tensor_tensor(pair[:, 1, :], pair[:, 1, :], earlier[:, :], ALU.mult))
                link(nc.vector.tensor_tensor(pair[:, 0, :], pair[:, 0, :], pair[:, 1, :], ALU.add))
                link(nc.vector.tensor_reduce(v3(3), q4[0], AX, ALU.add))
                order.step(nc.vector.tensor_scalar(v3(4), v3(3), 2.0, None, ALU.is_lt))
                link(nc.vector.tensor_reduce(gred[:, 3, :], v3(2), AX, ALU.max))
                nc.vector.tensor_tensor(v3(5), v3(2), over_e(gred[:, 3, :]), ALU.subtract).then_inc(mg_ev, 1)
                dve.wait_ge(mexp, g * 2 + 2)
                link(nc.vector.tensor_tensor(v3(6), v3(6), v3(4), ALU.mult))
                link(nc.vector.tensor_reduce(gred[:, 1, :], v3(6), AX, ALU.add))
                link(nc.vector.reciprocal(gred[:, 2, :], gred[:, 1, :]))
                link(nc.vector.tensor_tensor(v3(7), v3(6), over_e(gred[:, 2, :]), ALU.mult))
                for j in range(TG):
                    xt = X[:, bass.ds(g * TG + j, 1), :].rearrange("p a d -> p (a d)")
                    dve.wait_ge(m3, g * TG + (j + 1))
                    shared, first, second = M3[j % 2]
                    link(nc.vector.tensor_tensor(xt, xt, bank[shared][0:TP, 0:D], ALU.add))
                    for e in range(NE):
                        o = bank[(first, second)[e // 2]][0:TP, (e % 2) * D:(e % 2 + 1) * D]
                        ins = nc.vector.scalar_tensor_tensor(out=xt, in0=o, scalar=small[:, 7, NE * j + e:NE * j + e + 1],
                                                             in1=xt, op0=ALU.mult, op1=ALU.add)
                        if e < NE - 1:
                            link(ins)
                        else:
                            ins.then_inc(o_ok, 1)

            GATE_STEPS, COMBINE_STEPS = 16, TG * NE
            with dve.Fori(0, G - 1) as g:
                order.enter(g, LN_STEPS + GATE_STEPS + COMBINE_STEPS)
                second_ffn(g, True)
            order.leave(G - 1)
            second_ffn(G - 1, False)

        @block.scalar
        def _(act):
            def ln_copy(g, ln, dst):
                act.wait_ge(ln_t, g + (ln * G + 2))
                for k in range(KD):
                    nc.scalar.activation(dst(k), bank[k][:, 0:GN], ACT.Copy).then_inc(ln_ev, 1)

            EARLY = (TG - 1) * TP

            def keep_early(g):
                act.wait_ge(ln_t, g + 2)
                for k in range(KD):
                    nc.scalar.activation(pT0[:, k, 0:EARLY], bank[k][:, 0:EARLY], ACT.Copy).then_inc(early_cols, 1)

            def keep_late(g):
                for k in range(KD):
                    nc.scalar.activation(pT0[:, k, EARLY:GN], bank[k][:, EARLY:GN], ACT.Copy).then_inc(ln_ev, 1)

            keep_early(0)
            keep_late(0)

            def stage0(g, more):
                for j in range(TG):
                    if j == TG - 1 and more:
                        keep_early(g + 1)
                    act.wait_ge(hst_free, g * TG + (j + 1))
                    for b in (0, 1):
                        act.wait_ge(h_mm, g * (5 * TG) + (5 * j + b + 1))
                        nc.scalar.activation(hst[:, j % 2, b * 512:(b + 1) * 512], bank[2 + b][0:TP, :], ACT.Copy).then_inc(h_act, 1)
                if more:
                    act.wait_ge(h_mm, g * (5 * TG) + 5 * TG)
                    keep_late(g + 1)

            with act.Fori(0, G - 1) as g:
                stage0(g, True)
            stage0(G - 1, False)

            act.wait_ge(consts, 17)
            with act.Fori(0, NT) as t:
                act.wait_ge(tile_sum, t + 1)
                act.wait_ge(at_t, t * len(BLOCKS) + 1)
                act.wait_ge(over_ok, t + 1)
                for i in AB_ACT:
                    nc.scalar.activation(abf[:, i * GN:(i + 1) * GN], bank[1 + i][0:TP, 0:GN], ACT.Copy).then_inc(a_act, 1)
                for b, (lo, hi) in enumerate(BLOCKS):
                    act.wait_ge(at_t, t * len(BLOCKS) + (b + 2))
                    nc.scalar.activation(AT[:, lo:hi, bass.ds(t * TP, TP)],
                                         bank16[6 + b % 2][0:TP, :].rearrange("p (s n) -> p s n", n=P)[:, 0:hi - lo, 0:TP],
                                         ACT.Copy).then_inc(at_ev, 1)
                act.wait_ge(a_act, t * 3 + 6)
                act.wait_ge(a_dve, t * 2 + 4)
                nc.scalar.activation(over_junk, abf, ACT.Relu, bias=m_exact[0:TP, :],
                                     accum_out=over[:, bass.ds(t, 1)]).then_inc(over_ok, 1)

            act.wait_ge(ld_small, 16 * 15)
            with act.Fori(0, G) as g:
                ln_copy(g, 1, lambda k: XT[:, k, bass.ds(g * GN, GN)])
                act.wait_ge(wb_mm, g + 1)
                nc.scalar.activation(WB[:, bass.ds(g * GN, GN)], bank[2][:, 0:GN], ACT.Identity, bias=br_col[:, :]).then_inc(wb_ok, 1)
            with act.Fori(0, G) as g:
                act.wait_ge(diag_ok, 1)
                for m in range(HM):
                    act.wait_ge(f1, g * HM + (m + 1))
                    nc.scalar.activation(hT[:, m, :], bank[(m + 2) % 4][:, 0:GN], ACT.Gelu_apprx_tanh,
                                         bias=b1_col[:, m:m + 1]).then_inc(f1e, 1)

            act.wait_ge(flag_ok, 1)
            inexact = act.value_load(flag[0:1, 0:1], min_val=0, max_val=1)

            def first_part(g, layer):
                ts = bass.ds(g * TG, TG)
                if layer == 0:
                    act.wait_ge(y_ok, g * TG + TG)
                else:
                    act.wait_ge(c2e, g * TG + (TG + 4))
                nc.scalar.activation(Ys[:, ts, 0, :], Y[:, ts, :], ACT.Copy).then_inc(split_a, 1)

            def second_part(g, layer):
                n, ts = 2 * G * layer, bass.ds(g * TG, TG)
                act.wait_ge(split_d, g * 2 + (n + 1))
                nc.scalar.activation(Ys[:, ts, 1, :], res, ACT.Copy).then_inc(split_a, 1)

            with act.Fori(0, G) as g:
                first_part(g, 0)
                second_part(g, 0)
            for layer in range(2):
                act.wait_ge(split_d, (layer + 1) * 2 * G)
                with act.If(inexact > 0):
                    act.wait_ge(at_ok, 2)
                    with act.Fori(0, NT) as t:
                        act.wait_ge(few_t, t + (layer * NT + 2))
                        nc.scalar.activation(few_T[:, :, bass.ds(t * TP, TP)],
                                             bank[1][:, 0:KD * TP].rearrange("p (k n) -> p k n", k=KD), ACT.Copy).then_inc(few_ev, 1)
                    act.wait_ge(few_ev, 1 + (layer + 1) * NT)
                    act.wait_ge(few_dma, 32 * (layer + 1))
                    nc.scalar.activation(XT[:, :, :], few_T, ACT.Copy).then_inc(few_xt, 1)
                with act.Else():
                    for f in range(KD):
                        act.wait_ge(u_mm, (layer * KD + f + 1) * NT)
                        for i in (0, 2, 4):
                            nc.scalar.activation(XT[:, f, i * GN:(i + 1) * GN], bank[(5 * f + i) % 8][:, 0:GN], ACT.Copy).then_inc(u_act, 1)
                with act.Fori(0, G) as g:
                    for k in range(KD):
                        act.wait_ge(c1, g * KD + (layer * KD * G + k + 1))
                        nc.scalar.activation(ZT[:, bass.ds(g, 1), k, :].rearrange("p a n -> p (a n)"), bank[2 + k][:, 0:GN], ACT.Identity,
                                             bias=gin_col[:, 2 + 3 * layer, k:k + 1]).then_inc(c1e, 1)
                act.wait_ge(bn_ok, 5 + layer)

                def activate(g, behind=()):
                    for h in range(2):
                        act.wait_ge(c2, g * TG + (layer * NT + 2 * h + 2))
                        for k in range(KD):
                            half_z = ZT[:, bass.ds(g, 1), k, h * GN // 2:(h + 1) * GN // 2].rearrange("p a n -> p (a n)")
                            nc.scalar.activation(zs[:, h, k, :], half_z, ACT.Relu,
                                                 bias=bn_bi[:, k:k + 1], scale=bn_sc[:, k:k + 1]).then_inc(zs_ok, 1)
                        if behind:
                            behind[h](g - 1, 1)

                if layer == 0:
                    activate(0)
                    with act.Fori(1, G) as g:
                        activate(g, (first_part, second_part))
                    first_part(G - 1, 1)
                    second_part(G - 1, 1)
                else:
                    with act.Fori(0, G) as g:
                        activate(g)

            ln_copy(0, 3, lambda k: pT3[:, k, :])

            def second_ffn(g, more):
                for m in range(6):
                    act.wait_ge(m1, g * 6 + (m + 1))
                    dst, bias = (s1[:, m, :], sb1_col[:, m:m + 1]) if m < 2 else (e1[:, m - 2, :], eb1_col[:, m - 2:m - 1])
                    nc.scalar.activation(dst, bank[(5, 6)[m % 2]][:, 0:GN], ACT.Relu, bias=bias).then_inc(m1e, 1)
                act.wait_ge(mg_ev, g * 2 + 1)
                nc.scalar.activation(small[:, 1, :], small[:, 0, :], ACT.Exp).then_inc(mexp, 1)
                if more:
                    ln_copy(g + 1, 3, lambda k: pT3[:, k, :])
                act.wait_ge(mg_ev, g * 2 + 2)
                nc.scalar.activation(small[:, 6, :], small[:, 5, :], ACT.Exp).then_inc(mexp, 1)
                for m in range(5):
                    act.wait_ge(m2, g * 5 + (m + 1))
                    src = bank[(5, 6)[m % 2]]
                    if m == 0:
                        nc.scalar.activation(s2, src[:, 0:GN], ACT.Relu, bias=sb2_col[:, :]).then_inc(m2e, 1)
                    else:
                        nc.scalar.activation(e2[0:EH2, m - 1, :], src[0:EH2, 0:GN], ACT.Relu,
                                             bias=eb2_col[:, m - 1:m]).then_inc(m2e, 1)

            with act.Fori(0, G - 1) as g:
                second_ffn(g, True)
            second_ffn(G - 1, False)

        @block.tensor
        def _(pe):
            mm = nc.tensor.matmul

            pe.sem_inc(used, U)
            pe.sem_inc(few_used, U)
            pe.sem_inc(few_read, 1)
            pe.sem_inc(few_t, 1)
            pe.sem_inc(few_ev, 1)
            pe.sem_inc(h_act, 2)
            pe.sem_inc(h_dve, 3)
            pe.sem_inc(hst_free, 2)
            pe.sem_inc(tile_read, 1)
            pe.sem_inc(f1e, 4)
            pe.sem_inc(f2e, 8)
            pe.sem_inc(c1e, KD)
            pe.sem_inc(c2e, 4)
            pe.sem_inc(a_act, 3)
            pe.sem_inc(a_dve, 2)
            pe.sem_inc(over_ok, 1)
            pe.sem_inc(at_t, 1)
            pe.sem_inc(at_ev, 2)
            pe.sem_inc(c2, TG)
            pe.sem_inc(m1e, 2)
            pe.sem_inc(o_ok, 2)
            pe.sem_inc(ln_t, 1)
            pe.sem_inc(wb_ok, 1)

            def ln_transposes(g, ln, ev_before):
                pe.wait_ge(ln_nrm, g * TG + (ln * NT + TG))
                if ev_before is not None:
                    pe.wait_ge(ln_ev, ev_before)
                for k in range(KD):
                    for j in range(TG):
                        last = nc.tensor.transpose(bank[k][:, j * TP:(j + 1) * TP], nrm[:, j, k * P:(k + 1) * P], ident[0:TP, 0:TP])
                last.then_inc(ln_t, 1)

            def edge_columns(i):
                pe.wait_ge(edges_f, 1)
                pe.wait_ge(ln_ev, 2 * KD)
                if i == 2:
                    pe.wait_ge(edges_ev, 4)
                for j in range(CJ):
                    dst = bank[EDGE_BANKS[i]][:, j * TP:(j + 1) * TP] if j < CJ - 1 else bank[1][:, i * TP:(i + 1) * TP]
                    last = nc.tensor.transpose(dst, edge_f[:, i, j * P:(j + 1) * P], ident[0:TP, 0:TP])
                last.then_inc(edges_t, 1)

            def spread_limits():
                pe.wait_ge(edges_ev, 6)
                pe.wait_ge(ln_ev, G * KD)
                pe.wait_ge(spread_ok, 2)
                for i in range(2):
                    for (b, at), lo, hi in zip(SPREAD_BANKS[i], (0, 512), (512, CH)):
                        last = mm(bank[b][0:NT, at:at + hi - lo], ones[0:TP, 0:NT], spread[:, i, lo:hi], start=True, stop=True)
                last.then_inc(spread_bc, 1)

            def limits_to_row():
                pe.wait_ge(lohi_ok, 1)
                for i in range(2):
                    last = mm(bank[0][0:1, i * NT:(i + 1) * NT], lohi[:, i:i + 1], ident[0:NT, 0:NT], start=True, stop=True)
                last.then_inc(lohi_t, 1)

            def stage0(g, more, between=None):
                pe.wait_ge(early_cols, g * KD + KD)
                for j in range(TG):
                    if j == TG - 1:
                        pe.wait_ge(ln_ev, g * KD + KD)
                        if more:
                            ln_transposes(g + 1, 0, None)
                    for b in range(5):
                        if b < 2:
                            pe.wait_ge(h_act, g * (2 * TG) + (2 * j + b + 1))
                        else:
                            pe.wait_ge(h_dve, g * (3 * TG) + (3 * j + b - 1))
                        pe.wait_ge(w0_ok, min(b + 1, 4))
                        w = 512 if b < 4 else D
                        for k in range(KD):
                            rows_t = pT0[:, k, j * TP:(j + 1) * TP]
                            last = mm(bank[2 + b][0:TP, 0:w], rows_t, W0[:, k, b * 512:b * 512 + w],
                                      start=(k == 0), stop=(k == KD - 1))
                        last.then_inc(h_mm, 1)
                    if between is not None:
                        between(j)

            def group1(j):
                if j == 0:
                    edge_columns(0)
                    edge_columns(1)
                elif j == 1:
                    edge_columns(2)
                    pe.wait_ge(edges_ev, 6)

            def last_group(j):
                if j == 0:
                    spread_limits()
                elif j == 2:
                    limits_to_row()

            pe.wait_ge(consts, 17)
            ln_transposes(0, 0, None)
            stage0(0, True)
            stage0(1, True, group1)
            with pe.Fori(2, G - 1) as g:
                stage0(g, True)
            stage0(G - 1, False, last_group)
            pe.wait_ge(rng_ok, 1)

            summed = pe.alloc_register("summed")
            pe.reg_mov(summed, 1)
            landed = pe.alloc_register("landed")
            pe.reg_mov(landed, 16)

            def chunk(t, u, n, l, new=False):
                pe.wait_ge(hot, (n - 1) * 3 + (3 * u + 2))
                for i in range(AB):
                    if new:
                        if i in AB_ACT:
                            pe.wait_ge(a_act, t * 3 + (AB_ACT.index(i) + 1))
                        else:
                            pe.wait_ge(a_dve, t * 2 + (AB_DVE.index(i) + 1))
                    mm(bank[1 + i][:, 0:GN], hot16[:, u, :], hot_src[:, u, i * GN:(i + 1) * GN],
                       start=new, stop=True, skip_group_check=True)
                if new:
                    pe.wait_ge(tile_read, t + 1)
                pe.wait_ge(hot, (n - 1) * 3 + (3 * u + 3))
                pe.wait_ge(gathered[u], l)
                mm(bank[0][:, 0:D], onehot[:, u, :], msg[:, u, :], start=new, stop=True,
                   skip_group_check=True).then_inc(used, 1)

            def counters():
                return (pe.snap(summed, min_val=1, max_val=4 * NT * PAD),
                        pe.snap(landed, min_val=16, max_val=4 * 16 * NT * PAD))

            def count_round():
                pe.reg_add(summed, summed, U)
                pe.reg_add(landed, landed, 16)

            def transpose_rows(t, banks):
                pe.wait_ge(a_act, t * 3 + 6)
                pe.wait_ge(a_dve, t * 2 + 4)
                for b in banks:
                    lo, hi = BLOCKS[b]
                    pe.wait_ge(at_ev, t * len(BLOCKS) + (b + 1))
                    for s in range(lo, hi):
                        last = nc.tensor.transpose(bank16[6 + b % 2][0:TP, (s - lo) * P:(s - lo) * P + TP],
                                                   abf[:, s * TP:(s + 1) * TP], ident16[0:TP, 0:TP])
                    last.then_inc(at_t, 1)

            def tile(t, before):
                first = pe.value_load(rng[0:1, bass.ds(t, 1)], min_val=1, max_val=PRE + CH - 1)
                end = pe.value_load(rng[0:1, bass.ds(t + NT, 1)], min_val=PRE + 1, max_val=PRE + CH + 2 * U)
                skip = pe.value_load(rng[0:1, bass.ds(t + 2 * NT, 1)], min_val=0, max_val=U - 1)
                n, l = counters()
                chunk(t, 0, n, l, new=True)
                for u in range(1, U):
                    with pe.If(skip < u):
                        chunk(t, u, n, l)
                    with pe.Else():
                        pe.wait_ge(hot, (n - 1) * 3 + (3 * u + 3))
                        pe.wait_ge(gathered[u], l)
                        mm(bank[0][:, 0:2], zeros[:, :], zeros[:, 0:2], start=False, stop=True, skip_group_check=True).then_inc(used, 1)
                count_round()
                if before:
                    transpose_rows(t - 1, (0, 1))

                def whole_round():
                    n, l = counters()
                    for u in range(U):
                        chunk(t, u, n, l)
                    count_round()

                whole_round()
                if before:
                    transpose_rows(t - 1, (2,))
                with pe.Fori(first + 2 * U, end, U):
                    whole_round()
                mm(bank[0][:, 0:2], zeros[:, :], zeros[:, 0:2], start=False, stop=True, skip_group_check=True).then_inc(tile_sum, 1)

            pe.wait_ge(h_act, 2 + 2 * NT)
            pe.wait_ge(h_dve, 3 + 3 * NT)
            tile(0, False)
            with pe.Fori(1, NT) as t:
                tile(t, True)
            transpose_rows(NT - 1, (0, 1, 2))
            pe.wait_ge(wr_ok, KD)
            with pe.Fori(0, G) as g:
                ln_transposes(g, 1, g * KD + KD * G)
                pe.wait_ge(ln_ev, g * KD + (KD * G + KD))
                pe.wait_ge(wb_ok, g + 1)
                for k in range(KD):
                    last = mm(bank[2][:, 0:GN], wr_rep[:, k, :], XT[:, k, bass.ds(g * GN, GN)], start=(k == 0), stop=(k == KD - 1))
                last.then_inc(wb_mm, 1)
            pe.wait_ge(over_max_ok, 1)
            pe.wait_ge(at_ev, 2 + len(BLOCKS) * NT)
            mm(bank[7][0:1, 0:1], over_max[:, :], ones[0:TP, 0:1], start=True, stop=True).then_inc(over_mm, 1)
            pe.wait_ge(wb_ok, 1 + G)
            pe.wait_ge(ld_ffn, 48)
            pe.wait_ge(ld_small, 16 * 15)

            def hidden_rows(g, pair_no=None):
                for m in range(HM):
                    if m == 2 and pair_no is not None:
                        pe.wait_ge(ln_ev, pair_no * (2 * KD) + 2 * KD * G)
                    pe.wait_ge(f1e, g * HM + (m + 1))
                    for k in range(KD):
                        last = mm(bank[(m + 2) % 4][:, 0:GN], w1[:, k, m * P:(m + 1) * P], XT[:, k, bass.ds(g * GN, GN)],
                                  start=(k == 0), stop=(k == KD - 1))
                    last.then_inc(f1, 1)
                pe.wait_ge(f1e, g * HM + (HM + 4))

            def ffn_rows(g, odd):
                for j in range(TG):
                    pe.wait_ge(f2e, g * TG + (2 * (j // 2) + 2))
                    o = bank[4 + 2 * odd + j // 2][0:TP, j % 2 * D:(j % 2 + 1) * D]
                    for m in range(HM):
                        last = mm(o, hT[:, m, j * TP:(j + 1) * TP], w2[:, m, :], start=(m == 0), stop=(m == HM - 1))
                    last.then_inc(f2, 1)

            hidden_rows(0)
            ffn_rows(0, 0)
            pe.wait_ge(flag_ok, 1)
            inexact = pe.value_load(flag[0:1, 0:1], min_val=0, max_val=1)
            pe.reg_mov(summed, 1)
            pe.reg_mov(landed, 16)
            with pe.Fori(0, (G - 1) // 2) as pair_no:
                hidden_rows(pair_no * 2 + 1, pair_no)
                ffn_rows(pair_no * 2 + 1, 1)
                hidden_rows(pair_no * 2 + 2)
                ln_transposes(pair_no * 2, 2, None)
                ffn_rows(pair_no * 2 + 2, 0)
                ln_transposes(pair_no * 2 + 1, 2, pair_no * (2 * KD) + (2 * KD * G + KD))

            ln_transposes(G - 1, 2, 3 * KD * G - KD)
            pe.wait_ge(bn_ok, 4)
            for q in range(4):
                last = mm(bank[2][0:TP, q * P:(q + 1) * P], bn_rep[:, q, 0:TP], ident[:, :], start=True, stop=True)
            last.then_inc(bn_mm, 1)
            pe.wait_ge(ld_gin, 96)
            for layer in range(2):
                def few_round(new):
                    n = pe.snap(summed, min_val=1, max_val=4 * NT * PAD)
                    l = pe.snap(landed, min_val=16, max_val=4 * 16 * NT * PAD)
                    for u in range(U):
                        pe.wait_ge(few_made, n + u)
                        pe.wait_ge(few_landed[u], l)
                        mm(bank[0][:, 0:D], few_hot[:, u, :], few_msg[:, u, :], start=new and u == 0, stop=True,
                           skip_group_check=True).then_inc(few_used, 1)
                    pe.reg_add(summed, summed, U)
                    pe.reg_add(landed, landed, 16)

                with pe.If(inexact > 0):
                    pe.wait_ge(ln_ev, 3 * KD * G)
                    with pe.Fori(0, NT) as t:
                        first = pe.value_load(rng[0:1, bass.ds(t, 1)], min_val=1, max_val=PRE + CH - 1)
                        end = pe.value_load(rng[0:1, bass.ds(t + NT, 1)], min_val=PRE + 1, max_val=PRE + CH + 2 * U)
                        pe.wait_ge(few_read, t + (layer * NT + 1))
                        few_round(True)
                        with pe.Fori(first + U, end, U):
                            few_round(False)
                        mm(bank[0][:, 0:2], zeros[:, :], zeros[:, 0:2], start=False, stop=True,
                           skip_group_check=True).then_inc(few_sum, 1)
                        pe.wait_ge(few_read, t + (layer * NT + 2))
                        pe.wait_ge(few_ev, t + (layer * NT + 1))
                        for k in range(KD):
                            last = nc.tensor.transpose(bank[1][:, k * TP:(k + 1) * TP], few_tile[:, k * P:(k + 1) * P], ident[0:TP, 0:TP])
                        last.then_inc(few_t, 1)
                    pe.wait_ge(few_xt, layer + 1)
                with pe.Else():
                    pe.wait_ge(split_d, layer * 2 * G + 2)
                    pe.wait_ge(at_ok, 2)
                    for f in range(KD):
                        def neighbours(s, start):
                            for part in range(PARTS):
                                for i in range(AB):
                                    if start and part == 0:
                                        if f == 0 and i == 4 and layer == 1:
                                            pe.wait_ge(c2e, 4 + NT)
                                        if f == 1 and i >= 3:
                                            pe.wait_ge(u_act, layer * 6 + 1)
                                            pe.wait_ge(u_dve, layer * 4 + 1)
                                    w = Ys[:, bass.ds(s, 1), part, f * P:(f + 1) * P].rearrange("p a n -> p (a n)")
                                    v = AT[:, bass.ds(s, 1), i * GN:(i + 1) * GN].rearrange("p a n -> p (a n)")
                                    last = mm(bank[(5 * f + i) % 8][:, 0:GN], w, v, start=start and part == 0, stop=True,
                                              skip_group_check=True)
                            last.then_inc(u_mm, 1)
                        neighbours(0, True)
                        with pe.Fori(1, TG) as s:
                            neighbours(s, False)
                        with pe.Fori(1, G) as g:
                            pe.wait_ge(split_d, g * 2 + (layer * 2 * G + 2))
                            for j in range(TG):
                                neighbours(g * TG + j, False)
                    pe.wait_ge(u_act, layer * 6 + 6)
                    pe.wait_ge(u_dve, layer * 4 + 4)
                with pe.Fori(0, G) as g:
                    for m in range(KD):
                        pe.wait_ge(c1e, g * KD + (layer * KD * G + m + 1))
                        for k in range(KD):
                            last = mm(bank[2 + m][:, 0:GN], gw[:, 2 * layer, k, m * P:(m + 1) * P], XT[:, k, bass.ds(g * GN, GN)],
                                      start=(k == 0), stop=(k == KD - 1))
                        last.then_inc(c1, 1)
                with pe.Fori(0, G) as g:
                    for j in range(TG):
                        if j % 2 == 0:
                            pe.wait_ge(zs_ok, g * (2 * KD) + (layer * 2 * KD * G + (j // 2 + 1) * KD))
                        pe.wait_ge(c2e, g * TG + (layer * NT + j + 1))
                        o = bank[4 + j][0:TP, 0:D]
                        for k in range(KD):
                            mm(o, zs[:, j // 2, k, j % 2 * TP:(j % 2 + 1) * TP], gw[:, 2 * layer + 1, k, :], start=(k == 0), stop=False)
                        mm(o, ones[0:1, 0:TP], (b1b_row, b2b_row)[layer], start=False, stop=True).then_inc(c2, 1)

            pe.wait_ge(ld_moe, 16 * 10)
            pe.wait_ge(e2_ones, 1)
            ln_transposes(0, 3, 3 * KD * G)

            def second_ffn(g, more):
                pe.wait_ge(ln_ev, g * KD + (3 * KD * G + KD))
                pe.wait_ge(o_ok, g * TG + 1)
                for j in range(TG):
                    o = bank[7][0:TP, j * NE:(j + 1) * NE]
                    for k in range(KD):
                        mm(o, pT3[:, k, j * TP:(j + 1) * TP], gW[:, k, :], start=(k == 0), stop=False)
                    last = mm(o, ones[0:1, 0:TP], gb_row, start=False, stop=True)
                last.then_inc(mg, 1)
                for m in range(6):
                    pe.wait_ge(m1e, g * 6 + (m + 1))
                    for k in range(KD):
                        w = sW1[:, k, m * P:(m + 1) * P] if m < 2 else eW1[:, m - 2, k, :]
                        last = mm(bank[(5, 6)[m % 2]][:, 0:GN], w, pT3[:, k, :], start=(k == 0), stop=(k == KD - 1))
                    last.then_inc(m1, 1)
                if more:
                    ln_transposes(g + 1, 3, g * KD + (3 * KD * G + KD))
                pe.wait_ge(m1e, g * 6 + 8)
                for m in range(5):
                    if m >= 2:
                        pe.wait_ge(m2e, g * 5 + (m - 1))
                    if m == 0:
                        for k in range(KD):
                            last = mm(bank[5][:, 0:GN], sW2[:, k, :], s1[:, k, :], start=(k == 0), stop=(k == KD - 1))
                    else:
                        last = mm(bank[(5, 6)[m % 2]][0:EH2, 0:GN], eW2[:, m - 1, :], e1[:, m - 1, :], start=True, stop=True)
                    last.then_inc(m2, 1)
                pe.wait_ge(m2e, g * 5 + 5)
                pe.wait_ge(mg_ev, g * 2 + 1)
                for j in range(TG):
                    shared, first, second = M3[j % 2]
                    pe.wait_ge(o_ok, g * TG + (j + 1))
                    o = bank[shared][0:TP, 0:D]
                    mm(o, s2[:, j * TP:(j + 1) * TP], sW3, start=True, stop=True)
                    for e in range(NE):
                        last = mm(bank[(first, second)[e // 2]][0:TP, (e % 2) * D:(e % 2 + 1) * D], e2[:, e, j * TP:(j + 1) * TP],
                                  eW3[:, e, :], start=True, stop=True)
                    last.then_inc(m3, 1)

            with pe.Fori(0, G - 1) as g:
                second_ffn(g, True)
            second_ffn(G - 1, False)


_INS = ["x", "src", "dst", "edge_type_8", "L0_gnn_basis", "L0_gnn_comp", "L0_gnn_loop_weight", "L0_gnn_bias_param",
        "L0_ffn_wr", "L0_ffn_br", "L0_ffn_w1", "L0_ffn_b1", "L0_ffn_w2", "L0_ffn_b2",
        "L1_gnn_g0", "L1_gnn_b0", "L1_gnn_W1a", "L1_gnn_b1a", "L1_gnn_g1", "L1_gnn_bt1", "L1_gnn_W1b", "L1_gnn_b1b",
        "L1_gnn_W2a", "L1_gnn_b2a", "L1_gnn_g2", "L1_gnn_bt2", "L1_gnn_W2b", "L1_gnn_b2b",
        "L1_ffn_sW1", "L1_ffn_sb1", "L1_ffn_sW2", "L1_ffn_sb2", "L1_ffn_sW3", "L1_ffn_sb3",
        "L1_ffn_eW1", "L1_ffn_eb1", "L1_ffn_eW2", "L1_ffn_eb2", "L1_ffn_eW3", "L1_ffn_eb3", "L1_ffn_gW", "L1_ffn_gb"]


def kernel(**inputs):
    import numpy as _np
    import concourse.bacc as _bacc
    from concourse import mybir as _mybir
    from concourse.bass_utils import run_bass_kernel_spmd as _run

    nc = _bacc.Bacc("TRN2", target_bir_lowering=False, num_devices=1)
    arrays, args = {}, {}
    for name in _INS:
        v = _np.ascontiguousarray(inputs[name])
        arrays[f"in_{name}"] = v
        args[name] = nc.dram_tensor(f"in_{name}", v.shape, _mybir.dt.from_np(v.dtype), kind="ExternalInput").ap()
    out = nc.dram_tensor("out_dram", (N, D), _mybir.dt.float32, kind="ExternalOutput").ap()
    h_table = nc.dram_tensor("h_table", (N * R, D), _mybir.dt.float32, kind="Internal").ap()
    x_table = nc.dram_tensor("x_table", (N, D), _mybir.dt.float32, kind="Internal").ap()
    gnn_ffn_kernel(nc, args, out, h_table, x_table)
    r = _run(nc, [arrays], core_ids=[0])
    return r.results[0]["out_dram"]
```
